# Optimizing a Trainium2 kernel written in Bass

```python
import numpy as np
import jax
import jax.numpy as jnp

def _softmax(x, axis=-1):
    return jax.nn.softmax(x, axis=axis)

def _gelu(x):
    return jax.nn.gelu(x, approximate=True)

def _silu(x):
    return jax.nn.silu(x)

def _sigmoid(x):
    return jax.nn.sigmoid(x)

def _layernorm(x, axis=-1, eps=1e-05):
    m = jnp.mean(x, axis=axis, keepdims=True)
    v = jnp.var(x, axis=axis, keepdims=True)
    return (x - m) / jnp.sqrt(v + eps)

def _scatter_add(tgt, idx, src, axis=0):
    return tgt.at[idx].add(src)

def _segment_sum(src, seg, n):
    return jax.ops.segment_sum(src, seg, n)
kernel_name = 'mk_prb_d2_jaxref_r4_6d986c'

def setup_inputs(seed: int=0):
    np.random.seed(seed)
    _w = jnp.asarray

    def _L0_attn_setup():
        import jax, jax.numpy as jnp
        import numpy as np
        D_MODEL = 256
        NUM_HEADS = 16
        HEAD_DIM = D_MODEL // NUM_HEADS
        key = jax.random.key(seed)
        k0, k1, k2, k3, k4 = jax.random.split(key, 5)
        B, S, D = (4, 512, D_MODEL)
        std = np.sqrt(2.0 / (D + D)).astype(np.float32)
        return {'in_features': jax.random.normal(k0, (B, S, D), dtype=jnp.float32), 'Wq': jax.random.normal(k1, (D, D), dtype=jnp.float32) * std, 'Wk': jax.random.normal(k2, (D, D), dtype=jnp.float32) * std, 'Wv': jax.random.normal(k3, (D, D), dtype=jnp.float32) * std, 'Wo': jax.random.normal(k4, (D, D), dtype=jnp.float32) * std}
    _L0_attn_in = _L0_attn_setup()

    def _L0_ffn_setup():
        import jax, jax.numpy as jnp
        import numpy as np
        TOP_K = 2

        def _gelu(x):
            return jax.nn.gelu(x, approximate=False)
        key = jax.random.key(seed)
        ks = jax.random.split(key, 6)
        B, S, D, F, E = (2, 512, 256, 512, 8)
        sc_g = 1.0 / np.sqrt(D)

        def xav(k, shape, fan_in, fan_out):
            lim = np.sqrt(6.0 / (fan_in + fan_out))
            return jax.random.uniform(k, shape, jnp.float32, -lim, lim)
        return {'x': jax.random.normal(ks[0], (B, S, D), jnp.float32), 'Wg': xav(ks[1], (D, E), D, E), 'Wu': xav(ks[2], (E, D, F), D, F), 'Wd': xav(ks[3], (E, F, D), F, D), 'W1': xav(ks[4], (D, F), D, F), 'W2': xav(ks[5], (F, D), F, D)}
    _L0_ffn_in = _L0_ffn_setup()

    def _L1_attn_setup():
        import jax, jax.numpy as jnp
        import numpy as np
        import math
        B, L, HID, NH = (4, 1024, 256, 8)
        DH = HID // NH
        THETA = 10000.0

        def _rope_tables(seq_len, dh):
            half = dh // 2
            inv_freq = 1.0 / THETA ** (jnp.arange(half, dtype=jnp.float32) / half)
            freqs = jnp.arange(seq_len, dtype=jnp.float32)[:, None] * inv_freq[None, :]
            return (jnp.cos(freqs), jnp.sin(freqs))

        def _apply_rope(x, cos, sin):
            half = x.shape[-1] // 2
            x1, x2 = (x[..., :half], x[..., half:2 * half])
            c = cos[None, None]
            s = sin[None, None]
            return jnp.concatenate([x1 * c - x2 * s, x1 * s + x2 * c], axis=-1)
        key = jax.random.key(seed)
        ks = jax.random.split(key, 9)

        def xav(k, sh):
            lim = math.sqrt(6.0 / (sh[0] + sh[1]))
            return jax.random.uniform(k, sh, jnp.float32, -lim, lim)
        return {'x': jax.random.normal(ks[0], (B, L, HID), jnp.float32), 'norm_w': jnp.ones((HID,), jnp.float32), 'Wq': xav(ks[1], (HID, HID)), 'Wk': xav(ks[2], (HID, HID)), 'Wv': xav(ks[3], (HID, HID)), 'Wbeta': xav(ks[4], (NH, HID)), 'bbeta': jnp.full((NH,), 2.0, jnp.float32), 'Wig': xav(ks[5], (NH, HID)), 'big': jnp.zeros((NH,), jnp.float32), 'Wog': xav(ks[6], (NH, HID)), 'bog': jnp.zeros((NH,), jnp.float32), 'Wout': xav(ks[7], (HID, HID)), 'bout': jnp.zeros((HID,), jnp.float32)}
    _L1_attn_in = _L1_attn_setup()

    def _L1_ffn_setup():
        import jax, jax.numpy as jnp
        import numpy as np
        D_MODEL = 256
        D_FF = 1024
        NUM_EXPERTS = 8
        TOP_K = 2
        B, S = (4, 1024)
        key = jax.random.key(seed)
        ks = jax.random.split(key, 7)
        s_dm = 1.0 / np.sqrt(D_MODEL)
        s_ff = 1.0 / np.sqrt(D_FF)
        return {'x': jax.random.normal(ks[0], (B, S, D_MODEL), jnp.float32), 'router_w': jax.random.normal(ks[1], (D_MODEL, NUM_EXPERTS), jnp.float32) * s_dm, 'router_b': jnp.zeros((NUM_EXPERTS,), jnp.float32), 'w1': jax.random.normal(ks[2], (NUM_EXPERTS, D_MODEL, D_FF), jnp.float32) * s_dm, 'b1': jnp.zeros((NUM_EXPERTS, D_FF), jnp.float32), 'w2': jax.random.normal(ks[3], (NUM_EXPERTS, D_FF, D_MODEL), jnp.float32) * s_ff, 'b2': jnp.zeros((NUM_EXPERTS, D_MODEL), jnp.float32)}
    _L1_ffn_in = _L1_ffn_setup()
    _d = {'L0_attn_in_features': _L0_attn_in['in_features'], 'L0_attn_Wq': _L0_attn_in['Wq'], 'L0_attn_Wk': _L0_attn_in['Wk'], 'L0_attn_Wv': _L0_attn_in['Wv'], 'L0_attn_Wo': _L0_attn_in['Wo'], 'L0_ffn_Wg': _L0_ffn_in['Wg'], 'L0_ffn_Wu': _L0_ffn_in['Wu'], 'L0_ffn_Wd': _L0_ffn_in['Wd'], 'L0_ffn_W1': _L0_ffn_in['W1'], 'L0_ffn_W2': _L0_ffn_in['W2'], 'L1_attn_norm_w': _L1_attn_in['norm_w'], 'L1_attn_Wq': _L1_attn_in['Wq'], 'L1_attn_Wk': _L1_attn_in['Wk'], 'L1_attn_Wv': _L1_attn_in['Wv'], 'L1_attn_Wbeta': _L1_attn_in['Wbeta'], 'L1_attn_bbeta': _L1_attn_in['bbeta'], 'L1_attn_Wig': _L1_attn_in['Wig'], 'L1_attn_big': _L1_attn_in['big'], 'L1_attn_Wog': _L1_attn_in['Wog'], 'L1_attn_bog': _L1_attn_in['bog'], 'L1_attn_Wout': _L1_attn_in['Wout'], 'L1_attn_bout': _L1_attn_in['bout'], 'L1_ffn_router_w': _L1_ffn_in['router_w'], 'L1_ffn_router_b': _L1_ffn_in['router_b'], 'L1_ffn_w1': _L1_ffn_in['w1'], 'L1_ffn_b1': _L1_ffn_in['b1'], 'L1_ffn_w2': _L1_ffn_in['w2'], 'L1_ffn_b2': _L1_ffn_in['b2']}
    _x0 = _d['L0_attn_in_features']
    _d['L0_attn_in_features'] = jax.random.normal(jax.random.fold_in(jax.random.key(seed), 1), (8, 512, 256), dtype=_x0.dtype)
    del _x0
    return _d

def reference(L0_attn_in_features, L0_attn_Wq, L0_attn_Wk, L0_attn_Wv, L0_attn_Wo, L0_ffn_Wg, L0_ffn_Wu, L0_ffn_Wd, L0_ffn_W1, L0_ffn_W2, L1_attn_norm_w, L1_attn_Wq, L1_attn_Wk, L1_attn_Wv, L1_attn_Wbeta, L1_attn_bbeta, L1_attn_Wig, L1_attn_big, L1_attn_Wog, L1_attn_bog, L1_attn_Wout, L1_attn_bout, L1_ffn_router_w, L1_ffn_router_b, L1_ffn_w1, L1_ffn_b1, L1_ffn_w2, L1_ffn_b2):

    def _L0_attn_ref(in_features, Wq, Wk, Wv, Wo):
        import jax, jax.numpy as jnp
        import numpy as np
        D_MODEL = 256
        NUM_HEADS = 16
        HEAD_DIM = D_MODEL // NUM_HEADS
        B, S, D = in_features.shape
        H, Hd = (NUM_HEADS, HEAD_DIM)

        def split_heads(x):
            return x.reshape(B, S, H, Hd).transpose(0, 2, 1, 3)
        q = split_heads(in_features @ Wq.T)
        k = split_heads(in_features @ Wk.T)
        v = split_heads(in_features @ Wv.T)
        scale = 1.0 / jnp.sqrt(jnp.asarray(Hd, dtype=q.dtype))
        scores = jnp.einsum('bhsd,bhtd->bhst', q, k) * scale
        causal = jnp.tril(jnp.ones((S, S), dtype=bool))
        scores = jnp.where(causal[None, None], scores, -jnp.inf)
        attn = jax.nn.softmax(scores, axis=-1)
        out = jnp.einsum('bhst,bhtd->bhsd', attn, v)
        out = out.transpose(0, 2, 1, 3).reshape(B, S, D)
        return out @ Wo.T

    def _L0_ffn_ref(x, Wg, Wu, Wd, W1, W2):
        import jax, jax.numpy as jnp
        import numpy as np
        TOP_K = 2

        def _gelu(x):
            return jax.nn.gelu(x, approximate=False)
        B, S, D = x.shape
        E = Wu.shape[0]
        T = B * S
        xt = x.reshape(T, D)
        probs = jax.nn.softmax(xt @ Wg, axis=-1)
        topv, topi = jax.lax.top_k(probs, TOP_K)
        topv = topv / jnp.sum(topv, axis=-1, keepdims=True)
        cw = jnp.zeros((T, E), x.dtype).at[jnp.arange(T)[:, None], topi].set(topv)
        h = _gelu(jnp.einsum('td,edf->tef', xt, Wu))
        y = jnp.einsum('tef,efd->ted', h, Wd)
        moe = jnp.einsum('ted,te->td', y, cw)
        shared = _gelu(xt @ W1) @ W2
        return (shared + moe).reshape(B, S, D)

    def _L1_attn_ref(x, norm_w, Wq, Wk, Wv, Wbeta, bbeta, Wig, big, Wog, bog, Wout, bout):
        import jax, jax.numpy as jnp
        import numpy as np
        import math
        B, L, HID, NH = (4, 1024, 256, 8)
        DH = HID // NH
        THETA = 10000.0

        def _rope_tables(seq_len, dh):
            half = dh // 2
            inv_freq = 1.0 / THETA ** (jnp.arange(half, dtype=jnp.float32) / half)
            freqs = jnp.arange(seq_len, dtype=jnp.float32)[:, None] * inv_freq[None, :]
            return (jnp.cos(freqs), jnp.sin(freqs))

        def _apply_rope(x, cos, sin):
            half = x.shape[-1] // 2
            x1, x2 = (x[..., :half], x[..., half:2 * half])
            c = cos[None, None]
            s = sin[None, None]
            return jnp.concatenate([x1 * c - x2 * s, x1 * s + x2 * c], axis=-1)
        Bq, Lq, _ = x.shape
        h = x * jax.lax.rsqrt(jnp.mean(x * x, axis=-1, keepdims=True) + 1e-06) * norm_w

        def heads(W):
            return jnp.einsum('bld,ed->ble', h, W).reshape(Bq, Lq, NH, DH).transpose(0, 2, 1, 3)
        q, k, v = (heads(Wq), heads(Wk), heads(Wv))
        cos, sin = _rope_tables(Lq, DH)
        q = _apply_rope(q, cos, sin)
        k = _apply_rope(k, cos, sin)

        def gate(W, b):
            return jax.nn.sigmoid(jnp.einsum('bld,hd->blh', h, W) + b).transpose(0, 2, 1)
        beta, ig, og = (gate(Wbeta, bbeta), gate(Wig, big), gate(Wog, bog))
        scale = 1.0 / math.sqrt(DH)
        qT = q.transpose(2, 0, 1, 3)
        kT = k.transpose(2, 0, 1, 3)
        vT = v.transpose(2, 0, 1, 3)
        fT = beta.transpose(2, 0, 1)
        gT = ig.transpose(2, 0, 1)
        oT = og.transpose(2, 0, 1)
        M0 = jnp.zeros((Bq, NH, DH, DH), x.dtype)

        def step(M, inp):
            q_t, k_t, v_t, f_t, g_t, o_t = inp
            M = M * f_t[..., None, None] + g_t[..., None, None] * scale * (k_t[..., :, None] * v_t[..., None, :])
            y_t = jnp.einsum('bhd,bhde->bhe', q_t, M) * o_t[..., None]
            return (M, y_t)
        _, yT = jax.lax.scan(step, M0, (qT, kT, vT, fT, gT, oT))
        y = yT.transpose(1, 0, 2, 3).reshape(Bq, Lq, HID)
        return jnp.einsum('bld,ed->ble', y, Wout) + bout

    def _L1_ffn_ref(x, router_w, router_b, w1, b1, w2, b2):
        import jax, jax.numpy as jnp
        import numpy as np
        D_MODEL = 256
        D_FF = 1024
        NUM_EXPERTS = 8
        TOP_K = 2
        B, S = (4, 1024)
        Bx, Sx, D = x.shape
        xf = x.reshape(-1, D)
        logits = xf @ router_w + router_b
        top_w, sel = jax.lax.top_k(logits, TOP_K)
        gates = jax.nn.softmax(top_w, axis=-1)

        def body(i, acc):
            h = jax.nn.gelu(xf @ w1[i] + b1[i], approximate=False)
            out_i = h @ w2[i] + b2[i]
            gate_i = jnp.sum(gates * (sel == i), axis=-1, keepdims=True)
            return acc + out_i * gate_i
        out = jax.lax.fori_loop(0, NUM_EXPERTS, body, jnp.zeros_like(xf))
        return out.reshape(Bx, Sx, D)
    x = L0_attn_in_features
    xn = _layernorm(x, axis=-1)
    x = x + _L0_attn_ref(xn, L0_attn_Wq, L0_attn_Wk, L0_attn_Wv, L0_attn_Wo) + _L0_ffn_ref(xn, L0_ffn_Wg, L0_ffn_Wu, L0_ffn_Wd, L0_ffn_W1, L0_ffn_W2)
    xn = _layernorm(x, axis=-1)
    x = x + _L1_attn_ref(xn, L1_attn_norm_w, L1_attn_Wq, L1_attn_Wk, L1_attn_Wv, L1_attn_Wbeta, L1_attn_bbeta, L1_attn_Wig, L1_attn_big, L1_attn_Wog, L1_attn_bog, L1_attn_Wout, L1_attn_bout) + _L1_ffn_ref(xn, L1_ffn_router_w, L1_ffn_router_b, L1_ffn_w1, L1_ffn_b1, L1_ffn_w2, L1_ffn_b2)
    return x

_drawn_inputs = setup_inputs


def setup_inputs(seed=0):
    import zlib

    import numpy as np

    out = dict(_drawn_inputs(seed))
    spreads = {'L1_attn_norm_w': (1.0, 0.2),
     'L1_attn_bbeta': (2.0, 0.2),
     'L1_attn_big': (0.0, 0.434),
     'L1_attn_bog': (0.0, 0.8),
     'L1_attn_bout': (0.0, 0.1),
     'L1_ffn_router_b': (0.0, 0.1),
     'L1_ffn_b1': (0.0, 0.1),
     'L1_ffn_b2': (0.0, 0.1)}
    factors = {}
    for name, (base, spread) in spreads.items():
        noise = np.random.default_rng([zlib.crc32(name.encode()), seed]).standard_normal(out[name].shape)
        drawn = base * np.exp(spread * noise) if base else spread * noise
        out[name] = jnp.asarray(drawn.astype(out[name].dtype))
    for name, factor in factors.items():
        out[name] = (out[name] * factor).astype(out[name].dtype)
    return out
```

```python
from contextlib import ExitStack

import numpy as np
import concourse.bass as bass
from concourse import mybir

F32 = mybir.dt.float32
BF16 = mybir.dt.bfloat16
I32 = mybir.dt.int32
U32 = mybir.dt.uint32
ALU = mybir.AluOpType
ACT = mybir.ActivationFunctionType
AX = mybir.AxisListType

NB, S, D = 8, 512, 256
T = NB * S
NT = T // 128
E = 8
NTILE = (2 * T + E * 127) // 128
NSLOT = NTILE * 128
F0, F1 = 512, 1024
NEG = -1.0e30


class Line:

    def __init__(self, sem):
        self.sem, self.n, self.queue, self.seen = sem, 0, [], {}

    def wait(self, *ticks):
        for t in ticks:
            if t is None:
                continue
            if isinstance(t, list):
                self.wait(*t)
                continue
            sem, val = t
            if self.seen.get(id(sem), 0) < val:
                self.seen[id(sem)] = val
                self.queue.append(("wait", sem, val))

    def put(self, fn, *ticks):
        self.wait(*ticks)
        self.queue.append(("do", fn, None, 0))

    def do(self, fn, *ticks):
        self.wait(*ticks)
        self.n += 1
        self.queue.append(("do", fn, self.sem, 1))
        return (self.sem, self.n)

    def dma(self, fn, count, *ticks):
        self.wait(*ticks)
        count.n += 16
        self.queue.append(("do", fn, count.sem, 16))
        return (count.sem, count.n)

    def play(self, eng):
        for item in self.queue:
            if item[0] == "wait":
                eng.wait_ge(item[1], item[2])
            else:
                ins = item[1](eng)
                if item[2] is not None:
                    ins.then_inc(item[2], item[3])


class Count:

    def __init__(self, sem):
        self.sem, self.n = sem, 0


def build(nc, t, out):
    ctx = ExitStack()
    with ctx:
        def sem(name):
            return ctx.enter_context(nc.semaphore(name))

        def count(name):
            return Count(sem(name))

        pe, dve, act, pool, sp = (Line(sem("n_" + n)) for n in ("pe", "dve", "act", "pool", "sp"))

        top = [0]

        arena = ctx.enter_context(nc.sbuf_tensor("arena", [128, 53200], F32))

        def carve(n):
            a = top[0]
            top[0] += n
            assert top[0] <= 53200, top[0]
            return a

        def view(at, n, dt=F32):
            v = arena[:, at:at + n]
            return v if dt == F32 else v.bitcast(dt)

        PS = ctx.enter_context(nc.psum_tensor("PS", [128, 8, 512], F32))
        PSf = PS[:, :, :].rearrange("p b n -> p (b n)")

        def ps(bank, a, b):
            return PSf[:, bank * 512 + a:bank * 512 + b]

        Xs = nc.dram_tensor("Xs", (NSLOT, D), F32, kind="Internal").ap()
        Ys = nc.dram_tensor("Ys", (NSLOT, D), F32, kind="Internal").ap()
        XN = nc.dram_tensor("XN", (T, D), F32, kind="Internal").ap()

        ACC = view(carve(NT * D), NT * D).rearrange("p (i d) -> p i d", i=NT)
        xnT = view(carve(2 * T), 2 * T).rearrange("p (c t) -> p c t", c=2)
        CST = view(carve(t["cst"].shape[1]), t["cst"].shape[1])
        ident, Uinc, Ustr, Lstr, sel = (CST[:, 128 * k:128 * k + 128] for k in range(5))
        iota8 = CST[:, 640:648]
        iota128 = CST[:, 648:680]
        iotaT = CST[:, 680:752]
        onerow = CST[:, 752:753]
        hsel = CST[:, 753:769]
        cbf = view(carve(256), 256, BF16)
        identb, M1b, M2b, M2p = (cbf[:, 128 * k:128 * k + 128] for k in range(4))
        ones = view(carve(128), 128)
        small = carve(560)
        MV = view(small, 64).rearrange("p (i k) -> p i k", k=2)
        ST6 = view(small + 64, 24).rearrange("p (i k) -> p i k", k=6)
        RS = view(small + 88, 32)
        EPS = view(small + 120, 1)
        RT = view(small + 122, 32)
        SS = view(small + 154, 32)
        W12 = view(small + 186, 64).rearrange("p (k i) -> p k i", k=2)
        POS = view(small + 250, 64, I32).rearrange("p (k i) -> p k i", k=2)
        TEXP = view(small + 314, 72)
        TEXI = view(small + 386, 72, I32)
        TMPS = view(small + 458, 96)
        EPS6 = view(small + 121, 1)
        B1S = view(carve(512), 512, BF16)
        B2S = view(carve(128), 128, BF16)
        SEL = view(carve(512), 512, BF16)
        base = top[0]

        c_cst, c_x = count("c_cst"), [count(f"c_x{b}") for b in range(NB)]
        k_cst = sp.dma(lambda e: e.dma_start(CST[:, :], t["cst"]), c_cst)
        k_cst = sp.dma(lambda e: e.dma_start(cbf.bitcast(F32), t["cbf"]), c_cst)
        xv = t["x"].rearrange("(b i p) d -> b p i d", b=NB, p=128)
        k_x = [sp.dma(lambda e, b=b: e.dma_start(ACC[:, 4 * b:4 * b + 4, :], xv[b]), c_x[b]) for b in range(NB)]
        k_ones = pool.do(lambda e: e.memset(ones[:, :], 1.0))
        k_eps = pool.do(lambda e: e.memset(EPS[:, :], 1.0e-5))
        k_eps = pool.do(lambda e: e.memset(EPS6[:, :], 1.0e-6))

        def norm_and_route(layer, ready, region, free, wr, kwr, nr):
            top[0] = region
            xnb = [view(carve(1024), 1024).rearrange("p (i d) -> p i d", i=4) for _ in range(2)]
            lgt = [view(carve(512), 512) for _ in range(2)]
            junk = view(carve(256), 256)
            lgall = view(carve(NT * nr), NT * nr).rearrange("p (i n) -> p i n", i=NT)
            c_xn = [count(f"c_xn{layer}{k}") for k in range(2)]
            xnd = XN.rearrange("(b i p) d -> b p i d", b=NB, p=128)
            k_T, k_lgt, k_lgev, k_store = [None] * NB, [None] * NB, [None] * NB, [None] * NB
            k_norm, k_tr, k_evp, k_lgp, k_sq = {}, {}, {}, {}, None
            for b in range(NB):
                k_st = None
                for j in range(4):
                    i = 4 * b + j
                    k1 = dve.do(lambda e, i=i, j=j: e.bn_stats(ST6[:, j, :], ACC[:, i, :]), ready[b], free, k_norm.get(b - 1))
                    k_st = dve.do(lambda e, i=i, j=j: e.bn_aggr(MV[:, i, :], ST6[:, j, :]), k1)
                k2 = act.do(lambda e, b=b: e.activation(RS[:, 4 * b:4 * b + 4], MV[:, 4 * b:4 * b + 4, 1], ACT.Sqrt, bias=EPS[:, :]), k_st, k_eps)
                k3 = dve.do(lambda e, b=b: e.reciprocal(RS[:, 4 * b:4 * b + 4], RS[:, 4 * b:4 * b + 4]), k2)
                for j in range(4):
                    i = 4 * b + j
                    k_norm[b] = dve.do(lambda e, i=i, b=b, j=j: e.tensor_scalar(
                        xnb[b % 2][:, j, :], ACC[:, i, :], MV[:, i, 0:1], RS[:, i:i + 1], ALU.subtract, ALU.mult),
                        k3, k_store[b - 2] if b > 1 else None, k_tr.get(b - 2), k_sq)
                k_store[b] = sp.dma(lambda e, b=b: e.dma_start(xnd[b], xnb[b % 2][:, :, :]), c_xn[b % 2], k_norm[b])
                if layer:
                    for j in range(4):
                        i = 4 * b + j
                        k_sq = act.do(lambda e, i=i, b=b, j=j: e.activation(junk[:, :], xnb[b % 2][:, j, :], ACT.Square, accum_out=SS[:, i:i + 1]), k_norm[b], k_sq)
                pb = 2 * (b % 2)
                for j in range(4):
                    for c in range(2):
                        f = lambda e, b=b, j=j, c=c, pb=pb: e.transpose(ps(pb + c, 128 * j, 128 * j + 128), xnb[b % 2][:, j, 128 * c:128 * c + 128], ident)
                        if j == 3 and c == 1:
                            k_tr[b] = pe.do(f)
                        else:
                            pe.put(f, k_norm[b], k_evp.get(b - 2), k_cst)
                e1 = act.do(lambda e, b=b, pb=pb: e.activation(xnT[:, 0, 512 * b:512 * b + 512], ps(pb, 0, 512), ACT.Copy), k_tr[b], free)
                e2 = dve.do(lambda e, b=b, pb=pb: e.tensor_copy(xnT[:, 1, 512 * b:512 * b + 512], ps(pb + 1, 0, 512)), k_tr[b], free)
                k_evp[b] = k_T[b] = [e1, e2]
                qb = 4 + b % 2
                pe.put(lambda e, b=b, qb=qb: e.matmul(PS[0:nr, qb, :], wr[:, 0, 0:nr], xnT[:, 0, 512 * b:512 * b + 512], start=True, stop=False), k_T[b], kwr, k_lgt[b - 2] if b > 1 else None)
                k4 = pe.do(lambda e, b=b, qb=qb: e.matmul(PS[0:nr, qb, :], wr[:, 1, 0:nr], xnT[:, 1, 512 * b:512 * b + 512], start=False, stop=True))
                k_lgt[b] = dve.do(lambda e, b=b, qb=qb: e.tensor_copy(lgt[b % 2][0:nr, :], PS[0:nr, qb, :]), k4, k_lgp.get(b - 2))
                tb = 6 + b % 2
                for j in range(4):
                    f = lambda e, b=b, j=j, tb=tb: e.transpose(ps(tb, nr * j, nr * j + nr), lgt[b % 2][0:nr, 128 * j:128 * j + 128], ident[0:nr, 0:nr])
                    if j == 3:
                        k_lgp[b] = pe.do(f)
                    else:
                        pe.put(f, k_lgt[b], k_lgev[b - 2] if b > 1 else None)
                k_lgev[b] = dve.do(lambda e, b=b, tb=tb: e.tensor_copy(lgall[:, 4 * b:4 * b + 4, :], ps(tb, 0, 4 * nr).rearrange("p (i n) -> p i n", i=4)), k_lgp[b])
            return k_T, k_lgev, lgall, k_store, k_sq

        def top2(lg, k_lg, layer):
            full = lambda: view(carve(256), 256).rearrange("p (i e) -> p i e", i=NT)
            M8, IXF, OH1, OH2, C, A, B = (full() for _ in range(7))
            IX = view(carve(256), 256, U32).rearrange("p (i e) -> p i e", i=NT)
            NTB = view(carve(256), 256).rearrange("p (e j) -> p e j", e=8)
            CMP = view(carve(7 * 72), 7 * 72).rearrange("p (i e) -> p i e", e=7)
            n8 = [view(carve(8), 8) for _ in range(6)]
            LG = full()
            bc = lambda ap: ap.to_broadcast([128, NT, 8])
            k = k_lg
            V = lambda f, *w: dve.do(f, *w)
            if layer == 0:
                k = V(lambda e: e.tensor_reduce(TMPS[:, 0:32], lg, AX.X, ALU.max), k)
                k = V(lambda e: e.tensor_tensor(A, lg, bc(TMPS[:, 0:32].unsqueeze(2)), ALU.subtract), k)
                k = act.do(lambda e: e.activation(A, A, ACT.Exp), k)
                k = V(lambda e: e.tensor_reduce(TMPS[:, 32:64], A, AX.X, ALU.add), k)
                k = V(lambda e: e.reciprocal(TMPS[:, 32:64], TMPS[:, 32:64]), k)
                k = V(lambda e: e.tensor_tensor(LG, A, bc(TMPS[:, 32:64].unsqueeze(2)), ALU.mult), k)
            else:
                k = V(lambda e: e.tensor_copy(LG, lg), k)
            for i in range(NT):
                k1 = V(lambda e, i=i: e.max(M8[:, i, :], LG[:, i, :]), k)
            for i in range(NT):
                k2 = V(lambda e, i=i: e.max_index(IX[:, i, :], M8[:, i, :], LG[:, i, :]), k1)
            k = V(lambda e: e.tensor_copy(IXF, IX), k2)
            i8 = iota8.unsqueeze(1).to_broadcast([128, NT, 8])
            V(lambda e: e.tensor_tensor(OH1, i8, bc(IXF[:, :, 0:1]), ALU.is_equal), k)
            k = V(lambda e: e.tensor_tensor(OH2, i8, bc(IXF[:, :, 1:2]), ALU.is_equal), k)
            k = V(lambda e: e.tensor_tensor(C, OH1, OH2, ALU.add), k)
            m1, m2 = M8[:, :, 0], M8[:, :, 1]
            if layer == 0:
                w = V(lambda e: e.tensor_tensor(TMPS[:, 0:32], m1, m2, ALU.add), k)
                w = V(lambda e: e.reciprocal(TMPS[:, 0:32], TMPS[:, 0:32]), w)
                w = V(lambda e: e.tensor_tensor(W12[:, 0, :], m1, TMPS[:, 0:32], ALU.mult), w)
                k_w = V(lambda e: e.tensor_tensor(W12[:, 1, :], m2, TMPS[:, 0:32], ALU.mult), w)
            else:
                w = V(lambda e: e.tensor_tensor(TMPS[:, 0:32], m2, m1, ALU.subtract), k)
                w = act.do(lambda e: e.activation(TMPS[:, 32:64], TMPS[:, 0:32], ACT.Exp), w)
                w = V(lambda e: e.tensor_scalar(TMPS[:, 0:32], TMPS[:, 32:64], 1.0, None, ALU.add), w)
                w = V(lambda e: e.reciprocal(W12[:, 0, :], TMPS[:, 0:32]), w)
                k_w = V(lambda e: e.tensor_tensor(W12[:, 1, :], TMPS[:, 32:64], W12[:, 0, :], ALU.mult), w)
            Cf = C.rearrange("p i e -> p (i e)")
            pe.put(lambda e: e.matmul(ps(6, 0, 256), Ustr, Cf, start=True, stop=True), k, k_lg)
            k = pe.do(lambda e: e.matmul(ps(7, 0, 256), ones[:, :], Cf, start=True, stop=True), k_ones)
            TOT = A
            k = V(lambda e: e.tensor_copy(TOT, ps(7, 0, 256).rearrange("p (i e) -> p i e", i=NT)), k)
            k = V(lambda e: e.tensor_copy(B, TOT), k)
            src, dst = B, IXF
            for st in (1, 2, 4, 8, 16):
                V(lambda e, st=st, s=src, d=dst: e.tensor_copy(d[:, 0:st, :], s[:, 0:st, :]), k)
                k = V(lambda e, st=st, s=src, d=dst: e.tensor_tensor(d[:, st:NT, :], s[:, st:NT, :], s[:, 0:NT - st, :], ALU.add), k)
                src, dst = dst, src
            cum, oth = src, dst
            n_e = cum[:, NT - 1, :]
            k = V(lambda e: e.tensor_tensor(NTB, n_e.unsqueeze(2).to_broadcast([128, 8, 32]),
                                            iota128.unsqueeze(1).to_broadcast([128, 8, 32]), ALU.is_gt), k)
            k = V(lambda e: e.tensor_reduce(n8[0], NTB, AX.X, ALU.add), k)
            a, b_ = n8[0], n8[1]
            for st in (1, 2, 4):
                V(lambda e, st=st, s=a, d=b_: e.tensor_copy(d[:, 0:st], s[:, 0:st]), k)
                k = V(lambda e, st=st, s=a, d=b_: e.tensor_tensor(d[:, st:8], s[:, st:8], s[:, 0:8 - st], ALU.add), k)
                if st == 1:
                    a, b_ = n8[1], n8[2]
                elif st == 2:
                    a, b_ = n8[2], n8[3]
            tend = n8[3]
            k = V(lambda e: e.tensor_tensor(n8[4], tend, n8[0], ALU.subtract), k)
            k = V(lambda e: e.tensor_scalar(n8[4], n8[4], 128.0, None, ALU.mult), k)
            k5 = V(lambda e: e.tensor_tensor(CMP[:, 0:NTILE, :], tend[:, 0:7].unsqueeze(1).to_broadcast([128, NTILE, 7]),
                                             iotaT[:, 0:NTILE].unsqueeze(2).to_broadcast([128, NTILE, 7]), ALU.is_le), k)
            k5 = V(lambda e: e.tensor_reduce(TEXP[:, 0:NTILE], CMP[:, 0:NTILE, :], AX.X, ALU.add), k5)
            k_tex = V(lambda e: e.tensor_copy(TEXI[:, 0:NTILE], TEXP[:, 0:NTILE]), k5)
            k = V(lambda e: e.tensor_tensor(oth, cum, TOT, ALU.subtract), k)
            k = V(lambda e: e.tensor_tensor(oth, oth, n8[4].unsqueeze(1).to_broadcast([128, NT, 8]), ALU.add), k)
            k = V(lambda e: e.tensor_tensor(oth, ps(6, 0, 256).rearrange("p (i e) -> p i e", i=NT), oth, ALU.add), k)
            for n, oh in enumerate((OH1, OH2)):
                k = V(lambda e, oh=oh: e.tensor_tensor(oh, oh, oth, ALU.mult), k)
                k = V(lambda e, n=n, oh=oh: e.tensor_reduce(TMPS[:, 64:96], oh, AX.X, ALU.add), k)
                k = V(lambda e, n=n: e.tensor_copy(POS[:, n, :], TMPS[:, 64:96]), k)
            return k_w, k_tex, k

        def scatter(layer, k_store, k_pos, k_clear, nring=4):
            ring = [view(carve(256), 256) for _ in range(nring)]
            cl = [count(f"c_sl{layer}{n}") for n in range(nring)]
            cs = [count(f"c_ss{layer}{n}") for n in range(nring)]
            used = [None] * nring
            ends = []
            for i in range(NT):
                r = i % nring
                k = sp.dma(lambda e, i=i, r=r: e.dma_start(ring[r][:, :], XN[128 * i:128 * i + 128, :]), cl[r], k_store, k_pos, used[r])
                for n in range(2):
                    used[r] = pool.dma(lambda e, i=i, r=r, n=n: e.indirect_dma_start(
                        Xs, bass.IndirectOffsetOnAxis(ap=POS[:, n, i:i + 1], axis=0), ring[r][:, :], None), cs[r], k, k_clear, k_pos)
            return [(c.sem, c.n) for c in cs]

        def moe(layer, F, WU, WD, k_wu, k_wd, k_scat, k_tex, biases, free):
            nf = F // 128
            nh = F // 512
            xr = [view(carve(256), 256) for _ in range(3)]
            xt = [view(carve(256), 256) for _ in range(2)]
            h = [view(carve(F), F) for _ in range(2)]
            hT = [view(carve(F), F) for _ in range(2)]
            y = [view(carve(256), 256) for _ in range(2)]
            NH, NHT = len(h), len(hT)
            cl = [count(f"c_ml{layer}{n}") for n in range(3)]
            cy = [count(f"c_my{layer}{n}") for n in range(2)]
            load = {}
            k_xtp, k_xte, k_up, k_gelu, k_tr, k_hte, k_dn, k_ye, k_ys = ({} for _ in range(9))
            UPB = [1, 1 + nh]
            HTB = 1 + 2 * nh
            YB = 7
            val = {}

            def expert(e, i):
                val[i] = e.value_load(TEXI[0:1, i:i + 1], min_val=0, max_val=7)

            def load_in(i):
                if i < NTILE:
                    load[i] = sp.dma(lambda e, i=i: e.dma_start(xr[i % 3][:, :], Xs[128 * i:128 * i + 128, :]), cl[i % 3], k_scat, k_xtp.get(i - 3), free)

            def xtr(i):
                if i >= NTILE:
                    return
                for c in range(2):
                    f = lambda e, i=i, c=c: e.transpose(ps(0, 256 * (i % 2) + 128 * c, 256 * (i % 2) + 128 * c + 128), xr[i % 3][:, 128 * c:128 * c + 128], ident)
                    if c:
                        k_xtp[i] = pe.do(f)
                    else:
                        pe.put(f, load[i], k_xte.get(i - 1), free)
                k_xte[i] = dve.do(lambda e, i=i: e.tensor_copy(xt[i % 2][:, :], ps(0, 256 * (i % 2), 256 * (i % 2) + 256)), k_xtp[i], k_up.get(i - 2), free)

            def up(i):
                if i >= NTILE:
                    return
                pe.wait(k_xte[i], k_gelu.get(i - 2), k_wu, k_tex, free)
                pe.queue.append(("do", lambda e, i=i: expert(e, i), None, 0))
                for n in range(nh):
                    for c in range(2):
                        def f(e, i=i, n=n, c=c):
                            return e.matmul(ps(UPB[i % 2] + n, 0, 512), xt[i % 2][:, 128 * c:128 * c + 128],
                                            WU[:, bass.ds(val[i] * (2 * F) + (c * F + 512 * n), 512)],
                                            start=(c == 0), stop=(c == 1 and biases is None))
                        last = f
                        if biases is None and n == nh - 1 and c == 1:
                            k_up[i] = pe.do(f)
                        else:
                            pe.put(f)
                    if biases is not None:
                        def f(e, i=i, n=n):
                            return e.matmul(ps(UPB[i % 2] + n, 0, 512), biases[2][:, bass.ds(val[i] * 128, 128)],
                                            biases[0][:, 512 * n:512 * n + 512], start=False, stop=True)
                        if n == nh - 1:
                            k_up[i] = pe.do(f)
                        else:
                            pe.put(f)
                k_gelu[i] = act.do(lambda e, i=i: e.activation(h[i % NH][:, :], ps(UPB[i % 2], 0, F), ACT.Gelu), k_up[i], k_tr.get(i - NH), free)

            def htr(i):
                for c in range(nf):
                    f = lambda e, i=i, c=c: e.transpose(ps(HTB, 128 * c, 128 * c + 128), h[i % NH][:, 128 * c:128 * c + 128], ident)
                    if c == nf - 1:
                        k_tr[i] = pe.do(f)
                    else:
                        pe.put(f, k_gelu[i], k_hte.get(i - 1))
                k_hte[i] = dve.do(lambda e, i=i: e.tensor_copy(hT[i % NHT][:, :], ps(HTB, 0, F)), k_tr[i], k_dn.get(i - NHT), free)

            def down(i):
                pe.wait(k_hte[i], k_ye.get(i - 1), k_wd)
                o = 256 * (i % 2)
                for c in range(nf):
                    def f(e, i=i, c=c, o=o):
                        return e.matmul(ps(YB, o, o + 256), hT[i % NHT][:, 128 * c:128 * c + 128],
                                        WD[:, bass.ds(val[i] * (nf * 256) + c * 256, 256)], start=(c == 0), stop=(c == nf - 1 and biases is None))
                    if biases is None and c == nf - 1:
                        k_dn[i] = pe.do(f)
                    else:
                        pe.put(f)
                if biases is not None:
                    k_dn[i] = pe.do(lambda e, i=i, o=o: e.matmul(ps(YB, o, o + 256), biases[2][:, bass.ds(val[i] * 128, 128)],
                                                                biases[1][:, :], start=False, stop=True))
                k_ye[i] = act.do(lambda e, i=i, o=o: e.activation(y[i % 2][:, :], ps(YB, o, o + 256), ACT.Copy), k_dn[i], k_ys.get(i - 2), free)
                k_ys[i] = sp.dma(lambda e, i=i: e.dma_start(Ys[128 * i:128 * i + 128, :], y[i % 2][:, :]), cy[i % 2], k_ye[i], free)

            load_in(0), load_in(1), load_in(2)
            xtr(0), xtr(1)
            up(0)
            for i in range(NTILE):
                load_in(i + 3)
                htr(i)
                up(i + 1)
                xtr(i + 2)
                down(i)
            return [(c.sem, c.n) for c in cy], [k_dn[NTILE - 1], k_ye[NTILE - 1]]

        def combine(layer, k_y, k_w, k_acc, free):
            G = [view(carve(256), 256) for _ in range(6)]
            cg = [count(f"c_g{layer}{n}") for n in range(6)]
            used = [None] * 6
            done = []
            m = 0
            for i in range(NT):
                for n in range(2):
                    r = m % 6
                    m += 1
                    k = pool.dma(lambda e, i=i, n=n, r=r: e.indirect_dma_start(
                        G[r][:, :], None, Ys, bass.IndirectOffsetOnAxis(ap=POS[:, n, i:i + 1], axis=0)), cg[r], k_y, used[r], free)
                    used[r] = dve.do(lambda e, i=i, n=n, r=r: e.scalar_tensor_tensor(
                        ACC[:, i, :], G[r][:, :], W12[:, n, i:i + 1], ACC[:, i, :], ALU.mult, ALU.add), k, k_w, k_acc[i // 4], used[(m - 2) % 6])
                if i % 4 == 3:
                    done.append(used[(m - 1) % 6])
            return done

        WRV = view(carve(16), 16).rearrange("p (c n) -> p c n", c=2)
        c_wr, c_w = count("c_wr"), count("c_w")
        k_wr = sp.dma(lambda e: e.dma_start(WRV[:, :, :], t["Wg"]), c_wr)
        ATT = top[0]
        WQ = view(carve(512), 512).rearrange("p (c n) -> p c n", c=2)
        WK = view(carve(512), 512).rearrange("p (c n) -> p c n", c=2)
        WV = view(carve(512), 512).rearrange("p (c n) -> p c n", c=2)
        WO = view(carve(1024), 1024).rearrange("p (g n) -> p g n", g=4)
        for dst, name in ((WQ, "Wq"), (WK, "Wk"), (WV, "Wv"), (WO, "Wo")):
            k_w = sp.dma(lambda e, d=dst, n=name: e.dma_start(d[:, :, :], t[n]), c_w)
        Vb = [view(carve(2048), 2048).rearrange("p (i h d) -> p i h d", i=4, h=16) for _ in range(2)]
        STK = [[view(carve(2048), 2048, BF16).rearrange("p (j s) -> p j s", j=8) for _ in range(2)] for _ in range(3)]
        OT = [view(carve(512), 512) for _ in range(4)]
        RC = view(carve(512), 512)
        PT = [view(carve(768), 768, BF16).rearrange("p (k s) -> p k s", k=3) for _ in range(2)]
        R1 = [view(carve(512), 512) for _ in range(2)]
        NM = [view(carve(32), 32).rearrange("p (i j) -> p i j", i=4) for _ in range(2)]
        NM2 = view(carve(32), 32).rearrange("p (i j) -> p i j", i=4)
        NP = [view(carve(48), 48, BF16).rearrange("p (i k j) -> p i k j", i=4, k=3) for _ in range(2)]
        MT = [view(carve(256), 256, BF16) for _ in range(2)]
        ring0 = carve(1024)
        NPB = 6
        PREG = carve(NPB * 1280)
        PB = [view(PREG + 1280 * n, 1280) for n in range(NPB)]
        att_end = top[0]
        ZERO = view(PREG, 256)
        k_T, k_lg, lgall, k_store, _ = norm_and_route(0, k_x, PREG + 256, None, WRV, k_wr, 8)
        c_z = count("c_z")
        kz = pool.do(lambda e: e.memset(ZERO[:, :], 0.0))
        k_zero = sp.dma(lambda e: e.dma_start(Xs.rearrange("(i p) d -> p i d", p=128), ZERO.unsqueeze(1).to_broadcast([128, NTILE, 256])), c_z, kz)
        k_w12, k_tex, k_pos = top2(lgall, k_lg[-1], 0)
        assert top[0] <= att_end
        top[0] = ring0
        k_scat = scatter(0, k_store[-2:], k_pos, k_zero)
        k_pre = [k_pos, k_zero, k_tex, k_w12, *k_store[-2:]]
        free = []
        k_vinit = [pool.do(lambda e, v=v: e.memset(v, 0.0), *free) for v in Vb]
        k_vinit = [pool.do(lambda e, v=v: e.memset(v[:, :, :, 16:17], 1.0), *k_vinit) for v in Vb][-1]
        k_init = k_vinit
        for n in range(3):
            for m in range(2):
                k_init = pool.do(lambda e, s=STK[n][m]: e.memset(s[96:128, :, :], 0.0), k_init)
        for n in range(3):
            k_init = pool.do(lambda e, s=STK[n][1]: e.memset(s[96:99, :, :], 1.0), k_init)
        c_st = [[count(f"c_st{n}{m}") for m in range(2)] for n in range(3)]
        c_m = [count(f"c_m{n}") for n in range(3)]
        SLOTS = [[0, 0, 1, 1, 0, 2], [0, 1, 0, 1, 2, 0]]
        off = {3: 0, 2: 512, 0: 896, 1: 1024}
        offT = {0: 0, 1: 512, 3: 896, 2: 1024}
        SB0, TB0, OB, MB = 0, 3, 6, 7
        k_mb = [k_pos]
        k_stack, k_mrow, k_s, k_red, k_st_, k_exp, k_pv, k_pt, k_v = ({} for _ in range(9))
        k_pt_free = [None, None]
        k_stk_dma = {}
        NHB = 2 * NB

        def project(n):
            b, half = divmod(n, 2)
            if half == 0:
                vb = Vb[b % 2]
                for i in range(4):
                    for c in range(2):
                        f = lambda e, i=i, c=c: e.matmul(ps(MB, 0, 256), xnT[:, c, 512 * b + 128 * i:512 * b + 128 * i + 128], WV[:, c, :], start=(c == 0), stop=(c == 1))
                        if c:
                            k = pe.do(f)
                        else:
                            pe.put(f, k_T[b], k_w, k_mb[0], *free)
                    k_mb[0] = k_v[b] = act.do(lambda e, i=i, vb=vb: e.activation(vb[:, i, :, 0:16], ps(MB, 0, 256).rearrange("p (h d) -> p h d", h=16), ACT.Copy), k, k_vinit, k_pv.get((2 * b - 3, 1)))
            for m, W in enumerate((WQ, WK)):
                for c in range(2):
                    f = lambda e, m=m, W=W, c=c: e.matmul(ps(MB, 0, 512), W[:, c, 128 * half:128 * half + 128], xnT[:, c, 512 * b:512 * b + 512], start=(c == 0), stop=(c == 1))
                    if c:
                        k = pe.do(f)
                    else:
                        pe.put(f, k_T[b], k_w, k_mb[0], *free)
                pt, r1 = PT[m], R1[m]
                k1 = act.do(lambda e, pt=pt: e.activation(pt[:, 0, :], ps(MB, 0, 512), ACT.Copy), k, k_pt_free[m], *free)
                k2 = dve.do(lambda e, pt=pt, r1=r1: e.tensor_tensor(r1[:, :], ps(MB, 0, 512), pt[:, 0, :], ALU.subtract), k1, k_pt_free[m])
                k_mb[0] = k2
                k3 = pool.do(lambda e, pt=pt, r1=r1: e.tensor_copy(pt[:, 1, :], r1[:, :]), k2, k_init)
                k4 = pool.do(lambda e, pt=pt, r1=r1: e.tensor_tensor(pt[:, 2, :], r1[:, :], pt[:, 1, :], ALU.subtract), k3)
                dst = STK[n % 3][m]
                kk = None
                for sl, part in enumerate(SLOTS[m]):
                    for j in range(8):
                        kk = sp.dma(lambda e, dst=dst, pt=pt, sl=sl, part=part, j=j: e.dma_start(
                            dst[16 * sl:16 * sl + 16, j, :], pt[16 * j:16 * j + 16, part, :]),
                            c_st[n % 3][m], k4, k_st_.get((n - 3, 7)), k_s.get((n - 3, 7)), *free)
                k_pt_free[m] = kk
                k_stack[n, m] = kk

        def scores(n, j):
            q, k = STK[n % 3]
            for i in (3, 2, 0, 1):
                w = 128 * (i + 1)
                pe.put(lambda e, i=i, w=w: e.matmul(ps(SB0, off[i], off[i] + w), q[0:96, j, 128 * i:128 * i + 128], k[0:96, j, 0:w], start=True, stop=False),
                       k_stack[n, 0], k_stack[n, 1], k_red.get((n, j - 1)) if j else k_red.get((n - 1, 7)), k_init)
                kk = pe.do(lambda e, i=i, w=w: e.matmul(ps(SB0, off[i] + w - 128, off[i] + w), identb, M1b, start=False, stop=True))
                for r in {3: (3,), 2: (), 0: (2, 0), 1: (1,)}[i]:
                    k_red[n, j] = dve.do(lambda e, r=r: e.tensor_reduce(NM[n % 2][:, r, j:j + 1], ps(SB0, off[r], off[r] + 128 * (r + 1)), AX.X, ALU.max, negate=True), kk, k_pt.get(n - 2), *free)
            k_s[n, j] = kk

        def maxima(n):
            nm, np_, mt = NM[n % 2], NP[n % 2], MT[n % 2]
            k1 = dve.do(lambda e: e.tensor_copy(np_[:, :, 0, :], nm), k_red[n, 7], k_pt.get(n - 2))
            k1 = dve.do(lambda e: e.tensor_tensor(NM2, nm, np_[:, :, 0, :], ALU.subtract), k1)
            k1 = dve.do(lambda e: e.tensor_copy(np_[:, :, 1, :], NM2), k1)
            k1 = dve.do(lambda e: e.tensor_tensor(np_[:, :, 2, :], NM2, np_[:, :, 1, :], ALU.subtract), k1)
            pmt = ps(MB, 0, 256).bitcast(BF16)
            for i in range(4):
                f = lambda e, i=i: e.transpose(pmt[0:24, 128 * i:128 * i + 128], np_[:, i, :, :].rearrange("p k j -> p (k j)"), identb)
                if i == 3:
                    k_pt[n] = pe.do(f)
                else:
                    pe.put(f, k1, k_mb[0])
            k2 = act.do(lambda e: e.activation(mt[0:24, :], pmt[0:24, :], ACT.Copy), k_pt[n], k_mrow.get(n - 2), *free)
            k_mb[0] = k2
            for k in range(3):
                k_mrow[n] = sp.dma(lambda e, k=k: e.dma_start(STK[n % 3][0][96 + k:97 + k, :, :], mt[8 * k:8 * k + 8, :]), c_m[n % 3], k2, k_s[n, 7], k_st_.get((n - 3, 7)), k_init)

        def scoresT(n, j):
            q, k = STK[n % 3]
            prev = (n, j - 1) if j else (n - 1, 7)
            for kb in (0, 1, 3, 2):
                w = 512 - 128 * kb
                pe.put(lambda e, kb=kb, w=w: e.matmul(ps(TB0, offT[kb], offT[kb] + w), k[:, j, 128 * kb:128 * kb + 128], q[:, j, 128 * kb:512], start=True, stop=False),
                       k_mrow[n], k_exp.get(prev))
                kk = pe.do(lambda e, kb=kb: e.matmul(ps(TB0, offT[kb], offT[kb] + 128), identb, M2b, start=False, stop=True))
            k_st_[n, j] = kk
            idx = 8 * n + j
            o = idx - NPB
            k_exp[n, j] = act.do(lambda e: e.activation(PB[idx % NPB][:, :], ps(TB0, 0, 1280), ACT.Exp, scale=0.25), kk, k_pv.get((o // 8, (o % 8) // 4)) if o >= 0 else None, *k_pre)

        def values(n, g):
            b, half = divmod(n, 2)
            vb = Vb[b % 2]
            for kb in range(4):
                w = 512 - 128 * kb
                for j in range(4):
                    jj = 4 * g + j
                    p = PB[(8 * n + jj) % NPB]
                    f = lambda e, kb=kb, j=j, jj=jj, p=p, w=w: e.matmul(
                        PS[32 * j:32 * j + 32, OB, 128 * kb:512], vb[:, kb, 8 * half + jj, :], p[:, offT[kb]:offT[kb] + w], start=(kb == 0), stop=(kb == 3))
                    if kb == 3 and j == 3:
                        k_pv[n, g] = pe.do(f)
                    else:
                        pe.put(f, k_exp[n, jj], k_v[b], k_ob[0])
            G = 2 * half + g
            ot = OT[G]
            k1 = act.do(lambda e: e.activation(ot[:, :], ps(OB, 0, 512), ACT.Copy), k_pv[n, g], k_wo.get(b - 1), *free)
            k_ob[0] = k1
            k2 = pe.do(lambda e: e.matmul(ps(MB, 0, 512), sel, ot[:, :], start=True, stop=True), k1, k_mb[0])
            k3 = dve.do(lambda e: e.reciprocal(RC[:, :], ps(MB, 0, 512)), k2, k_nrm[0])
            k_mb[0] = k3
            k_nrm[0] = pool.do(lambda e: e.tensor_tensor(ot[:, :], ot[:, :], RC[:, :], ALU.mult), k3, k2)

        def output(b):
            for i in range(4):
                for g in range(4):
                    f = lambda e, i=i, g=g: e.matmul(ps(MB, 0, 256), OT[g][:, 128 * i:128 * i + 128], WO[:, g, :], start=(g == 0), stop=(g == 3))
                    if g == 3:
                        k = pe.do(f)
                    else:
                        pe.put(f, k_nrm[0], k_mb[0])
                k_wo[b] = k
                k_acc0[b] = k_mb[0] = dve.do(lambda e, i=i: e.tensor_tensor(ACC[:, 4 * b + i, :], ps(MB, 0, 256), ACC[:, 4 * b + i, :], ALU.add), k)

        k_ob, k_nrm, k_wo, k_acc0 = [k_pos], [None], {}, {}
        project(0)
        project(1)
        for j in range(8):
            scores(0, j)
        maxima(0)
        for n in range(NHB):
            if n + 2 < NHB:
                project(n + 2)
            for j in range(8):
                if n + 1 < NHB:
                    scores(n + 1, j)
                scoresT(n, j)
                if j == 5:
                    values(n, 0)
            if n + 1 < NHB:
                maxima(n + 1)
            values(n, 1)
            if n % 2:
                output(n // 2)

        top[0] = ATT
        free = [k_wo[NB - 1], k_nrm[0], k_acc0[NB - 1]]
        W1 = view(carve(1024), 1024).rearrange("p (c n) -> p c n", c=2)
        W2 = view(carve(1024), 1024).rearrange("p (c n) -> p c n", c=4)
        hs = [view(carve(2048), 2048).rearrange("p (c n) -> p c n", c=4) for _ in range(2)]
        WU = view(carve(8192), 8192)
        WD = view(carve(8192), 8192)
        c_w0, c_wu, c_wd = count("c_w0"), count("c_wu"), count("c_wd")
        k_w0 = sp.dma(lambda e: e.dma_start(W1[:, :, :], t["W1"]), c_w0, *free)
        k_w0 = sp.dma(lambda e: e.dma_start(W2[:, :, :], t["W2"]), c_w0)
        for q in range(4):
            k_wu = sp.dma(lambda e, q=q: e.dma_start(WU[:, 2048 * q:2048 * q + 2048], t["Wu"][:, 2048 * q:2048 * q + 2048]), c_wu)
        for q in range(4):
            k_wd = sp.dma(lambda e, q=q: e.dma_start(WD[:, 2048 * q:2048 * q + 2048], t["Wd"][:, 2048 * q:2048 * q + 2048]), c_wd)
        k_g, k_h, k_dn, k_acc1 = {}, {}, {}, {}

        def shared_up(b):
            for fc in range(4):
                bank = (4 * b + fc) % 4
                for c in range(2):
                    f = lambda e, fc=fc, c=c, bank=bank: e.matmul(ps(bank, 0, 512), W1[:, c, 128 * fc:128 * fc + 128], xnT[:, c, 512 * b:512 * b + 512], start=(c == 0), stop=(c == 1))
                    if c:
                        k = pe.do(f)
                    else:
                        pe.put(f, k_w0, k_g.get((b - 1, fc)), *free)
                k_g[b, fc] = act.do(lambda e, fc=fc, bank=bank: e.activation(hs[b % 2][:, fc, :], ps(bank, 0, 512), ACT.Gelu), k, k_dn.get(b - 2), *free)

        def shared_down(b):
            for i in range(4):
                bank = 4 + i
                for fc in range(4):
                    f = lambda e, i=i, fc=fc, bank=bank: e.matmul(ps(bank, 0, 256), hs[b % 2][:, fc, 128 * i:128 * i + 128], W2[:, fc, :], start=(fc == 0), stop=(fc == 3))
                    if fc == 3:
                        k_dn[b] = pe.do(f)
                    else:
                        pe.put(f, k_g[b, 3], k_acc1.get(b - 1), *free)
                k_acc1[b] = dve.do(lambda e, i=i, bank=bank: e.tensor_tensor(ACC[:, 4 * b + i, :], ps(bank, 0, 256), ACC[:, 4 * b + i, :], ALU.add), k_dn[b], k_acc0[b])

        shared_up(0)
        for b in range(NB):
            if b + 1 < NB:
                shared_up(b + 1)
            shared_down(b)
        free2 = [*free, k_dn[NB - 1], k_acc1[NB - 1]]
        k_y, k_end = moe(0, F0, WU, WD, k_wu, k_wd, k_scat, k_tex, None, free2)
        k_x1 = combine(0, k_y, k_w12, k_acc1, [*free, *k_end])

        top[0] = base
        fre = [*k_end, k_x1[-1]]
        WCR = view(carve(64), 64).rearrange("p (c n) -> p c n", c=2)
        NW = view(carve(2), 2)
        QKW = view(carve(1536), 1536).rearrange("p (c n) -> p c n", c=2)
        WOUT = view(carve(512), 512).rearrange("p (c n) -> p c n", c=2)
        COS = view(carve(128), 128).rearrange("p (i d) -> p i d", i=4)
        SIN = view(carve(128), 128).rearrange("p (i d) -> p i d", i=4)
        GB = view(carve(24), 24)
        RB = view(carve(8), 8)
        BO = view(carve(256), 256)
        LREG = top[0]
        bsp = view(LREG, 1024)
        c_w1, c_br = count("c_w1"), count("c_br")
        ends = [k_dn[NB - 1], *k_end]
        for dst, name in ((WCR, "Wcr"), (NW, "nw"), (QKW, "Wqkv"), (WOUT, "Wout"), (COS, "cos"), (SIN, "sin"), (GB, "gb"), (RB, "rb"), (BO, "bo"), (SEL.bitcast(F32), "sel")):
            k_w1 = sp.dma(lambda e, d=dst, n=name: e.dma_start(d, t[n]), c_w1, *ends)
        k_nw = k_w1
        for c in range(2):
            k_nw = pool.do(lambda e, c=c: e.tensor_scalar(QKW[:, c, :], QKW[:, c, :], NW[:, c:c + 1], None, ALU.mult), k_w1)
            k_nw = pool.do(lambda e, c=c: e.tensor_scalar(WCR[:, c, 8:32], WCR[:, c, 8:32], NW[:, c:c + 1], None, ALU.mult), k_w1)
        k_b3 = pool.do(lambda e: e.memset(B1S, 0.0), *ends)
        k_b3 = pool.do(lambda e: e.memset(B2S, 0.0), *ends)
        c_bl = count("c_bl")
        bf = view(LREG, 1280)
        b3 = view(LREG + 1280, 3 * 640, BF16).rearrange("p (k n) -> p k n", k=3)
        kb = sp.dma(lambda e: e.dma_start(bf[0:8, 0:1024], t["b1"]), c_bl, *ends)
        kb = sp.dma(lambda e: e.dma_start(bf[0:8, 1024:1280], t["b2"]), c_bl)
        for k in range(3):
            kb = pool.do(lambda e, k=k: e.tensor_copy(b3[0:8, k, :], bf[0:8, :]), kb)
            if k < 2:
                kb = pool.do(lambda e, k=k: e.tensor_tensor(bf[0:8, :], bf[0:8, :], b3[0:8, k, :], ALU.subtract), kb)
        for k in range(3):
            k_br = sp.dma(lambda e, k=k: e.dma_start(B1S[8 * k:8 * k + 8, :], b3[0:8, k, 0:1024]), c_br, kb, k_b3)
            k_br = sp.dma(lambda e, k=k: e.dma_start(B2S[8 * k:8 * k + 8, :], b3[0:8, k, 1024:1280]), c_br, kb, k_b3)

        k_T, k_lg, lgall, k_store, k_sq = norm_and_route(1, k_x1, LREG, [*fre, k_br], WCR, [k_nw], 32)
        TB = top[0]
        GZ = view(carve(NT * 24), NT * 24).rearrange("p (i n) -> p i n", i=NT)
        LRT = view(carve(256), 256).rearrange("p (i e) -> p i e", i=NT)
        k = dve.do(lambda e: e.tensor_tensor(LRT, lgall[:, :, 0:8], RB.unsqueeze(1).to_broadcast([128, NT, 8]), ALU.add), k_lg[-1], k_w1)
        kr = act.do(lambda e: e.activation(RT[:, :], SS[:, :], ACT.Sqrt, bias=EPS6[:, :], scale=1.0 / D), k_sq)
        kr = dve.do(lambda e: e.reciprocal(RT[:, :], RT[:, :]), kr)
        kz = dve.do(lambda e: e.tensor_tensor(GZ, lgall[:, :, 8:32], RT.unsqueeze(2).to_broadcast([128, NT, 24]), ALU.mult), kr)
        kz = dve.do(lambda e: e.tensor_tensor(GZ, GZ, GB.unsqueeze(1).to_broadcast([128, NT, 24]), ALU.add), kz)
        kz = act.do(lambda e: e.activation(GZ, GZ, ACT.Exp, scale=-1.0), kz)
        kz = dve.do(lambda e: e.tensor_scalar(GZ, GZ, 2.0 ** 62, 1.0, ALU.min, ALU.add), kz)
        k_w12, k_tex, k_pos = top2(LRT, k, 1)
        k_scat = scatter(1, k_store[-2:], k_pos, None)
        TBE = max(top[0], LREG + 9800)
        top[0] = TBE
        g_r, g_o = (view(carve(256), 256).rearrange("p (i h) -> p i h", i=NT) for _ in range(2))
        LF, EF, EU = (view(carve(256), 256).rearrange("p (i h) -> p i h", i=NT) for _ in range(3))
        ETA = view(carve(512), 512).rearrange("p (g i h) -> p g i h", g=2, i=NT)
        ET = view(carve(64), 64).rearrange("p (g i) -> p g i", g=2)
        kl = act.do(lambda e: e.activation(LF, GZ[:, :, 0:8], ACT.Ln), kz, *fre)
        kg = dve.do(lambda e: e.reciprocal(GZ[:, :, 8:24], GZ[:, :, 8:24]), kz)
        rb = RT.unsqueeze(2).to_broadcast([128, NT, 8])
        kg = dve.do(lambda e: e.tensor_tensor(GZ[:, :, 8:24], GZ[:, :, 8:24], RT.unsqueeze(2).to_broadcast([128, NT, 16]), ALU.mult), kg)
        kg1 = dve.do(lambda e: e.tensor_scalar(g_r, GZ[:, :, 8:16], float(1.0 / np.sqrt(32.0)), None, ALU.mult), kg)
        k_gates = dve.do(lambda e: e.tensor_copy(g_o, GZ[:, :, 16:24]), kg)
        LFf = LF.rearrange("p i h -> p (i h)")
        kd = None
        for n, (mat, dst) in enumerate(((Uinc, EF), (Lstr, EU), (ones, None))):
            kd = pe.do(lambda e, mat=mat: e.matmul(ps(0, 0, 256), mat[:, :], LFf, start=True, stop=True), kl, kd, k_T[-1])
            if dst is not None:
                kd = act.do(lambda e, dst=dst: e.activation(dst, ps(0, 0, 256).rearrange("p (i h) -> p i h", i=NT), ACT.Exp, scale=-1.0), kd, *fre)
            else:
                for g in range(2):
                    kd = act.do(lambda e, g=g: e.activation(ETA[:, g, :, :], ps(0, 0, 256).rearrange("p (i h) -> p i h", i=NT), ACT.Exp, scale=-1.0), kd)
        for g in range(2):
            kd = dve.do(lambda e, g=g: e.tensor_tensor(ETA[:, g, :, :], ETA[:, g, :, :], hsel[:, 8 * g:8 * g + 8].unsqueeze(1).to_broadcast([128, NT, 8]), ALU.mult), kd)
        k_dec = dve.do(lambda e: e.tensor_reduce(ET, ETA, AX.X, ALU.add), kd)

        MST = view(carve(2048), 2048).rearrange("p (b g n) -> p b g n", b=NB, g=2)
        R0 = top[0]
        top[0] = LREG
        lf = [k_pos, k_gates, k_dec, kg1, *k_scat]
        T1, T2 = (view(carve(512), 512).rearrange("p (h d) -> p h d", h=16) for _ in range(2))
        QO2, QE2, KR2, KD2, VP2 = ([view(carve(256), 256) for _ in range(2)] for _ in range(5))
        LU = view(carve(1024), 1024).rearrange("p (h n) -> p h n", h=8)
        DD2 = [view(carve(1024), 1024).rearrange("p (g n) -> p g n", g=2) for _ in range(2)]
        QB = [view(carve(512), 512).rearrange("p (j n) -> p j n", j=4) for _ in range(2)]
        QET = view(carve(256), 256)
        KT = view(carve(256), 256)
        WT = [view(carve(512), 512) for _ in range(2)]
        YT = view(carve(256), 256)
        XB = view(carve(256), 256)
        assert top[0] <= TBE, (top[0], TBE)
        h8 = lambda ap: ap.rearrange("p (h d) -> p h d", h=8)
        kq0 = pool.do(lambda e: e.memset(QB[0], 0.0), *lf)
        kq0 = pool.do(lambda e: e.memset(QB[1], 0.0), *lf)
        order = [4 * b + c for c in range(4) for b in range(NB)]
        K = {}
        k_m = {}
        k_acc2 = {}

        def front(i, p, pp, par):
            c4 = i % 4
            QO, QE, KR, KD, VP, DD = (z[par] for z in (QO2, QE2, KR2, KD2, VP2, DD2))
            tok = slice(128 * i, 128 * i + 128)
            for c in range(2):
                f = lambda e, c=c: e.matmul(ps(0, 0, 512), xnT[:, c, tok], QKW[:, c, 0:512], start=(c == 0), stop=(c == 1))
                if c:
                    kqk = pe.do(f)
                else:
                    pe.put(f, k_T[-1], k_nw, K.get(("rope", p)), *lf)
            for c in range(2):
                f = lambda e, c=c: e.matmul(ps(1, 0, 256), xnT[:, c, tok], QKW[:, c, 512:768], start=(c == 0), stop=(c == 1))
                if c:
                    kv = pe.do(f)
                else:
                    pe.put(f, K.get(("vp", p)))
            a = pool.do(lambda e: e.tensor_tensor(LU, Uinc.unsqueeze(1).to_broadcast([128, 8, 128]), LF[:, i, :].unsqueeze(2).to_broadcast([128, 8, 128]), ALU.mult), K.get(("D", p)), kbd, *lf)
            for g in range(2):
                pe.put(lambda e, g=g: e.matmul(ps(2 + g, 0, 512), Lstr, LU[:, 4 * g:4 * g + 4, :].rearrange("p h n -> p (h n)"), start=True, stop=False), a, K.get(("DD", p)))
                kD = pe.do(lambda e, g=g: e.matmul(ps(2 + g, 0, 512).rearrange("p (h n) -> p h n", h=4), identb, M2p.unsqueeze(1).to_broadcast([128, 4, 128]), start=False, stop=True))
            K["D", i] = kD
            q3 = ps(0, 0, 512).rearrange("p (h d) -> p h d", h=16)
            cs, sn = COS[:, c4, :], SIN[:, c4, :]
            bc = lambda ap: ap.unsqueeze(1).to_broadcast([128, 16, ap.shape[1]])
            r1 = dve.do(lambda e: e.tensor_tensor(T1, q3, bc(cs), ALU.mult), kqk, K.get(("rot", p)), *lf)
            dve.put(lambda e: e.tensor_tensor(T2[:, :, 0:16], q3[:, :, 16:32], bc(sn[:, 0:16]), ALU.mult), K.get(("rot", p)))
            r2 = dve.do(lambda e: e.tensor_tensor(T2[:, :, 16:32], q3[:, :, 0:16], bc(sn[:, 16:32]), ALU.mult))
            K["rope", i] = r2
            rr = pool.do(lambda e: e.tensor_tensor(T1, T1, T2, ALU.add), r2)
            hb = lambda ap: ap.unsqueeze(2).to_broadcast([128, 8, 32])
            a1 = pool.do(lambda e: e.tensor_tensor(h8(QO), T1[:, 0:8, :], hb(g_o[:, i, :]), ALU.mult), rr, K.get(("T", pp)))
            a2 = pool.do(lambda e: e.tensor_scalar(h8(KR), T1[:, 8:16, :], RT[:, i:i + 1], None, ALU.mult), K.get(("T", pp)))
            K["rot", i] = a2
            a3 = pool.do(lambda e: e.tensor_tensor(h8(QE), h8(QO), hb(EF[:, i, :]), ALU.mult), a1, K.get(("T", pp)))
            a4 = pool.do(lambda e: e.tensor_tensor(h8(KD), h8(KR), hb(EU[:, i, :]), ALU.mult), a2, K.get(("dM", pp)))
            K["pre", i] = a4
            K["vp", i] = dve.do(lambda e: e.tensor_tensor(h8(VP), h8(ps(1, 0, 256)), hb(g_r[:, i, :]), ALU.mult), kv, K.get(("dM", pp)))
            K["DD", i] = act.do(lambda e: e.activation(DD, PS[:, 2:4, :], ACT.Exp, scale=-1.0), kD, K.get(("W", pp)), *lf)

        def back(i, p, par):
            b, c4 = divmod(i, 4)
            QO, QE, KR, KD, VP, DD = (z[par] for z in (QO2, QE2, KR2, KD2, VP2, DD2))
            for g in range(2):
                for n, src in enumerate((QO, KR, QE)):
                    if n == 2 and c4 == 0:
                        continue
                    f = lambda e, g=g, n=n, src=src: e.transpose(ps(4 + g, 128 * n, 128 * n + 128), src[:, 128 * g:128 * g + 128], ident)
                    kt = pe.do(f, K["pre", i], K.get(("ev", p)), K.get(("acc", p)), K.get(("dMe", p)))
            K["T", i] = kt
            ev = []
            for g in range(2):
                def copy(dst, src, *ticks, g=g):
                    if g == 0:
                        return act.do(lambda e: e.activation(dst, src, ACT.Copy), *ticks)
                    return dve.do(lambda e: e.tensor_copy(dst, src), *ticks)
                for j in range(4):
                    ev.append(copy(QB[g][32 * j:32 * j + 32, j, :], PS[32 * j:32 * j + 32, 4 + g, 0:128], kt, K.get(("A", p)), kq0))
                ev.append(copy(KT[:, 128 * g:128 * g + 128], ps(4 + g, 128, 256), kt, K.get(("A", p))))
                if c4:
                    ev.append(copy(QET[:, 128 * g:128 * g + 128], ps(4 + g, 256, 384), kt, K.get(("Y", p))))
            K["ev", i] = [ev[-1], *ev]
            for g in range(2):
                kA = pe.do(lambda e, g=g: e.matmul(ps(6, 0, 512), KT[:, 128 * g:128 * g + 128], QB[g].rearrange("p j n -> p (j n)"), start=True, stop=True), *ev, K.get(("W", p)) if g == 0 else K.get(("W", i)))
                K["W", i] = dve.do(lambda e, g=g: e.tensor_tensor(WT[g][:, :], ps(6, 0, 512), DD[:, g, :], ALU.mult), kA, K["DD", i], K.get(("Y", p)))
            K["A", i] = kA
            for g in range(2):
                if c4:
                    pe.put(lambda e, g=g: e.matmul(ps(7, 128 * g, 128 * g + 128), MST[:, b, g, :], QET[:, 128 * g:128 * g + 128], start=True, stop=False, skip_group_check=True), k_m[b], K.get(("ye", p)))
                for j in range(4):
                    h = 4 * g + j
                    kY = pe.do(lambda e, g=g, j=j, h=h: e.matmul(PS[32 * j:32 * j + 32, 7, 128 * g:128 * g + 128], VP[:, 32 * h:32 * h + 32], WT[g][:, 128 * j:128 * j + 128],
                                                                start=(c4 == 0), stop=True, skip_group_check=True), K["W", i], K["vp", i], K.get(("ye", p)))
            K["Y", i] = kY
            for g in range(2):
                kM = pe.do(lambda e, g=g: e.matmul(ps(5, 128 * g, 128 * g + 128), KD[:, 128 * g:128 * g + 128], VP[:, 128 * g:128 * g + 128], start=True, stop=True, skip_group_check=True))
            K["dM", i] = kM
            K["ye", i] = act.do(lambda e: e.activation(YT[:, :], ps(7, 0, 256), ACT.Copy), kY, K.get(("O", p)))
            for g in range(2):
                if c4 == 0:
                    km = dve.do(lambda e, g=g: e.tensor_tensor(MST[:, b, g, :], ps(5, 128 * g, 128 * g + 128), BD, ALU.mult), kM, kbd)
                else:
                    k1 = dve.do(lambda e, g=g: e.tensor_tensor(MTMP[:, :], ps(5, 128 * g, 128 * g + 128), BD, ALU.mult), kM, kbd, k_m[b] if g == 0 else km)
                    km = dve.do(lambda e, g=g: e.scalar_tensor_tensor(MST[:, b, g, :], MST[:, b, g, :], ET[:, g, i:i + 1], MTMP[:, :], ALU.mult, ALU.add), k1, kY)
            k_m[b] = km
            K["dMe", i] = km
            for g in range(2):
                kO = pe.do(lambda e, g=g: e.matmul(ps(4, 0, 256), YT[:, 128 * g:128 * g + 128], WOUT[:, g, :], start=(g == 0), stop=(g == 1)), K["ye", i], K["ev", i])
            K["O", i] = kO
            kx = pool.do(lambda e: e.tensor_tensor(XB[:, :], ACC[:, i, :], BO[:, :], ALU.add), K.get(("acc", p)), k_w1)
            K["acc", i] = k_acc2[i] = dve.do(lambda e: e.tensor_tensor(ACC[:, i, :], ps(4, 0, 256), XB[:, :], ALU.add), kO, kx)

        top[0] = R0
        BD = view(carve(128), 128)
        MTMP = view(carve(128), 128)
        REND = top[0]
        kbd = pool.do(lambda e: e.memset(BD[:, :], 0.0), kq0, *fre)
        for j in range(4):
            kbd = pool.do(lambda e, j=j: e.memset(BD[32 * j:32 * j + 32, 32 * j:32 * j + 32], 1.0), kbd)
        front(order[0], None, None, 0)
        for n, i in enumerate(order):
            before = order[n - 1] if n else None
            if n + 1 < len(order):
                front(order[n + 1], i, before, (n + 1) % 2)
            back(i, before, n % 2)
        last = order[-1]
        fre1 = [K["O", last], K["acc", last], K["dMe", last], K["W", last]]
        top[0] = base
        WU1 = view(carve(16384), 16384)
        WD1 = view(carve(16384), 16384)
        c_u1 = count("c_u1")
        for q in range(8):
            k_u1 = sp.dma(lambda e, q=q: e.dma_start(WU1[:, 2048 * q:2048 * q + 2048], t["w1"][:, 2048 * q:2048 * q + 2048]), c_u1, *fre1)
        for q in range(8):
            k_u1 = sp.dma(lambda e, q=q: e.dma_start(WD1[:, 2048 * q:2048 * q + 2048], t["w2"][:, 2048 * q:2048 * q + 2048]), c_u1, *fre1)
        top[0] = NT * D
        k_y, k_end = moe(1, F1, WU1, WD1, k_u1, k_u1, k_scat, k_tex, (B1S, B2S, SEL), [*fre1, k_br])
        kacc = [k_acc2[4 * b + 3] for b in range(NB)]
        k_o = combine(1, k_y, k_w12, [K["acc", last]] * NB, [*fre1, *k_end])
        c_o = count("c_o")
        ov = out.rearrange("(b i p) d -> b p i d", b=NB, p=128)
        for b in range(NB):
            sp.dma(lambda e, b=b: e.dma_start(ov[b], ACC[:, 4 * b:4 * b + 4, :]), c_o, k_o[b])
        sp.wait((c_o.sem, c_o.n))

        block = ctx.enter_context(nc.Block())
        block.sync(sp.play)
        block.gpsimd(pool.play)
        block.scalar(act.play)
        block.tensor(pe.play)
        block.vector(dve.play)


def kernel(**inputs):
    import concourse.bacc as bacc
    from concourse.bass_utils import run_bass_kernel_spmd as run

    a = {k: np.ascontiguousarray(v) for k, v in inputs.items()}
    f32 = np.float32

    def rows(w):
        c = w.shape[0] // 128
        return np.ascontiguousarray(w.reshape(c, 128, -1).transpose(1, 0, 2))

    def experts(w):
        e, k, n = w.shape
        return np.ascontiguousarray(w.reshape(e, k // 128, 128, n).transpose(2, 0, 1, 3).reshape(128, -1))

    def over(v):
        return np.ascontiguousarray(np.broadcast_to(v, (128, v.shape[-1])))

    r = np.arange(128)
    ident = np.eye(128, dtype=f32)
    uinc = (r[:, None] <= r[None, :]).astype(f32)
    ustr = (r[:, None] < r[None, :]).astype(f32)
    lstr = (r[:, None] > r[None, :]).astype(f32)
    sel = (r[:, None] == 32 * (r[None, :] // 32) + 16).astype(f32)
    hsel = np.concatenate([(4 * g + r[:, None] // 32 == np.arange(8)[None, :]).astype(f32) for g in range(2)], 1)
    one = np.zeros((128, 1), f32)
    cst = np.concatenate([ident, uinc, ustr, lstr, sel, over(np.arange(8, dtype=f32)), over(128 * np.arange(32, dtype=f32)),
                          over(np.arange(72, dtype=f32)), one, hsel], 1).astype(f32)
    bfb = mybir.dt.np(BF16)
    cbf = np.concatenate([ident, np.where(r[None, :] > r[:, None], NEG, 0.0), np.where(r[None, :] < r[:, None], NEG, 0.0),
                          np.where(r[None, :] < r[:, None], -NEG, 0.0)], 1).astype(bfb)
    cbf = np.ascontiguousarray(cbf).view(f32)
    half = 16
    selx = np.zeros((128, 8, 128), f32)
    for e in range(8):
        selx[[e, 8 + e, 16 + e], e, :] = 1.0
    selx = np.ascontiguousarray(selx.reshape(128, 1024).astype(bfb)).view(f32)
    inv = (1.0 / np.power(f32(10000.0), np.arange(half, dtype=f32) / f32(half))).astype(f32)
    fr = np.arange(S, dtype=f32)[:, None] * inv[None, :]
    cos, sin = np.cos(fr.astype(np.float64)).astype(f32), np.sin(fr.astype(np.float64)).astype(f32)
    cos = np.concatenate([cos, cos], 1).reshape(4, 128, 32).transpose(1, 0, 2)
    sin = np.concatenate([-sin, sin], 1).reshape(4, 128, 32).transpose(1, 0, 2)
    wo = np.zeros((4, 4, 32, D), f32)
    wo[:, :, 0:16, :] = a["L0_attn_Wo"].T.reshape(4, 4, 16, D)
    arrays = {
        "x": a["L0_attn_in_features"].reshape(T, D),
        "cst": cst, "cbf": cbf,
        "Wg": rows(a["L0_ffn_Wg"]),
        "Wq": rows(a["L0_attn_Wq"].T), "Wk": rows(a["L0_attn_Wk"].T), "Wv": rows(a["L0_attn_Wv"].T),
        "Wo": np.ascontiguousarray(wo.reshape(4, 128, D).transpose(1, 0, 2)),
        "W1": rows(a["L0_ffn_W1"]), "W2": rows(a["L0_ffn_W2"]),
        "Wu": experts(a["L0_ffn_Wu"]), "Wd": experts(a["L0_ffn_Wd"]),
        "Wcr": rows(np.concatenate([a["L1_ffn_router_w"], a["L1_attn_Wbeta"].T, a["L1_attn_Wig"].T, a["L1_attn_Wog"].T], 1)),
        "nw": np.ascontiguousarray(a["L1_attn_norm_w"].reshape(2, 128).T),
        "Wqkv": rows(np.concatenate([a["L1_attn_Wq"].T, a["L1_attn_Wk"].T, a["L1_attn_Wv"].T], 1)),
        "Wout": rows(a["L1_attn_Wout"].T),
        "cos": np.ascontiguousarray(cos), "sin": np.ascontiguousarray(sin),
        "gb": over(np.concatenate([a["L1_attn_bbeta"], a["L1_attn_big"], a["L1_attn_bog"]])),
        "rb": over(a["L1_ffn_router_b"]), "bo": over(a["L1_attn_bout"]),
        "b1": a["L1_ffn_b1"], "b2": a["L1_ffn_b2"],
        "sel": selx, "w1": experts(a["L1_ffn_w1"]), "w2": experts(a["L1_ffn_w2"]),
    }
    nc = bacc.Bacc("TRN2", target_bir_lowering=False, num_devices=1)
    t = {n: nc.dram_tensor("in_" + n, v.shape, mybir.dt.from_np(v.dtype), kind="ExternalInput").ap() for n, v in arrays.items()}
    out = nc.dram_tensor("out_0", (T, D), F32, kind="ExternalOutput").ap()
    build(nc, t, out)
    res = run(nc, [{"in_" + n: np.ascontiguousarray(v) for n, v in arrays.items()}], core_ids=[0])
    return res.results[0]["out_0"].reshape(NB, S, D)
```

```python
from contextlib import ExitStack

import numpy as np
import concourse.bass as bass
from concourse import mybir

F32 = mybir.dt.float32
BF16 = mybir.dt.bfloat16
I32 = mybir.dt.int32
U32 = mybir.dt.uint32
ALU = mybir.AluOpType
ACT = mybir.ActivationFunctionType
AX = mybir.AxisListType

NB, S, D = 8, 512, 256
T = NB * S
NT = T // 128
E = 8
NTILE = (2 * T + E * 127) // 128
NSLOT = NTILE * 128
F0, F1 = 512, 1024
NEG = -1.0e30
LIMIT = 53200


class Line:

    def __init__(self, sem):
        self.sem, self.n, self.queue, self.seen = sem, 0, [], {}

    def wait(self, *ticks):
        for t in ticks:
            if t is None:
                continue
            if isinstance(t, list):
                self.wait(*t)
                continue
            sem, val = t
            if self.seen.get(id(sem), 0) < val:
                self.seen[id(sem)] = val
                self.queue.append(("wait", sem, val))

    def put(self, fn, *ticks):
        self.wait(*ticks)
        self.queue.append(("do", fn, None, 0))

    def do(self, fn, *ticks):
        self.wait(*ticks)
        self.n += 1
        self.queue.append(("do", fn, self.sem, 1))
        return (self.sem, self.n)

    def dma(self, fn, count, *ticks):
        self.wait(*ticks)
        count.n += 16
        self.queue.append(("do", fn, count.sem, 16))
        return (count.sem, count.n)

    def play(self, eng):
        for item in self.queue:
            if item[0] == "wait":
                eng.wait_ge(item[1], item[2])
            else:
                ins = item[1](eng)
                if item[2] is not None:
                    ins.then_inc(item[2], item[3])


class Count:

    def __init__(self, sem):
        self.sem, self.n = sem, 0


def build(nc, t, out):
    ctx = ExitStack()
    with ctx:
        def sem(name):
            return ctx.enter_context(nc.semaphore(name))

        def count(name):
            return Count(sem(name))

        pe, dve, act, pool, sp = (Line(sem("n_" + n)) for n in ("pe", "dve", "act", "pool", "sp"))

        top = [0]

        arena = ctx.enter_context(nc.sbuf_tensor("arena", [128, 53200], F32))

        def carve(n):
            a = top[0]
            top[0] += n
            assert top[0] <= LIMIT, top[0]
            return a

        def view(at, n, dt=F32):
            v = arena[:, at:at + n]
            return v if dt == F32 else v.bitcast(dt)

        PS = ctx.enter_context(nc.psum_tensor("PS", [128, 8, 512], F32))
        PSf = PS[:, :, :].rearrange("p b n -> p (b n)")

        def ps(bank, a, b):
            return PSf[:, bank * 512 + a:bank * 512 + b]

        Xs = nc.dram_tensor("Xs", (NSLOT, D), F32, kind="Internal").ap()
        Ys = nc.dram_tensor("Ys", (NSLOT, D), F32, kind="Internal").ap()
        SPL = nc.dram_tensor("SPL", (3, 2, 128, 3, S), BF16, kind="Internal").ap()
        XN = nc.dram_tensor("XN", (T, D), F32, kind="Internal").ap()

        ACC = view(carve(NT * D), NT * D).rearrange("p (i d) -> p i d", i=NT)
        xnT = view(carve(2 * T), 2 * T).rearrange("p (c t) -> p c t", c=2)
        CST = view(carve(t["cst"].shape[1]), t["cst"].shape[1])
        ident, Uinc, Ustr, Lstr, sel = (CST[:, 128 * k:128 * k + 128] for k in range(5))
        iota8 = CST[:, 640:648]
        iota128 = CST[:, 648:680]
        iotaT = CST[:, 680:752]
        onerow = CST[:, 752:753]
        hsel = CST[:, 753:769]
        cbf = view(carve(256), 256, BF16)
        identb, M1b, M2b, M2p = (cbf[:, 128 * k:128 * k + 128] for k in range(4))
        ones = view(carve(128), 128)
        small = carve(560)
        MV = view(small, 64).rearrange("p (i k) -> p i k", k=2)
        ST6 = view(small + 64, 24).rearrange("p (i k) -> p i k", k=6)
        RS = view(small + 88, 32)
        EPS = view(small + 120, 1)
        RT = view(small + 122, 32)
        SS = view(small + 154, 32)
        W12 = view(small + 186, 64).rearrange("p (k i) -> p k i", k=2)
        POS = view(small + 250, 64, I32).rearrange("p (k i) -> p k i", k=2)
        TEXP = view(small + 314, 72)
        TEXI = view(small + 386, 72, I32)
        TMPS = view(small + 458, 96)
        EPS6 = view(small + 121, 1)
        B1S = view(carve(512), 512, BF16)
        B2S = view(carve(128), 128, BF16)
        SEL = view(carve(512), 512, BF16)
        base = top[0]

        c_cst, c_x = count("c_cst"), [count(f"c_x{b}") for b in range(NB)]
        k_cst = sp.dma(lambda e: e.dma_start(CST[:, :], t["cst"]), c_cst)
        k_cst = sp.dma(lambda e: e.dma_start(cbf.bitcast(F32), t["cbf"]), c_cst)
        xv = t["x"].rearrange("(b i p) d -> b p i d", b=NB, p=128)
        k_x = [sp.dma(lambda e, b=b: e.dma_start(ACC[:, 4 * b:4 * b + 4, :], xv[b]), c_x[b]) for b in range(NB)]
        k_ones = pool.do(lambda e: e.memset(ones[:, :], 1.0))
        k_eps = pool.do(lambda e: e.memset(EPS[:, :], 1.0e-5))
        k_eps = pool.do(lambda e: e.memset(EPS6[:, :], 1.0e-6))

        def norm_and_route(layer, ready, region, free, wr, kwr, nr, lgall, freeT):
            top[0] = region
            xnb = [view(carve(1024), 1024).rearrange("p (i d) -> p i d", i=4) for _ in range(2)]
            lgt = [view(carve(512), 512) for _ in range(2)]
            junk = view(carve(256), 256)
            lgall = lgall.rearrange("p (i n) -> p i n", i=NT)
            k_last = {}
            c_xn = [count(f"c_xn{layer}{k}") for k in range(2)]
            xnd = XN.rearrange("(b i p) d -> b p i d", b=NB, p=128)
            k_T, k_lgt, k_lgev, k_store = [None] * NB, [None] * NB, [None] * NB, [None] * NB
            k_norm, k_tr, k_evp, k_lgp, k_sq = {}, {}, {}, {}, None
            res = (k_T, k_lgev, lgall, k_store, k_last)
            yield res
            for b in range(NB):
                k_st = None
                for j in range(4):
                    i = 4 * b + j
                    k1 = dve.do(lambda e, i=i, j=j: e.bn_stats(ST6[:, j, :], ACC[:, i, :]), ready[b], free, k_norm.get(b - 1))
                    k_st = dve.do(lambda e, i=i, j=j: e.bn_aggr(MV[:, i, :], ST6[:, j, :]), k1)
                k2 = act.do(lambda e, b=b: e.activation(RS[:, 4 * b:4 * b + 4], MV[:, 4 * b:4 * b + 4, 1], ACT.Sqrt, bias=EPS[:, :]), k_st, k_eps)
                k3 = dve.do(lambda e, b=b: e.reciprocal(RS[:, 4 * b:4 * b + 4], RS[:, 4 * b:4 * b + 4]), k2)
                for j in range(4):
                    i = 4 * b + j
                    k_norm[b] = dve.do(lambda e, i=i, b=b, j=j: e.tensor_scalar(
                        xnb[b % 2][:, j, :], ACC[:, i, :], MV[:, i, 0:1], RS[:, i:i + 1], ALU.subtract, ALU.mult),
                        k3, k_store[b - 2] if b > 1 else None, k_tr.get(b - 2), k_sq)
                k_store[b] = sp.dma(lambda e, b=b: e.dma_start(xnd[b], xnb[b % 2][:, :, :]), c_xn[b % 2], k_norm[b])
                if layer:
                    for j in range(4):
                        i = 4 * b + j
                        k_sq = act.do(lambda e, i=i, b=b, j=j: e.activation(junk[:, :], xnb[b % 2][:, j, :], ACT.Square, accum_out=SS[:, i:i + 1]), k_norm[b], k_sq)
                pb, qb, tb = (4, 6, 7) if layer else (2 * (b % 2), 4 + b % 2, 6 + b % 2)
                ago = 1 if layer else 2
                for j in range(4):
                    for c in range(2):
                        f = lambda e, b=b, j=j, c=c, pb=pb: e.transpose(ps(pb + c, 128 * j, 128 * j + 128), xnb[b % 2][:, j, 128 * c:128 * c + 128], ident)
                        if j == 3 and c == 1:
                            k_tr[b] = pe.do(f)
                        else:
                            pe.put(f, k_norm[b], k_evp.get(b - ago), k_cst)
                e1 = act.do(lambda e, b=b, pb=pb: e.activation(xnT[:, 0, 512 * b:512 * b + 512], ps(pb, 0, 512), ACT.Copy), k_tr[b], free, freeT[b])
                e2 = dve.do(lambda e, b=b, pb=pb: e.tensor_copy(xnT[:, 1, 512 * b:512 * b + 512], ps(pb + 1, 0, 512)), k_tr[b], free, freeT[b])
                k_evp[b] = k_T[b] = [e1, e2]
                pe.put(lambda e, b=b, qb=qb: e.matmul(PS[0:nr, qb, :], wr[:, 0, 0:nr], xnT[:, 0, 512 * b:512 * b + 512], start=True, stop=False), k_T[b], kwr, k_lgt[b - ago] if b >= ago else None)
                k4 = pe.do(lambda e, b=b, qb=qb: e.matmul(PS[0:nr, qb, :], wr[:, 1, 0:nr], xnT[:, 1, 512 * b:512 * b + 512], start=False, stop=True))
                k_lgt[b] = dve.do(lambda e, b=b, qb=qb: e.tensor_copy(lgt[b % 2][0:nr, :], PS[0:nr, qb, :]), k4, k_lgp.get(b - 2))
                for j in range(4):
                    f = lambda e, b=b, j=j, tb=tb: e.transpose(ps(tb, nr * j, nr * j + nr), lgt[b % 2][0:nr, 128 * j:128 * j + 128], ident[0:nr, 0:nr])
                    if j == 3:
                        k_lgp[b] = pe.do(f)
                    else:
                        pe.put(f, k_lgt[b], k_lgev[b - ago] if b >= ago else None)
                k_lgev[b] = dve.do(lambda e, b=b, tb=tb: e.tensor_copy(lgall[:, 4 * b:4 * b + 4, :], ps(tb, 0, 4 * nr).rearrange("p (i n) -> p i n", i=4)), k_lgp[b])
                k_last.update(sq=k_sq, pe=k_lgp[b], norm=k_norm[b])
                yield res

        def top2(lg, k_lg, layer, bank, res):
            full = lambda: view(carve(256), 256).rearrange("p (i e) -> p i e", i=NT)
            two = carve(512)
            M8 = view(two, 256).rearrange("p (i e) -> p i e", i=NT)
            LG = view(two + 256, 256).rearrange("p (i e) -> p i e", i=NT)
            NTB = view(two, 256).rearrange("p (e j) -> p e j", e=8)
            CMP = view(two, 7 * 72).rearrange("p (i e) -> p i e", e=7)
            ix = carve(256)
            IX = view(ix, 256, U32).rearrange("p (i e) -> p i e", i=NT)
            IXF = view(ix, 256).rearrange("p (i e) -> p i e", i=NT)
            OH1, OH2, C, A, B = (full() for _ in range(5))
            n8 = [view(carve(8), 8) for _ in range(5)]
            bc = lambda ap: ap.to_broadcast([128, NT, 8])
            k = k_lg
            V = lambda f, *w: dve.do(f, *w)
            if layer == 0:
                k = V(lambda e: e.tensor_reduce(TMPS[:, 0:32], lg, AX.X, ALU.max), k)
                k = V(lambda e: e.tensor_tensor(A, lg, bc(TMPS[:, 0:32].unsqueeze(2)), ALU.subtract), k)
                k = act.do(lambda e: e.activation(A, A, ACT.Exp), k)
                k = V(lambda e: e.tensor_reduce(TMPS[:, 32:64], A, AX.X, ALU.add), k)
                k = V(lambda e: e.reciprocal(TMPS[:, 32:64], TMPS[:, 32:64]), k)
                k = V(lambda e: e.tensor_tensor(LG, A, bc(TMPS[:, 32:64].unsqueeze(2)), ALU.mult), k)
            else:
                k = V(lambda e: e.tensor_copy(LG, lg), k)
            yield
            for i in range(NT):
                if i % 6 == 5:
                    yield
                k1 = V(lambda e, i=i: e.max(M8[:, i, :], LG[:, i, :]), k)
            for i in range(NT):
                if i % 4 == 3:
                    yield
                k2 = V(lambda e, i=i: e.max_index(IX[:, i, :], M8[:, i, :], LG[:, i, :]), k1)
            k = V(lambda e: e.tensor_copy(IXF, IX), k2)
            i8 = iota8.unsqueeze(1).to_broadcast([128, NT, 8])
            V(lambda e: e.tensor_tensor(OH1, i8, bc(IXF[:, :, 0:1]), ALU.is_equal), k)
            k = V(lambda e: e.tensor_tensor(OH2, i8, bc(IXF[:, :, 1:2]), ALU.is_equal), k)
            k = V(lambda e: e.tensor_tensor(C, OH1, OH2, ALU.add), k)
            m1, m2 = M8[:, :, 0], M8[:, :, 1]
            if layer == 0:
                w = V(lambda e: e.tensor_tensor(TMPS[:, 0:32], m1, m2, ALU.add), k)
                w = V(lambda e: e.reciprocal(TMPS[:, 0:32], TMPS[:, 0:32]), w)
                w = V(lambda e: e.tensor_tensor(W12[:, 0, :], m1, TMPS[:, 0:32], ALU.mult), w)
                k_w = V(lambda e: e.tensor_tensor(W12[:, 1, :], m2, TMPS[:, 0:32], ALU.mult), w)
            else:
                w = V(lambda e: e.tensor_tensor(TMPS[:, 0:32], m2, m1, ALU.subtract), k)
                w = act.do(lambda e: e.activation(TMPS[:, 32:64], TMPS[:, 0:32], ACT.Exp), w)
                w = V(lambda e: e.tensor_scalar(TMPS[:, 0:32], TMPS[:, 32:64], 1.0, None, ALU.add), w)
                w = V(lambda e: e.reciprocal(W12[:, 0, :], TMPS[:, 0:32]), w)
                k_w = V(lambda e: e.tensor_tensor(W12[:, 1, :], TMPS[:, 32:64], W12[:, 0, :], ALU.mult), w)
            Cf = C.rearrange("p i e -> p (i e)")
            yield
            pe.put(lambda e: e.matmul(ps(bank[1], 0, 256), Ustr, Cf, start=True, stop=True), k, k_lg, bank[0])
            k = pe.do(lambda e: e.matmul(ps(bank[1], 256, 512), ones[:, :], Cf, start=True, stop=True), k_ones)
            TOT = A
            k = V(lambda e: e.tensor_copy(TOT, ps(bank[1], 256, 512).rearrange("p (i e) -> p i e", i=NT)), k)
            k = V(lambda e: e.tensor_copy(C, ps(bank[1], 0, 256).rearrange("p (i e) -> p i e", i=NT)), k)
            bank[0] = k
            k = V(lambda e: e.tensor_copy(B, TOT), k)
            yield
            src, dst = B, IXF
            for st in (1, 2, 4, 8, 16):
                V(lambda e, st=st, s=src, d=dst: e.tensor_copy(d[:, 0:st, :], s[:, 0:st, :]), k)
                k = V(lambda e, st=st, s=src, d=dst: e.tensor_tensor(d[:, st:NT, :], s[:, st:NT, :], s[:, 0:NT - st, :], ALU.add), k)
                src, dst = dst, src
            cum, oth = src, dst
            n_e = cum[:, NT - 1, :]
            yield
            k = V(lambda e: e.tensor_tensor(NTB, n_e.unsqueeze(2).to_broadcast([128, 8, 32]),
                                            iota128.unsqueeze(1).to_broadcast([128, 8, 32]), ALU.is_gt), k)
            k = V(lambda e: e.tensor_reduce(n8[0], NTB, AX.X, ALU.add), k)
            a, b_ = n8[0], n8[1]
            for st in (1, 2, 4):
                V(lambda e, st=st, s=a, d=b_: e.tensor_copy(d[:, 0:st], s[:, 0:st]), k)
                k = V(lambda e, st=st, s=a, d=b_: e.tensor_tensor(d[:, st:8], s[:, st:8], s[:, 0:8 - st], ALU.add), k)
                if st == 1:
                    a, b_ = n8[1], n8[2]
                elif st == 2:
                    a, b_ = n8[2], n8[3]
            tend = n8[3]
            yield
            k = V(lambda e: e.tensor_tensor(n8[4], tend, n8[0], ALU.subtract), k)
            k = V(lambda e: e.tensor_scalar(n8[4], n8[4], 128.0, None, ALU.mult), k)
            k5 = V(lambda e: e.tensor_tensor(CMP[:, 0:NTILE, :], tend[:, 0:7].unsqueeze(1).to_broadcast([128, NTILE, 7]),
                                             iotaT[:, 0:NTILE].unsqueeze(2).to_broadcast([128, NTILE, 7]), ALU.is_le), k)
            k5 = V(lambda e: e.tensor_reduce(TEXP[:, 0:NTILE], CMP[:, 0:NTILE, :], AX.X, ALU.add), k5)
            k_tex = V(lambda e: e.tensor_copy(TEXI[:, 0:NTILE], TEXP[:, 0:NTILE]), k5)
            k = V(lambda e: e.tensor_tensor(oth, cum, TOT, ALU.subtract), k)
            k = V(lambda e: e.tensor_tensor(oth, oth, n8[4].unsqueeze(1).to_broadcast([128, NT, 8]), ALU.add), k)
            k = V(lambda e: e.tensor_tensor(oth, C, oth, ALU.add), k)
            yield
            for n, oh in enumerate((OH1, OH2)):
                k = V(lambda e, oh=oh: e.tensor_tensor(oh, oh, oth, ALU.mult), k)
                k = V(lambda e, n=n, oh=oh: e.tensor_reduce(TMPS[:, 64:96], oh, AX.X, ALU.add), k)
                k = V(lambda e, n=n: e.tensor_copy(POS[:, n, :], TMPS[:, 64:96]), k)
            res.update(w12=k_w, tex=k_tex, pos=k)

        def scatter(layer, k_store, k_pos, k_clear, res, nring=4):
            ring = [view(carve(256), 256) for _ in range(nring)]
            cl = [count(f"c_sl{layer}{n}") for n in range(nring)]
            cs = [count(f"c_ss{layer}{n}") for n in range(nring)]
            used = [None] * nring
            for i in range(NT):
                yield
                r = i % nring
                k = sp.dma(lambda e, i=i, r=r: e.dma_start(ring[r][:, :], XN[128 * i:128 * i + 128, :]), cl[r], k_store, k_pos, used[r])
                for n in range(2):
                    used[r] = pool.dma(lambda e, i=i, r=r, n=n: e.indirect_dma_start(
                        Xs, bass.IndirectOffsetOnAxis(ap=POS[:, n, i:i + 1], axis=0), ring[r][:, :], None), cs[r], k, k_clear, k_pos)
            res["scat"] = [(c.sem, c.n) for c in cs]
            yield

        def moe(layer, F, WU, WD, k_wu, k_wd, k_scat, k_tex, biases, free):
            nf = F // 128
            nh = F // 512
            xr = [view(carve(256), 256) for _ in range(3)]
            xt = [view(carve(256), 256) for _ in range(2)]
            h = [view(carve(F), F) for _ in range(2)]
            hT = [view(carve(F), F) for _ in range(2)]
            y = [view(carve(256), 256) for _ in range(2)]
            NH, NHT = len(h), len(hT)
            cl = [count(f"c_ml{layer}{n}") for n in range(3)]
            cy = [count(f"c_my{layer}{n}") for n in range(2)]
            load = {}
            k_xtp, k_xte, k_up, k_gelu, k_tr, k_hte, k_dn, k_ye, k_ys = ({} for _ in range(9))
            UPB = [1, 1 + nh]
            HTB = 1 + 2 * nh
            YB = 7
            val = {}

            def expert(e, i):
                val[i] = e.value_load(TEXI[0:1, i:i + 1], min_val=0, max_val=7)

            def load_in(i):
                if i < NTILE:
                    load[i] = sp.dma(lambda e, i=i: e.dma_start(xr[i % 3][:, :], Xs[128 * i:128 * i + 128, :]), cl[i % 3], k_scat, k_xtp.get(i - 3), free)

            def xtr(i):
                if i >= NTILE:
                    return
                for c in range(2):
                    f = lambda e, i=i, c=c: e.transpose(ps(0, 256 * (i % 2) + 128 * c, 256 * (i % 2) + 128 * c + 128), xr[i % 3][:, 128 * c:128 * c + 128], ident)
                    if c:
                        k_xtp[i] = pe.do(f)
                    else:
                        pe.put(f, load[i], k_xte.get(i - 1), free)
                k_xte[i] = dve.do(lambda e, i=i: e.tensor_copy(xt[i % 2][:, :], ps(0, 256 * (i % 2), 256 * (i % 2) + 256)), k_xtp[i], k_up.get(i - 2), free)

            def up(i):
                if i >= NTILE:
                    return
                pe.wait(k_xte[i], k_gelu.get(i - 2), k_wu, k_tex, free)
                pe.queue.append(("do", lambda e, i=i: expert(e, i), None, 0))
                for n in range(nh):
                    for c in range(2):
                        def f(e, i=i, n=n, c=c):
                            return e.matmul(ps(UPB[i % 2] + n, 0, 512), xt[i % 2][:, 128 * c:128 * c + 128],
                                            WU[:, bass.ds(val[i] * (2 * F) + (c * F + 512 * n), 512)],
                                            start=(c == 0), stop=(c == 1 and biases is None))
                        last = f
                        if biases is None and n == nh - 1 and c == 1:
                            k_up[i] = pe.do(f)
                        else:
                            pe.put(f)
                    if biases is not None:
                        def f(e, i=i, n=n):
                            return e.matmul(ps(UPB[i % 2] + n, 0, 512), biases[2][:, bass.ds(val[i] * 128, 128)],
                                            biases[0][:, 512 * n:512 * n + 512], start=False, stop=True)
                        if n == nh - 1:
                            k_up[i] = pe.do(f)
                        else:
                            pe.put(f)
                k_gelu[i] = act.do(lambda e, i=i: e.activation(h[i % NH][:, :], ps(UPB[i % 2], 0, F), ACT.Gelu), k_up[i], k_tr.get(i - NH), free)

            def htr(i):
                for c in range(nf):
                    f = lambda e, i=i, c=c: e.transpose(ps(HTB, 128 * c, 128 * c + 128), h[i % NH][:, 128 * c:128 * c + 128], ident)
                    if c == nf - 1:
                        k_tr[i] = pe.do(f)
                    else:
                        pe.put(f, k_gelu[i], k_hte.get(i - 1))
                k_hte[i] = dve.do(lambda e, i=i: e.tensor_copy(hT[i % NHT][:, :], ps(HTB, 0, F)), k_tr[i], k_dn.get(i - NHT), free)

            def down(i):
                pe.wait(k_hte[i], k_ye.get(i - 1), k_wd)
                o = 256 * (i % 2)
                for c in range(nf):
                    def f(e, i=i, c=c, o=o):
                        return e.matmul(ps(YB, o, o + 256), hT[i % NHT][:, 128 * c:128 * c + 128],
                                        WD[:, bass.ds(val[i] * (nf * 256) + c * 256, 256)], start=(c == 0), stop=(c == nf - 1 and biases is None))
                    if biases is None and c == nf - 1:
                        k_dn[i] = pe.do(f)
                    else:
                        pe.put(f)
                if biases is not None:
                    k_dn[i] = pe.do(lambda e, i=i, o=o: e.matmul(ps(YB, o, o + 256), biases[2][:, bass.ds(val[i] * 128, 128)],
                                                                biases[1][:, :], start=False, stop=True))
                k_ye[i] = act.do(lambda e, i=i, o=o: e.activation(y[i % 2][:, :], ps(YB, o, o + 256), ACT.Copy), k_dn[i], k_ys.get(i - 2), free)
                k_ys[i] = sp.dma(lambda e, i=i: e.dma_start(Ys[128 * i:128 * i + 128, :], y[i % 2][:, :]), cy[i % 2], k_ye[i], free)

            load_in(0), load_in(1), load_in(2)
            xtr(0), xtr(1)
            up(0)
            for i in range(NTILE):
                load_in(i + 3)
                htr(i)
                up(i + 1)
                xtr(i + 2)
                down(i)
            return [(c.sem, c.n) for c in cy], [k_dn[NTILE - 1], k_ye[NTILE - 1], k_hte[NTILE - 1], k_gelu[NTILE - 1]]

        def combine(layer, k_y, k_w, k_acc, free, done):
            G = [view(carve(256), 256) for _ in range(6)]
            cg = [count(f"c_g{layer}{n}") for n in range(6)]
            used = [None] * 6
            m = 0
            for i in range(NT):
                for n in range(2):
                    r = m % 6
                    m += 1
                    k = pool.dma(lambda e, i=i, n=n, r=r: e.indirect_dma_start(
                        G[r][:, :], None, Ys, bass.IndirectOffsetOnAxis(ap=POS[:, n, i:i + 1], axis=0)), cg[r], k_y, used[r], free)
                    used[r] = dve.do(lambda e, i=i, n=n, r=r: e.scalar_tensor_tensor(
                        ACC[:, i, :], G[r][:, :], W12[:, n, i:i + 1], ACC[:, i, :], ALU.mult, ALU.add), k, k_w, k_acc[i // 4], used[(m - 2) % 6])
                if i % 4 == 3:
                    done[i // 4] = used[(m - 1) % 6]
                    yield

        WRV = view(carve(16), 16).rearrange("p (c n) -> p c n", c=2)
        c_wr, c_w = count("c_wr"), count("c_w")
        k_wr = sp.dma(lambda e: e.dma_start(WRV[:, :, :], t["Wg"]), c_wr)
        ATT = top[0]
        WQ = view(carve(512), 512).rearrange("p (c n) -> p c n", c=2)
        WK = view(carve(512), 512).rearrange("p (c n) -> p c n", c=2)
        WV = view(carve(512), 512).rearrange("p (c n) -> p c n", c=2)
        WO = view(carve(1024), 1024).rearrange("p (g n) -> p g n", g=4)
        for dst, name in ((WQ, "Wq"), (WK, "Wk"), (WV, "Wv"), (WO, "Wo")):
            k_w = sp.dma(lambda e, d=dst, n=name: e.dma_start(d[:, :, :], t[n]), c_w)
        Vb = [view(carve(2048), 2048).rearrange("p (i h d) -> p i h d", i=4, h=16) for _ in range(2)]
        STK2 = top[0] + 4 * 2048
        STK = [[view(carve(2048), 2048, BF16).rearrange("p (j s) -> p j s", j=8) for _ in range(2)] for _ in range(3)]
        OT = [view(carve(512), 512) for _ in range(4)]
        RC = view(carve(512), 512)
        R16 = view(carve(16), 16)
        PT = [view(carve(768), 768, BF16).rearrange("p (k s) -> p k s", k=3) for _ in range(2)]
        R1 = [view(carve(512), 512) for _ in range(2)]
        NM = [view(carve(32), 32).rearrange("p (i j) -> p i j", i=4) for _ in range(2)]
        NM2 = view(carve(32), 32).rearrange("p (i j) -> p i j", i=4)
        NP = [view(carve(48), 48, BF16).rearrange("p (i k j) -> p i k j", i=4, k=3) for _ in range(2)]
        MT = [view(carve(256), 256, BF16) for _ in range(2)]
        NPB = 5
        PB = [view(carve(1280), 1280) for n in range(NPB)]
        ZERO = view(carve(128), 128)
        lgall = view(carve(256), 256)
        route0 = top[0]
        assert route0 + 2100 <= LIMIT, route0
        ln0 = norm_and_route(0, k_x, STK2, None, WRV, k_wr, 8, lgall, [None] * NB)
        k_T, k_lg, lgall, k_store, k_last = next(ln0)
        for _ in ln0:
            pass
        c_z = count("c_z")
        kz = pool.do(lambda e: e.memset(ZERO[:, :], 0.0))
        for h in range(2):
            k_zero = sp.dma(lambda e, h=h: e.dma_start(Xs.rearrange("(i p) (h d) -> h p i d", p=128, h=2)[h], ZERO.unsqueeze(1).to_broadcast([128, NTILE, 128])), c_z, kz)
        R0 = {}
        top[0] = route0
        k_mb = [[k_last["pe"], k_lg[-1]], 7]

        def routing0():
            top[0] = route0
            yield from top2(lgall, k_lg[-1], 0, k_mb, R0)
            assert top[0] <= LIMIT
            top[0] = route0
            yield from scatter(0, k_store[-2:], R0["pos"], k_zero, R0)

        free = []
        k_vinit = [pool.do(lambda e, v=v: e.memset(v, 0.0), *free) for v in Vb]
        k_vinit = [pool.do(lambda e, v=v: e.memset(v[:, :, :, 16:17], 1.0), *k_vinit) for v in Vb][-1]
        k_init = k_vinit
        for n in range(3):
            w = [k_last["pe"], k_last["norm"], *k_store[-2:]] if n == 2 else None
            for m in range(2):
                k_init = pool.do(lambda e, s=STK[n][m]: e.memset(s[96:128, :, :], 0.0), k_init, w)
        for n in range(3):
            k_init = pool.do(lambda e, s=STK[n][1]: e.memset(s[96:99, :, :], 1.0), k_init)
        c_st = [[count(f"c_st{n}{m}") for m in range(2)] for n in range(3)]
        c_sp = [[count(f"c_sp{n}{m}") for m in range(2)] for n in range(3)]
        c_m = [count(f"c_m{n}") for n in range(3)]
        SLOTS = [[0, 0, 1, 1, 0, 2], [0, 1, 0, 1, 2, 0]]
        off = {3: 0, 2: 512, 0: 896, 1: 1024}
        offT = {0: 0, 1: 512, 3: 896, 2: 1024}
        SB0, TB0, OB, MB = 0, 3, 6, 7
        k_stack, k_mrow, k_s, k_red, k_st_, k_exp, k_pv, k_pt, k_v = ({} for _ in range(9))
        k_pt_free = [None, None]
        k_stk_dma = {}
        NHB = 2 * NB

        def project(n):
            b, half = divmod(n, 2)
            todo = []
            for m, W in enumerate((WQ, WK)):
                for c in range(2):
                    f = lambda e, m=m, W=W, c=c: e.matmul(ps(MB, 0, 512), W[:, c, 128 * half:128 * half + 128], xnT[:, c, 512 * b:512 * b + 512], start=(c == 0), stop=(c == 1))
                    if c:
                        k = pe.do(f)
                    else:
                        pe.put(f, k_T[b], k_w, k_mb[0], *free)
                pt, r1 = PT[m], R1[m]
                k1 = act.do(lambda e, pt=pt: e.activation(pt[:, 0, :], ps(MB, 0, 512), ACT.Copy), k, k_pt_free[m], *free)
                k2 = dve.do(lambda e, pt=pt, r1=r1: e.tensor_tensor(r1[:, :], ps(MB, 0, 512), pt[:, 0, :], ALU.subtract), k1, k_pt_free[m])
                k_mb[0] = k2
                k3 = pool.do(lambda e, pt=pt, r1=r1: e.tensor_copy(pt[:, 1, :], r1[:, :]), k2, k_init)
                k4 = pool.do(lambda e, pt=pt, r1=r1: e.tensor_tensor(pt[:, 2, :], r1[:, :], pt[:, 1, :], ALU.subtract), k3)
                dst = STK[n % 3][m]
                box = SPL[n % 3, m]
                k_pt_free[m] = sp.dma(lambda e, box=box, pt=pt: e.dma_start(box, pt), c_sp[n % 3][m], k4, k_stack.get((n - 3, m)))
                todo.append((m, dst, box))
                if m == 0:
                    yield
            for m, dst, box in todo:
                for sl, part in enumerate(SLOTS[m]):
                    kk = sp.dma(lambda e, dst=dst, box=box, sl=sl, part=part: e.dma_start(
                        dst[16 * sl:16 * sl + 16, :, :], box[:, part, :].rearrange("(j d) s -> d j s", j=8)),
                        c_st[n % 3][m], k_pt_free[m], k_st_.get((n - 3, 7)), k_s.get((n - 3, 7)))
                k_stack[n, m] = kk

        def project_v(b):
            vb = Vb[b % 2]
            for i in range(4):
                for c in range(2):
                    f = lambda e, i=i, c=c: e.matmul(ps(MB, 0, 256), xnT[:, c, 512 * b + 128 * i:512 * b + 128 * i + 128], WV[:, c, :], start=(c == 0), stop=(c == 1))
                    if c:
                        k = pe.do(f)
                    else:
                        pe.put(f, k_T[b], k_w, k_mb[0], *free)
                k_mb[0] = k_v[b] = act.do(lambda e, i=i, vb=vb: e.activation(vb[:, i, :, 0:16], ps(MB, 0, 256).rearrange("p (h d) -> p h d", h=16), ACT.Copy), k, k_vinit, k_pv.get((2 * b - 3, 1)))
                yield

        def scores(n, j):
            q, k = STK[n % 3]
            for i in (3, 2, 0, 1):
                w = 128 * (i + 1)
                pe.put(lambda e, i=i, w=w: e.matmul(ps(SB0, off[i], off[i] + w), q[0:96, j, 128 * i:128 * i + 128], k[0:96, j, 0:w], start=True, stop=False),
                       k_stack[n, 0], k_stack[n, 1], k_sbank[off[i] // 512], k_init)
                kk = pe.do(lambda e, i=i, w=w: e.matmul(ps(SB0, off[i] + w - 128, off[i] + w), identb, M1b, start=False, stop=True))
                for r in {3: (3,), 2: (), 0: (2, 0), 1: (1,)}[i]:
                    k_sbank[off[r] // 512] = k_red[n, j] = dve.do(lambda e, r=r: e.tensor_reduce(NM[n % 2][:, r, j:j + 1], ps(SB0, off[r], off[r] + 128 * (r + 1)), AX.X, ALU.max, negate=True), kk, k_pt.get(n - 2), *free)
            k_s[n, j] = kk

        def maxima(n):
            yield
            nm, np_, mt = NM[n % 2], NP[n % 2], MT[n % 2]
            k1 = dve.do(lambda e: e.tensor_copy(np_[:, :, 0, :], nm), k_red[n, 7], k_pt.get(n - 2))
            k1 = dve.do(lambda e: e.tensor_tensor(NM2, nm, np_[:, :, 0, :], ALU.subtract), k1)
            k1 = dve.do(lambda e: e.tensor_copy(np_[:, :, 1, :], NM2), k1)
            k1 = dve.do(lambda e: e.tensor_tensor(np_[:, :, 2, :], NM2, np_[:, :, 1, :], ALU.subtract), k1)
            yield
            pmt = ps(MB, 0, 256).bitcast(BF16)
            for i in range(4):
                f = lambda e, i=i: e.transpose(pmt[0:24, 128 * i:128 * i + 128], np_[:, i, :, :].rearrange("p k j -> p (k j)"), identb)
                if i == 3:
                    k_pt[n] = pe.do(f)
                else:
                    pe.put(f, k1, k_mb[0])
            k2 = act.do(lambda e: e.activation(mt[0:24, :], pmt[0:24, :], ACT.Copy), k_pt[n], k_mrow.get(n - 2), *free)
            k_mb[0] = k2
            for k in range(3):
                k_mrow[n] = sp.dma(lambda e, k=k: e.dma_start(STK[n % 3][0][96 + k:97 + k, :, :], mt[8 * k:8 * k + 8, :]), c_m[n % 3], k2, k_s[n, 7], k_st_.get((n - 3, 7)), k_init)

        def scoresT(n, j):
            q, k = STK[n % 3]
            idx = 8 * n + j
            o = idx - NPB
            for kb in (0, 1, 3, 2):
                w = 512 - 128 * kb
                pe.put(lambda e, kb=kb, w=w: e.matmul(ps(TB0, offT[kb], offT[kb] + w), k[:, j, 128 * kb:128 * kb + 128], q[:, j, 128 * kb:512], start=True, stop=False),
                       k_mrow[n], k_tbank[offT[kb] // 512])
                kk = pe.do(lambda e, kb=kb: e.matmul(ps(TB0, offT[kb], offT[kb] + 128), identb, M2b, start=False, stop=True))
                if kb in (0, 2):
                    lo, hi = (0, 512) if kb == 0 else (512, 1280)
                    k_exp[n, j] = act.do(lambda e, lo=lo, hi=hi: e.activation(PB[idx % NPB][:, lo:hi], ps(TB0, lo, hi), ACT.Exp, scale=0.25), kk, k_pv.get((o // 8, (o % 8) // 4)) if o >= 0 else None)
                    for bank in range(lo // 512, (hi + 511) // 512):
                        k_tbank[bank] = k_exp[n, j]
            k_st_[n, j] = kk

        def values(n, g):
            b, half = divmod(n, 2)
            vb = Vb[b % 2]
            for kb in range(4):
                w = 512 - 128 * kb
                for j in range(4):
                    jj = 4 * g + j
                    p = PB[(8 * n + jj) % NPB]
                    f = lambda e, kb=kb, j=j, jj=jj, p=p, w=w: e.matmul(
                        PS[32 * j:32 * j + 32, OB, 128 * kb:512], vb[:, kb, 8 * half + jj, :], p[:, offT[kb]:offT[kb] + w], start=(kb == 0), stop=(kb == 3))
                    if kb == 3 and j == 3:
                        k_pv[n, g] = pe.do(f)
                    else:
                        pe.put(f, k_exp[n, jj], k_v[b], *k_ob)
            assert b == 0 or b - 1 in k_wo
            G = 2 * half + g
            ot = OT[G]
            k1 = act.do(lambda e: e.activation(ot[:, :], ps(OB, 0, 512), ACT.Copy), k_pv[n, g], k_wo.get(b - 1), *free)
            k_ob[:] = [k1]
            yield
            for i in range(4):
                f = lambda e, i=i: e.transpose(ps(MB, 128 * i, 128 * i + 128), ot[:, 128 * i:128 * i + 128], ident)
                if i == 3:
                    k2 = pe.do(f)
                else:
                    pe.put(f, k1, k_mb[0])
            tm = ps(MB, 0, 512).rearrange("p (h r) -> p h r", r=32)
            k3 = dve.do(lambda e: e.reciprocal(R16, tm[:, :, 16]), k2, k_nrm[0])
            k_mb[0] = k3 = dve.do(lambda e: e.tensor_tensor(RC[:, :].rearrange("p (h r) -> p h r", r=32), tm, R16.unsqueeze(2).to_broadcast([128, 16, 32]), ALU.mult), k3)
            yield
            for i in range(4):
                f = lambda e, i=i: e.transpose(ps(MB, 128 * i, 128 * i + 128), RC[:, 128 * i:128 * i + 128], ident)
                if i == 3:
                    k4 = pe.do(f)
                else:
                    pe.put(f, k3, k_mb[0])
            k_mb[0] = k_nrm[0] = act.do(lambda e: e.activation(ot[:, :], ps(MB, 0, 512), ACT.Copy), k4, k2)

        def output(b):
            for i in range(4):
                for g in range(4):
                    f = lambda e, i=i, g=g: e.matmul(ps(MB, 0, 256), OT[g][:, 128 * i:128 * i + 128], WO[:, g, :], start=(g == 0), stop=(g == 3))
                    if g == 3:
                        k = pe.do(f)
                    else:
                        pe.put(f, k_nrm[0], k_mb[0])
                if i == 3:
                    k_wo[b] = k
                k_acc0[b] = k_mb[0] = dve.do(lambda e, i=i: e.tensor_tensor(ACC[:, 4 * b + i, :], ps(MB, 0, 256), ACC[:, 4 * b + i, :], ALU.add), k)
                yield

        k_sbank, k_tbank = [None] * 3, [None] * 3
        k_ob, k_nrm, k_wo, k_acc0 = [k_last["pe"], k_lg[-1]], [None], {}, {}
        steps = []

        def later(order, gen):
            steps.append((order, len(done_steps), gen))
            done_steps.append(None)
            steps.sort(key=lambda x: x[:2])

        done_steps = []

        def step():
            while steps:
                try:
                    next(steps[0][2])
                    return
                except StopIteration:
                    steps.pop(0)

        for n in range(2):
            for _ in project(n):
                pass
        for _ in project_v(0):
            pass
        rt = routing0()
        LEAD, NH = 11, 8 * NHB
        for idx in range(-LEAD, NH + 1):
            if idx % 8 == 0 and 2 <= idx // 8 + 2 < NHB:
                later(0, project(idx // 8 + 2))
                if idx % 16 == 0:
                    later(3, project_v(idx // 16 + 1))
            lead = idx + LEAD
            if lead < NH:
                scores(lead // 8, lead % 8)
                if lead % 8 == 7:
                    later(0, maxima(lead // 8))
                step()
            if 0 <= idx < NH:
                scoresT(idx // 8, idx % 8)
            if idx >= 4 and idx % 4 == 0:
                gq = idx // 4 - 1
                vals = values(gq // 2, gq % 2)
                next(vals)
                later(1, vals)
                if gq % 4 == 3:
                    later(2, output(gq // 4))
            step()
            if idx >= 0:
                next(rt, None)
        while steps:
            step()
        for _ in rt:
            pass

        top[0] = base
        free = [k_wo[NB - 1], k_nrm[0], k_acc0[NB - 1], *R0["scat"]]
        WU = view(carve(8192), 8192)
        WD = view(carve(8192), 8192)
        top[0] = LIMIT - 11520
        W1 = view(carve(1024), 1024).rearrange("p (c n) -> p c n", c=2)
        W2 = view(carve(1024), 1024).rearrange("p (c n) -> p c n", c=4)
        hs = [view(carve(2048), 2048).rearrange("p (c n) -> p c n", c=4) for _ in range(2)]
        c_w0, c_wu, c_wd = count("c_w0"), count("c_wu"), count("c_wd")
        k_w0 = sp.dma(lambda e: e.dma_start(W1[:, :, :], t["W1"]), c_w0, *free)
        k_w0 = sp.dma(lambda e: e.dma_start(W2[:, :, :], t["W2"]), c_w0)
        for q in range(4):
            k_wu = sp.dma(lambda e, q=q: e.dma_start(WU[:, 2048 * q:2048 * q + 2048], t["Wu"][:, 2048 * q:2048 * q + 2048]), c_wu)
        for q in range(4):
            k_wd = sp.dma(lambda e, q=q: e.dma_start(WD[:, 2048 * q:2048 * q + 2048], t["Wd"][:, 2048 * q:2048 * q + 2048]), c_wd)
        k_g, k_sd, k_dn, k_acc1 = {}, [None, None], {}, {}

        def shared_up(b):
            for fc in range(4):
                bank = fc % 2
                for c in range(2):
                    f = lambda e, fc=fc, c=c, bank=bank: e.matmul(ps(bank, 0, 512), W1[:, c, 128 * fc:128 * fc + 128], xnT[:, c, 512 * b:512 * b + 512], start=(c == 0), stop=(c == 1))
                    if c:
                        k = pe.do(f)
                    else:
                        pe.put(f, k_w0, k_g.get((b - 1, fc + 2) if fc < 2 else (b, fc - 2)), *free)
                k_g[b, fc] = act.do(lambda e, fc=fc, bank=bank: e.activation(hs[b % 2][:, fc, :], ps(bank, 0, 512), ACT.Gelu), k, k_dn.get(b - 2), *free)

        def shared_down(b):
            for i in range(4):
                bank = 2 + i % 2
                for fc in range(4):
                    f = lambda e, i=i, fc=fc, bank=bank: e.matmul(ps(bank, 0, 256), hs[b % 2][:, fc, 128 * i:128 * i + 128], W2[:, fc, :], start=(fc == 0), stop=(fc == 3))
                    if fc == 3:
                        k_dn[b] = pe.do(f)
                    else:
                        pe.put(f, k_g[b, 3], k_sd[i % 2], *free)
                k_sd[i % 2] = k_acc1[b] = dve.do(lambda e, i=i, bank=bank: e.tensor_tensor(ACC[:, 4 * b + i, :], ps(bank, 0, 256), ACC[:, 4 * b + i, :], ALU.add), k_dn[b], k_acc0[b])

        HB = NB // 2
        shared_up(0)
        for b in range(HB):
            if b + 1 < HB:
                shared_up(b + 1)
            shared_down(b)
        k_y, k_end = moe(0, F0, WU, WD, k_wu, k_wd, R0["scat"], R0["tex"], None, [*free, k_acc1[HB - 1], k_g[HB - 1, 3]])
        free = [*free, *k_end]
        k_x1 = {}
        comb = combine(0, k_y, R0["w12"], k_acc1, free, k_x1)
        top[0] = base
        WCR = view(carve(64), 64).rearrange("p (c n) -> p c n", c=2)
        NW = view(carve(2), 2)
        QKW = view(carve(1536), 1536).rearrange("p (c n) -> p c n", c=2)
        WOUT = view(carve(512), 512).rearrange("p (c n) -> p c n", c=2)
        COS = view(carve(128), 128).rearrange("p (i d) -> p i d", i=4)
        SIN = view(carve(128), 128).rearrange("p (i d) -> p i d", i=4)
        GB = view(carve(24), 24)
        RB = view(carve(8), 8)
        BO = view(carve(256), 256)
        LREG = top[0]
        c_w1, c_br = count("c_w1"), count("c_br")
        ends = k_end
        for dst, name in ((WCR, "Wcr"), (NW, "nw"), (QKW, "Wqkv"), (WOUT, "Wout"), (COS, "cos"), (SIN, "sin"), (GB, "gb"), (RB, "rb"), (BO, "bo"), (SEL.bitcast(F32), "sel")):
            k_w1 = sp.dma(lambda e, d=dst, n=name: e.dma_start(d, t[n]), c_w1, *ends)
        k_nw = k_w1
        for c in range(2):
            k_nw = pool.do(lambda e, c=c: e.tensor_scalar(QKW[:, c, :], QKW[:, c, :], NW[:, c:c + 1], None, ALU.mult), k_w1)
            k_nw = pool.do(lambda e, c=c: e.tensor_scalar(WCR[:, c, 8:32], WCR[:, c, 8:32], NW[:, c:c + 1], None, ALU.mult), k_w1)
        k_b3 = pool.do(lambda e: e.memset(B1S, 0.0), *ends)
        k_b3 = pool.do(lambda e: e.memset(B2S, 0.0), *ends)
        c_bl = count("c_bl")
        bf = view(LREG, 1280)
        b3 = view(LREG + 1280, 3 * 640, BF16).rearrange("p (k n) -> p k n", k=3)
        kb = sp.dma(lambda e: e.dma_start(bf[0:8, 0:1024], t["b1"]), c_bl, *ends)
        kb = sp.dma(lambda e: e.dma_start(bf[0:8, 1024:1280], t["b2"]), c_bl)
        for k in range(3):
            kb = pool.do(lambda e, k=k: e.tensor_copy(b3[0:8, k, :], bf[0:8, :]), kb)
            if k < 2:
                kb = pool.do(lambda e, k=k: e.tensor_tensor(bf[0:8, :], bf[0:8, :], b3[0:8, k, :], ALU.subtract), kb)
        for k in range(3):
            k_br = sp.dma(lambda e, k=k: e.dma_start(B1S[8 * k:8 * k + 8, :], b3[0:8, k, 0:1024]), c_br, kb, k_b3)
            k_br = sp.dma(lambda e, k=k: e.dma_start(B2S[8 * k:8 * k + 8, :], b3[0:8, k, 1024:1280]), c_br, kb, k_b3)

        top[0] = LREG + 9800
        g_r, g_o, LF, EF, EU = (view(carve(256), 256).rearrange("p (i h) -> p i h", i=NT) for _ in range(5))
        ET = view(carve(64), 64).rearrange("p (g i) -> p g i", g=2)
        MST = view(carve(2048), 2048).rearrange("p (b g n) -> p b g n", b=NB, g=2)
        BD = view(carve(128), 128)
        MTMP = view(carve(128), 128)
        low_end = top[0]
        lgall = view(carve(NT * 32), NT * 32)
        GZ = view(carve(NT * 24), NT * 24).rearrange("p (i n) -> p i n", i=NT)
        LRT = view(carve(256), 256).rearrange("p (i e) -> p i e", i=NT)
        eta = carve(512)
        ETA = view(eta, 512).rearrange("p (g i h) -> p g i h", g=2, i=NT)
        route1 = top[0]
        route1_end = route1 + 2100
        k_xfree = {b: k_g[b, 3] for b in range(HB)}
        ln1 = norm_and_route(1, k_x1, LREG, [*k_end, k_br], WCR, [k_nw], 32, lgall, k_xfree)
        k_T, k_lg, lgall, k_store, k_last = next(ln1)
        shared_up(HB)
        nl = 0
        for b in range(HB, NB):
            if b + 1 < NB:
                shared_up(b + 1)
            shared_down(b)
            k_xfree[b] = k_g[b, 3]
            if b < NB - 1:
                for _ in range(1 if b > HB else 2):
                    next(comb), next(ln1)
        for _ in comb:
            pass
        for _ in ln1:
            pass
        fre = [*k_end, k_x1[NB - 1], k_last["pe"], k_last["norm"], k_last["sq"], *k_store[-2:], k_dn[NB - 1], k_acc1[NB - 1]]
        k = dve.do(lambda e: e.tensor_tensor(LRT, lgall[:, :, 0:8], RB.unsqueeze(1).to_broadcast([128, NT, 8]), ALU.add), k_lg[-1], k_w1, *fre)
        k_lrt = k
        kr = act.do(lambda e: e.activation(RT[:, :], SS[:, :], ACT.Sqrt, bias=EPS6[:, :], scale=1.0 / D), k_last["sq"])
        kr = dve.do(lambda e: e.reciprocal(RT[:, :], RT[:, :]), kr)
        kz = dve.do(lambda e: e.tensor_tensor(GZ, lgall[:, :, 8:32], RT.unsqueeze(2).to_broadcast([128, NT, 24]), ALU.mult), kr)
        kz = dve.do(lambda e: e.tensor_tensor(GZ, GZ, GB.unsqueeze(1).to_broadcast([128, NT, 24]), ALU.add), kz)
        kz = act.do(lambda e: e.activation(GZ, GZ, ACT.Exp, scale=-1.0), kz)
        kz = dve.do(lambda e: e.tensor_scalar(GZ, GZ, 2.0 ** 62, 1.0, ALU.min, ALU.add), kz)
        kl = act.do(lambda e: e.activation(LF, GZ[:, :, 0:8], ACT.Ln), kz, *fre)
        kg = dve.do(lambda e: e.reciprocal(GZ[:, :, 8:24], GZ[:, :, 8:24]), kz)
        kg = dve.do(lambda e: e.tensor_tensor(GZ[:, :, 8:24], GZ[:, :, 8:24], RT.unsqueeze(2).to_broadcast([128, NT, 16]), ALU.mult), kg)
        kg1 = dve.do(lambda e: e.tensor_scalar(g_r, GZ[:, :, 8:16], float(1.0 / np.sqrt(32.0)), None, ALU.mult), kg)
        k_gates = dve.do(lambda e: e.tensor_copy(g_o, GZ[:, :, 16:24]), kg)
        LFf = LF.rearrange("p i h -> p (i h)")
        kd = None
        for n, (mat, dst) in enumerate(((Uinc, EF), (Lstr, EU), (ones, None))):
            kd = pe.do(lambda e, mat=mat: e.matmul(ps(0, 0, 256), mat[:, :], LFf, start=True, stop=True), kl, kd, k_T[NB - 1])
            if dst is not None:
                kd = act.do(lambda e, dst=dst: e.activation(dst, ps(0, 0, 256).rearrange("p (i h) -> p i h", i=NT), ACT.Exp, scale=-1.0), kd, *fre)
            else:
                for g in range(2):
                    kd = act.do(lambda e, g=g: e.activation(ETA[:, g, :, :], ps(0, 0, 256).rearrange("p (i h) -> p i h", i=NT), ACT.Exp, scale=-1.0), kd)
        for g in range(2):
            kd = dve.do(lambda e, g=g: e.tensor_tensor(ETA[:, g, :, :], ETA[:, g, :, :], hsel[:, 8 * g:8 * g + 8].unsqueeze(1).to_broadcast([128, NT, 8]), ALU.mult), kd)
        k_dec = dve.do(lambda e: e.tensor_reduce(ET, ETA, AX.X, ALU.add), kd)
        RR1 = {}
        bank5 = [None, 5]

        def routing1():
            top[0] = route1
            yield from top2(LRT, k_lrt, 1, bank5, RR1)
            assert top[0] <= route1_end
            top[0] = route1
            yield from scatter(1, k_store[-2:], RR1["pos"], None, RR1)

        rt = routing1()

        top[0] = LREG
        lf = [k_gates, k_dec, kg1]
        T1, T2 = (view(carve(512), 512).rearrange("p (h d) -> p h d", h=16) for _ in range(2))
        QO2, QE2, KR2, KD2, VP2 = ([view(carve(256), 256) for _ in range(2)] for _ in range(5))
        LU = view(carve(1024), 1024).rearrange("p (h n) -> p h n", h=8)
        DD2 = [view(carve(1024), 1024).rearrange("p (g n) -> p g n", g=2) for _ in range(2)]
        QB = [view(carve(512), 512).rearrange("p (j n) -> p j n", j=4) for _ in range(2)]
        QET = view(carve(256), 256)
        KT = view(carve(256), 256)
        WT = [view(carve(512), 512) for _ in range(2)]
        YT = view(carve(256), 256)
        XB = view(carve(256), 256)
        assert top[0] <= LREG + 9800
        h8 = lambda ap: ap.rearrange("p (h d) -> p h d", h=8)
        kq0 = pool.do(lambda e: e.memset(QB[0], 0.0), *lf)
        kq0 = pool.do(lambda e: e.memset(QB[1], 0.0), *lf)
        order = [4 * b + c for c in range(4) for b in range(NB)]
        K = {}
        k_m = {}
        k_acc2 = {}

        def front(i, p, pp, par):
            c4 = i % 4
            QO, QE, KR, KD, VP, DD = (z[par] for z in (QO2, QE2, KR2, KD2, VP2, DD2))
            tok = slice(128 * i, 128 * i + 128)
            for c in range(2):
                f = lambda e, c=c: e.matmul(ps(0, 0, 512), xnT[:, c, tok], QKW[:, c, 0:512], start=(c == 0), stop=(c == 1))
                if c:
                    kqk = pe.do(f)
                else:
                    pe.put(f, k_T[-1], k_nw, K.get(("rope", p)), *lf)
            for c in range(2):
                f = lambda e, c=c: e.matmul(ps(1, 0, 256), xnT[:, c, tok], QKW[:, c, 512:768], start=(c == 0), stop=(c == 1))
                if c:
                    kv = pe.do(f)
                else:
                    pe.put(f, K.get(("vp", p)))
            a = pool.do(lambda e: e.tensor_tensor(LU, Uinc.unsqueeze(1).to_broadcast([128, 8, 128]), LF[:, i, :].unsqueeze(2).to_broadcast([128, 8, 128]), ALU.mult), K.get(("D", p)), kbd, *lf)
            for g in range(2):
                pe.put(lambda e, g=g: e.matmul(ps(2 + g, 0, 512), Lstr, LU[:, 4 * g:4 * g + 4, :].rearrange("p h n -> p (h n)"), start=True, stop=False), a, K.get(("DD", p)))
                kD = pe.do(lambda e, g=g: e.matmul(ps(2 + g, 0, 512).rearrange("p (h n) -> p h n", h=4), identb, M2p.unsqueeze(1).to_broadcast([128, 4, 128]), start=False, stop=True))
            K["D", i] = kD
            q3 = ps(0, 0, 512).rearrange("p (h d) -> p h d", h=16)
            cs, sn = COS[:, c4, :], SIN[:, c4, :]
            bc = lambda ap: ap.unsqueeze(1).to_broadcast([128, 16, ap.shape[1]])
            r1 = dve.do(lambda e: e.tensor_tensor(T1, q3, bc(cs), ALU.mult), kqk, K.get(("rot", p)), *lf)
            dve.put(lambda e: e.tensor_tensor(T2[:, :, 0:16], q3[:, :, 16:32], bc(sn[:, 0:16]), ALU.mult), K.get(("rot", p)))
            r2 = dve.do(lambda e: e.tensor_tensor(T2[:, :, 16:32], q3[:, :, 0:16], bc(sn[:, 16:32]), ALU.mult))
            K["rope", i] = r2
            rr = pool.do(lambda e: e.tensor_tensor(T1, T1, T2, ALU.add), r2)
            hb = lambda ap: ap.unsqueeze(2).to_broadcast([128, 8, 32])
            a1 = pool.do(lambda e: e.tensor_tensor(h8(QO), T1[:, 0:8, :], hb(g_o[:, i, :]), ALU.mult), rr, K.get(("T", pp)))
            a2 = pool.do(lambda e: e.tensor_scalar(h8(KR), T1[:, 8:16, :], RT[:, i:i + 1], None, ALU.mult), K.get(("T", pp)))
            K["rot", i] = a2
            a3 = pool.do(lambda e: e.tensor_tensor(h8(QE), h8(QO), hb(EF[:, i, :]), ALU.mult), a1, K.get(("T", pp)))
            a4 = pool.do(lambda e: e.tensor_tensor(h8(KD), h8(KR), hb(EU[:, i, :]), ALU.mult), a2, K.get(("dM", pp)))
            K["pre", i] = a4
            K["vp", i] = dve.do(lambda e: e.tensor_tensor(h8(VP), h8(ps(1, 0, 256)), hb(g_r[:, i, :]), ALU.mult), kv, K.get(("dM", pp)))
            K["DD", i] = act.do(lambda e: e.activation(DD, PS[:, 2:4, :], ACT.Exp, scale=-1.0), kD, K.get(("W", pp)), *lf)

        def back(i, p, par):
            b, c4 = divmod(i, 4)
            QO, QE, KR, KD, VP, DD = (z[par] for z in (QO2, QE2, KR2, KD2, VP2, DD2))
            for g in range(2):
                for n, src in enumerate((QO, KR, QE)):
                    if n == 2 and c4 == 0:
                        continue
                    f = lambda e, g=g, n=n, src=src: e.transpose(ps(4 + g, 128 * n, 128 * n + 128), src[:, 128 * g:128 * g + 128], ident)
                    kt = pe.do(f, K["pre", i], K.get(("ev", p)), K.get(("acc", p)), K.get(("dMe", p)), bank5[0])
            K["T", i] = kt
            ev = []
            for g in range(2):
                def copy(dst, src, *ticks, g=g):
                    if g == 0:
                        return act.do(lambda e: e.activation(dst, src, ACT.Copy), *ticks)
                    return dve.do(lambda e: e.tensor_copy(dst, src), *ticks)
                for j in range(4):
                    ev.append(copy(QB[g][32 * j:32 * j + 32, j, :], PS[32 * j:32 * j + 32, 4 + g, 0:128], kt, K.get(("A", p)), kq0))
                ev.append(copy(KT[:, 128 * g:128 * g + 128], ps(4 + g, 128, 256), kt, K.get(("A", p))))
                if c4:
                    ev.append(copy(QET[:, 128 * g:128 * g + 128], ps(4 + g, 256, 384), kt, K.get(("Y", p))))
            K["ev", i] = [ev[-1], *ev]
            for g in range(2):
                kA = pe.do(lambda e, g=g: e.matmul(ps(6, 0, 512), KT[:, 128 * g:128 * g + 128], QB[g].rearrange("p j n -> p (j n)"), start=True, stop=True), *ev, K.get(("W", p)) if g == 0 else K.get(("W", i)))
                K["W", i] = dve.do(lambda e, g=g: e.tensor_tensor(WT[g][:, :], ps(6, 0, 512), DD[:, g, :], ALU.mult), kA, K["DD", i], K.get(("Y", p)))
            K["A", i] = kA
            for g in range(2):
                if c4:
                    pe.put(lambda e, g=g: e.matmul(ps(7, 128 * g, 128 * g + 128), MST[:, b, g, :], QET[:, 128 * g:128 * g + 128], start=True, stop=False, skip_group_check=True), k_m[b], K.get(("ye", p)))
                for j in range(4):
                    h = 4 * g + j
                    kY = pe.do(lambda e, g=g, j=j, h=h: e.matmul(PS[32 * j:32 * j + 32, 7, 128 * g:128 * g + 128], VP[:, 32 * h:32 * h + 32], WT[g][:, 128 * j:128 * j + 128],
                                                                start=(c4 == 0), stop=True, skip_group_check=True), K["W", i], K["vp", i], K.get(("ye", p)))
            K["Y", i] = kY
            for g in range(2):
                kM = pe.do(lambda e, g=g: e.matmul(ps(5, 128 * g, 128 * g + 128), KD[:, 128 * g:128 * g + 128], VP[:, 128 * g:128 * g + 128], start=True, stop=True, skip_group_check=True))
            K["dM", i] = kM
            K["ye", i] = act.do(lambda e: e.activation(YT[:, :], ps(7, 0, 256), ACT.Copy), kY, K.get(("O", p)))
            for g in range(2):
                if c4 == 0:
                    km = dve.do(lambda e, g=g: e.tensor_tensor(MST[:, b, g, :], ps(5, 128 * g, 128 * g + 128), BD, ALU.mult), kM, kbd)
                else:
                    k1 = dve.do(lambda e, g=g: e.tensor_tensor(MTMP[:, :], ps(5, 128 * g, 128 * g + 128), BD, ALU.mult), kM, kbd, k_m[b] if g == 0 else km)
                    km = dve.do(lambda e, g=g: e.scalar_tensor_tensor(MST[:, b, g, :], MST[:, b, g, :], ET[:, g, i:i + 1], MTMP[:, :], ALU.mult, ALU.add), k1, kY)
            k_m[b] = km
            K["dMe", i] = km
            for g in range(2):
                kO = pe.do(lambda e, g=g: e.matmul(ps(4, 0, 256), YT[:, 128 * g:128 * g + 128], WOUT[:, g, :], start=(g == 0), stop=(g == 1)), K["ye", i], K["ev", i])
            K["O", i] = kO
            kx = pool.do(lambda e: e.tensor_tensor(XB[:, :], ACC[:, i, :], BO[:, :], ALU.add), K.get(("acc", p)), k_w1)
            K["acc", i] = k_acc2[i] = dve.do(lambda e: e.tensor_tensor(ACC[:, i, :], ps(4, 0, 256), XB[:, :], ALU.add), kO, kx)

        kbd = pool.do(lambda e: e.memset(BD[:, :], 0.0), kq0, *fre)
        for j in range(4):
            kbd = pool.do(lambda e, j=j: e.memset(BD[32 * j:32 * j + 32, 32 * j:32 * j + 32], 1.0), kbd)
        WD1 = view(base, 16384)
        wu1 = LIMIT - 16384
        assert low_end <= wu1 and base + 16384 <= wu1
        WU1 = view(wu1, 16384)
        c_u1, c_d1 = count("c_u1"), count("c_d1")

        def load_wu(q, *ticks):
            return sp.dma(lambda e: e.dma_start(WU1[:, 2048 * q:2048 * q + 2048], t["w1"][:, 2048 * q:2048 * q + 2048]), c_u1, *ticks)

        early = [q for q in range(8) if wu1 + 2048 * q >= route1_end]
        for q in early:
            load_wu(q, *fre)
        front(order[0], None, None, 0)
        for n, i in enumerate(order):
            before = order[n - 1] if n else None
            if n + 1 < len(order):
                front(order[n + 1], i, before, (n + 1) % 2)
            back(i, before, n % 2)
            bank5[0] = K["dMe", i]
            next(rt, None)
            if n > 8:
                next(rt, None)
        last = order[-1]
        fre1 = [K["O", last], K["acc", last], K["dMe", last], K["W", last]]
        for _ in rt:
            pass
        for q in range(8):
            if q not in early:
                k_u1 = load_wu(q, *RR1["scat"], *fre1)
        for q in range(8):
            k_d1 = sp.dma(lambda e, q=q: e.dma_start(WD1[:, 2048 * q:2048 * q + 2048], t["w2"][:, 2048 * q:2048 * q + 2048]), c_d1, *fre1)
        top[0] = NT * D
        k_y, k_end = moe(1, F1, WU1, WD1, k_u1, k_d1, RR1["scat"], RR1["tex"], (B1S, B2S, SEL), [*fre1, k_br])
        k_o = {}
        for _ in combine(1, k_y, RR1["w12"], [K["acc", last]] * NB, [*fre1, *k_end], k_o):
            pass
        c_o = count("c_o")
        ov = out.rearrange("(b i p) d -> b p i d", b=NB, p=128)
        for b in range(NB):
            sp.dma(lambda e, b=b: e.dma_start(ov[b], ACC[:, 4 * b:4 * b + 4, :]), c_o, k_o[b])
        sp.wait((c_o.sem, c_o.n))

        block = ctx.enter_context(nc.Block())
        block.sync(sp.play)
        block.gpsimd(pool.play)
        block.scalar(act.play)
        block.tensor(pe.play)
        block.vector(dve.play)


def kernel(**inputs):
    import concourse.bacc as bacc
    from concourse.bass_utils import run_bass_kernel_spmd as run

    a = {k: np.ascontiguousarray(v) for k, v in inputs.items()}
    f32 = np.float32

    def rows(w):
        c = w.shape[0] // 128
        return np.ascontiguousarray(w.reshape(c, 128, -1).transpose(1, 0, 2))

    def experts(w):
        e, k, n = w.shape
        return np.ascontiguousarray(w.reshape(e, k // 128, 128, n).transpose(2, 0, 1, 3).reshape(128, -1))

    def over(v):
        return np.ascontiguousarray(np.broadcast_to(v, (128, v.shape[-1])))

    r = np.arange(128)
    ident = np.eye(128, dtype=f32)
    uinc = (r[:, None] <= r[None, :]).astype(f32)
    ustr = (r[:, None] < r[None, :]).astype(f32)
    lstr = (r[:, None] > r[None, :]).astype(f32)
    sel = (r[:, None] == 32 * (r[None, :] // 32) + 16).astype(f32)
    hsel = np.concatenate([(4 * g + r[:, None] // 32 == np.arange(8)[None, :]).astype(f32) for g in range(2)], 1)
    one = np.zeros((128, 1), f32)
    cst = np.concatenate([ident, uinc, ustr, lstr, sel, over(np.arange(8, dtype=f32)), over(128 * np.arange(32, dtype=f32)),
                          over(np.arange(72, dtype=f32)), one, hsel], 1).astype(f32)
    bfb = mybir.dt.np(BF16)
    cbf = np.concatenate([ident, np.where(r[None, :] > r[:, None], NEG, 0.0), np.where(r[None, :] < r[:, None], NEG, 0.0),
                          np.where(r[None, :] < r[:, None], -NEG, 0.0)], 1).astype(bfb)
    cbf = np.ascontiguousarray(cbf).view(f32)
    half = 16
    selx = np.zeros((128, 8, 128), f32)
    for e in range(8):
        selx[[e, 8 + e, 16 + e], e, :] = 1.0
    selx = np.ascontiguousarray(selx.reshape(128, 1024).astype(bfb)).view(f32)
    inv = (1.0 / np.power(f32(10000.0), np.arange(half, dtype=f32) / f32(half))).astype(f32)
    fr = np.arange(S, dtype=f32)[:, None] * inv[None, :]
    cos, sin = np.cos(fr.astype(np.float64)).astype(f32), np.sin(fr.astype(np.float64)).astype(f32)
    cos = np.concatenate([cos, cos], 1).reshape(4, 128, 32).transpose(1, 0, 2)
    sin = np.concatenate([-sin, sin], 1).reshape(4, 128, 32).transpose(1, 0, 2)
    wo = np.zeros((4, 4, 32, D), f32)
    wo[:, :, 0:16, :] = a["L0_attn_Wo"].T.reshape(4, 4, 16, D)
    arrays = {
        "x": a["L0_attn_in_features"].reshape(T, D),
        "cst": cst, "cbf": cbf,
        "Wg": rows(a["L0_ffn_Wg"]),
        "Wq": rows(a["L0_attn_Wq"].T), "Wk": rows(a["L0_attn_Wk"].T), "Wv": rows(a["L0_attn_Wv"].T),
        "Wo": np.ascontiguousarray(wo.reshape(4, 128, D).transpose(1, 0, 2)),
        "W1": rows(a["L0_ffn_W1"]), "W2": rows(a["L0_ffn_W2"]),
        "Wu": experts(a["L0_ffn_Wu"]), "Wd": experts(a["L0_ffn_Wd"]),
        "Wcr": rows(np.concatenate([a["L1_ffn_router_w"], a["L1_attn_Wbeta"].T, a["L1_attn_Wig"].T, a["L1_attn_Wog"].T], 1)),
        "nw": np.ascontiguousarray(a["L1_attn_norm_w"].reshape(2, 128).T),
        "Wqkv": rows(np.concatenate([a["L1_attn_Wq"].T, a["L1_attn_Wk"].T, a["L1_attn_Wv"].T], 1)),
        "Wout": rows(a["L1_attn_Wout"].T),
        "cos": np.ascontiguousarray(cos), "sin": np.ascontiguousarray(sin),
        "gb": over(np.concatenate([a["L1_attn_bbeta"], a["L1_attn_big"], a["L1_attn_bog"]])),
        "rb": over(a["L1_ffn_router_b"]), "bo": over(a["L1_attn_bout"]),
        "b1": a["L1_ffn_b1"], "b2": a["L1_ffn_b2"],
        "sel": selx, "w1": experts(a["L1_ffn_w1"]), "w2": experts(a["L1_ffn_w2"]),
    }
    nc = bacc.Bacc("TRN2", target_bir_lowering=False, num_devices=1)
    t = {n: nc.dram_tensor("in_" + n, v.shape, mybir.dt.from_np(v.dtype), kind="ExternalInput").ap() for n, v in arrays.items()}
    out = nc.dram_tensor("out_0", (T, D), F32, kind="ExternalOutput").ap()
    build(nc, t, out)
    res = run(nc, [{"in_" + n: np.ascontiguousarray(v) for n, v in arrays.items()}], core_ids=[0])
    return res.results[0]["out_0"].reshape(NB, S, D)
```

```python
from contextlib import ExitStack

import numpy as np
import concourse.bass as bass
from concourse import mybir

F32 = mybir.dt.float32
BF16 = mybir.dt.bfloat16
I32 = mybir.dt.int32
U32 = mybir.dt.uint32
ALU = mybir.AluOpType
ACT = mybir.ActivationFunctionType
AX = mybir.AxisListType

NB, S, D = 8, 512, 256
T = NB * S
NT = T // 128
E = 8
NTILE = (2 * T + E * 127) // 128
NSLOT = NTILE * 128
ROW = D + 2
F0, F1 = 512, 1024
NEG = -1.0e30
LIMIT = 53200


class Line:

    def __init__(self, sem):
        self.sem, self.n, self.queue, self.seen = sem, 0, [], {}

    def wait(self, *ticks):
        for t in ticks:
            if t is None:
                continue
            if isinstance(t, list):
                self.wait(*t)
                continue
            sem, val = t
            if self.seen.get(id(sem), 0) < val:
                self.seen[id(sem)] = val
                self.queue.append(("wait", sem, val))

    def put(self, fn, *ticks):
        self.wait(*ticks)
        self.queue.append(("do", fn, None, 0))

    def do(self, fn, *ticks):
        self.wait(*ticks)
        self.n += 1
        self.queue.append(("do", fn, self.sem, 1))
        return (self.sem, self.n)

    def dma(self, fn, count, *ticks):
        self.wait(*ticks)
        count.n += 16
        self.queue.append(("do", fn, count.sem, 16))
        return (count.sem, count.n)

    def play(self, eng):
        for item in self.queue:
            if item[0] == "wait":
                eng.wait_ge(item[1], item[2])
            else:
                ins = item[1](eng)
                if item[2] is not None:
                    ins.then_inc(item[2], item[3])


class Count:

    def __init__(self, sem):
        self.sem, self.n = sem, 0


def build(nc, t, out):
    ctx = ExitStack()
    with ctx:
        def sem(name):
            return ctx.enter_context(nc.semaphore(name))

        def count(name):
            return Count(sem(name))

        pe, dve, act, pool, sp = (Line(sem("n_" + n)) for n in ("pe", "dve", "act", "pool", "sp"))

        top = [0]

        arena = ctx.enter_context(nc.sbuf_tensor("arena", [128, 53200], F32))

        def carve(n):
            a = top[0]
            top[0] += n
            assert top[0] <= LIMIT, top[0]
            return a

        def view(at, n, dt=F32):
            v = arena[:, at:at + n]
            return v if dt == F32 else v.bitcast(dt)

        PS = ctx.enter_context(nc.psum_tensor("PS", [128, 8, 512], F32))
        PSf = PS[:, :, :].rearrange("p b n -> p (b n)")

        def ps(bank, a, b):
            return PSf[:, bank * 512 + a:bank * 512 + b]

        Xs = [nc.dram_tensor(f"Xs{n}", (NSLOT, ROW), F32, kind="Internal").ap() for n in range(2)]
        SUM = nc.dram_tensor("SUM", (T + 128, D), F32, kind="Internal").ap()
        SPL = nc.dram_tensor("SPL", (3, 2, 128, 3, S), BF16, kind="Internal").ap()
        XN = nc.dram_tensor("XN", (T, D), F32, kind="Internal").ap()

        ACC = view(carve(NT * D), NT * D).rearrange("p (i d) -> p i d", i=NT)
        xnT = view(carve(2 * T), 2 * T).rearrange("p (c t) -> p c t", c=2)
        CST = view(carve(t["cst"].shape[1]), t["cst"].shape[1])
        ident, Uinc, Ustr, Lstr = (CST[:, 128 * k:128 * k + 128] for k in range(4))
        iota8 = CST[:, 512:520]
        iota128 = CST[:, 520:552]
        iotaT = CST[:, 552:624]
        hsel = CST[:, 624:640]
        token = CST[:, 640:672]
        NONE = CST[:, 672:672 + ROW]
        cbf = view(carve(256), 256, BF16)
        identb, M1b, M2b, M2p = (cbf[:, 128 * k:128 * k + 128] for k in range(4))
        ones = view(carve(128), 128)
        small = carve(560)
        MV = view(small, 64).rearrange("p (i k) -> p i k", k=2)
        ST6 = view(small + 64, 24).rearrange("p (i k) -> p i k", k=6)
        RS = view(small + 88, 32)
        EPS = view(small + 120, 1)
        RT = view(small + 122, 32)
        SS = view(small + 154, 32)
        MI = view(small + 186, 8, I32)
        MW = view(small + 194, 8)
        POS = view(small + 250, 64, I32).rearrange("p (k i) -> p k i", k=2)
        TEXP = view(small + 314, 72)
        TEXI = view(small + 386, 72, I32)
        TMPS = view(small + 458, 96)
        EPS6 = view(small + 121, 1)
        META = view(carve(128), 128).rearrange("p (i k n) -> p i k n", i=NT, k=2)
        B1S = view(carve(512), 512, BF16)
        B2S = view(carve(128), 128, BF16)
        SEL = view(carve(512), 512, BF16)
        base = top[0]

        c_cst, c_x = count("c_cst"), [count(f"c_x{b}") for b in range(NB)]
        k_cst = sp.dma(lambda e: e.dma_start(CST[:, :], t["cst"]), c_cst)
        k_cst = sp.dma(lambda e: e.dma_start(cbf.bitcast(F32), t["cbf"]), c_cst)
        xv = t["x"].rearrange("(b i p) d -> b p i d", b=NB, p=128)
        k_x = [sp.dma(lambda e, b=b: e.dma_start(ACC[:, 4 * b:4 * b + 4, :], xv[b]), c_x[b]) for b in range(NB)]
        k_ones = pool.do(lambda e: e.memset(ones[:, :], 1.0))
        k_eps = pool.do(lambda e: e.memset(EPS[:, :], 1.0e-5))
        k_eps = pool.do(lambda e: e.memset(EPS6[:, :], 1.0e-6))

        def norm_and_route(layer, ready, region, free, wr, kwr, nr, lgall, freeT, banks, deep):
            top[0] = region
            xnb = [view(carve(1024), 1024).rearrange("p (i d) -> p i d", i=4) for _ in range(deep)]
            lgt = [view(carve(512), 512) for _ in range(deep)]
            junk = view(carve(256), 256) if layer else None
            lgall = lgall.rearrange("p (i n) -> p i n", i=NT)
            k_last = {"at": (0, 0)}
            c_xn = [count(f"c_xn{layer}{k}") for k in range(2)]
            xnd = XN.rearrange("(b i p) d -> b p i d", b=NB, p=128)
            k_T, k_lgt, k_lgev, k_store = [None] * NB, [None] * NB, [None] * NB, [None] * NB
            k_norm, k_tr, k_lgp, k_sq, k_root = {}, {}, {}, None, {}
            yield k_T, k_lgev, lgall, k_store, k_last

            def take():
                banks.append(banks.pop(0))
                return banks[-1]

            def stats(b):
                for j in range(4):
                    k = dve.do(lambda e, i=4 * b + j, j=j: e.bn_stats(ST6[:, j, :], ACC[:, i, :]), ready[b], free, *k_st.values())
                for j in range(4):
                    k_st[b] = dve.do(lambda e, i=4 * b + j, j=j: e.bn_aggr(MV[:, i, :], ST6[:, j, :]), k)

            def root(bs):
                lo, hi = 4 * bs[0], 4 * bs[-1] + 4
                k = act.do(lambda e: e.activation(RS[:, lo:hi], MV[:, lo:hi, 1], ACT.Sqrt, bias=EPS[:, :]), k_st[bs[-1]], k_eps)
                k_root.update({b: k for b in bs})

            k_st = {}
            for b in range(NB):
                x, lt = xnb[b % deep], lgt[b % deep]
                if layer:
                    if b not in k_root:
                        stats(b)
                        root([b])
                elif b not in k_root:
                    bs = [0, 1] if b == 0 else list(range(b, NB))
                    for n in bs:
                        stats(n)
                        if b:
                            yield
                    root(bs)
                k3 = dve.do(lambda e, b=b: e.reciprocal(RS[:, 4 * b:4 * b + 4], RS[:, 4 * b:4 * b + 4]), k_root[b])
                for j in range(4):
                    i = 4 * b + j
                    k_norm[b] = dve.do(lambda e, i=i, j=j, x=x: e.tensor_scalar(
                        x[:, j, :], ACC[:, i, :], MV[:, i, 0:1], RS[:, i:i + 1], ALU.subtract, ALU.mult),
                        k3, free, k_store[b - deep] if b >= deep else None, k_tr.get(b - deep), k_sq)
                k_store[b] = sp.dma(lambda e, b=b, x=x: e.dma_start(xnd[b], x[:, :, :]), c_xn[b % 2], k_norm[b])
                if layer:
                    for j in range(4):
                        i = 4 * b + j
                        k_sq = act.do(lambda e, i=i, j=j, x=x: e.activation(junk[:, :], x[:, j, :], ACT.Square, accum_out=SS[:, i:i + 1]), k_norm[b], k_sq)
                k_last["at"] = (b, 1)
                yield
                evac = []
                for c in range(2):
                    bk = take()
                    for j in range(4):
                        f = lambda e, j=j, c=c, x=x, n=bk[1]: e.transpose(ps(n, 128 * j, 128 * j + 128), x[:, j, 128 * c:128 * c + 128], ident)
                        if j == 3:
                            k_tr[b] = pe.do(f)
                        else:
                            pe.put(f, k_norm[b], bk[0], k_cst)
                    if c == 0:
                        bk[0] = act.do(lambda e, b=b, n=bk[1]: e.activation(xnT[:, 0, 512 * b:512 * b + 512], ps(n, 0, 512), ACT.Copy), k_tr[b], freeT[b])
                        if layer == 0 and b:
                            yield
                    else:
                        bk[0] = dve.do(lambda e, b=b, n=bk[1]: e.tensor_copy(xnT[:, 1, 512 * b:512 * b + 512], ps(n, 0, 512)), k_tr[b], freeT[b])
                    evac.append(bk[0])
                k_T[b] = evac
                k_last["at"] = (b, 2)
                yield
                bk = take()
                pe.put(lambda e, b=b, n=bk[1]: e.matmul(ps(n, 0, 512), wr[:, 0, :], xnT[:, 0, 512 * b:512 * b + 512], start=True, stop=False), k_T[b], kwr, bk[0])
                k4 = pe.do(lambda e, b=b, n=bk[1]: e.matmul(ps(n, 0, 512), wr[:, 1, :], xnT[:, 1, 512 * b:512 * b + 512], start=False, stop=True))
                bk[0] = k_lgt[b] = dve.do(lambda e, n=bk[1], lt=lt: e.tensor_copy(lt[0:nr, :], PS[0:nr, n, :]), k4, k_lgp.get(b - deep))
                k_last["at"] = (b, 3)
                yield
                bk = take()
                for j in range(4):
                    f = lambda e, j=j, n=bk[1], lt=lt: e.transpose(ps(n, nr * j, nr * j + nr), lt[0:nr, 128 * j:128 * j + 128], ident[0:nr, 0:nr])
                    if j == 3:
                        k_lgp[b] = pe.do(f)
                    else:
                        pe.put(f, k_lgt[b], bk[0])
                bk[0] = k_lgev[b] = dve.do(lambda e, b=b, n=bk[1]: e.tensor_copy(lgall[:, 4 * b:4 * b + 4, :], ps(n, 0, 4 * nr).rearrange("p (i n) -> p i n", i=4)), k_lgp[b])
                if layer and b + 1 < NB and b + 1 in ready:
                    stats(b + 1)
                    root([b + 1])
                k_last.update(sq=k_sq, pe=k_lgp[b], norm=k_norm[b], at=(b + 1, 0))
                yield

        def top2(lg, k_lg, layer, bank, res):
            full = lambda: view(carve(256), 256).rearrange("p (i e) -> p i e", i=NT)
            two = carve(512)
            M8 = view(two, 256).rearrange("p (i e) -> p i e", i=NT)
            LG = view(two + 256, 256).rearrange("p (i e) -> p i e", i=NT)
            NTB = view(two, 256).rearrange("p (e j) -> p e j", e=8)
            CMP = view(two, 7 * 72).rearrange("p (i e) -> p i e", e=7)
            ix = carve(256)
            IX = view(ix, 256, U32).rearrange("p (i e) -> p i e", i=NT)
            IXF = view(ix, 256).rearrange("p (i e) -> p i e", i=NT)
            OH1, OH2, C, A, B = (full() for _ in range(5))
            n8 = [view(carve(8), 8) for _ in range(5)]
            bc = lambda ap: ap.to_broadcast([128, NT, 8])
            k = k_lg
            V = lambda f, *w: dve.do(f, *w)
            if layer == 0:
                k = V(lambda e: e.tensor_reduce(TMPS[:, 0:32], lg, AX.X, ALU.max), k)
                k = V(lambda e: e.tensor_tensor(A, lg, bc(TMPS[:, 0:32].unsqueeze(2)), ALU.subtract), k)
                k = act.do(lambda e: e.activation(A, A, ACT.Exp), k)
                k = V(lambda e: e.tensor_reduce(TMPS[:, 32:64], A, AX.X, ALU.add), k)
                k = V(lambda e: e.reciprocal(TMPS[:, 32:64], TMPS[:, 32:64]), k)
                k = V(lambda e: e.tensor_tensor(LG, A, bc(TMPS[:, 32:64].unsqueeze(2)), ALU.mult), k)
            else:
                k = V(lambda e: e.tensor_copy(LG, lg), k)
            yield
            for i in range(NT):
                if i % 6 == 5:
                    yield
                k1 = V(lambda e, i=i: e.max(M8[:, i, :], LG[:, i, :]), k)
            for i in range(NT):
                if i % 4 == 3:
                    yield
                k2 = V(lambda e, i=i: e.max_index(IX[:, i, :], M8[:, i, :], LG[:, i, :]), k1)
            k = V(lambda e: e.tensor_copy(IXF, IX), k2)
            i8 = iota8.unsqueeze(1).to_broadcast([128, NT, 8])
            V(lambda e: e.tensor_tensor(OH1, i8, bc(IXF[:, :, 0:1]), ALU.is_equal), k)
            k = V(lambda e: e.tensor_tensor(OH2, i8, bc(IXF[:, :, 1:2]), ALU.is_equal), k)
            k = V(lambda e: e.tensor_tensor(C, OH1, OH2, ALU.add), k)
            m1, m2 = M8[:, :, 0], M8[:, :, 1]
            if layer == 0:
                w = V(lambda e: e.tensor_tensor(TMPS[:, 0:32], m1, m2, ALU.add), k)
                w = V(lambda e: e.reciprocal(TMPS[:, 0:32], TMPS[:, 0:32]), w)
                w = V(lambda e: e.tensor_tensor(META[:, :, 0, 0], m1, TMPS[:, 0:32], ALU.mult), w, k_meta[0])
                k_w = V(lambda e: e.tensor_tensor(META[:, :, 1, 0], m2, TMPS[:, 0:32], ALU.mult), w)
            else:
                w = V(lambda e: e.tensor_tensor(TMPS[:, 0:32], m2, m1, ALU.subtract), k)
                w = act.do(lambda e: e.activation(TMPS[:, 32:64], TMPS[:, 0:32], ACT.Exp), w)
                w = V(lambda e: e.tensor_scalar(TMPS[:, 0:32], TMPS[:, 32:64], 1.0, None, ALU.add), w)
                w = V(lambda e: e.reciprocal(META[:, :, 0, 0], TMPS[:, 0:32]), w, k_meta[0])
                k_w = V(lambda e: e.tensor_tensor(META[:, :, 1, 0], TMPS[:, 32:64], META[:, :, 0, 0], ALU.mult), w)
            Cf = C.rearrange("p i e -> p (i e)")
            yield
            pe.put(lambda e: e.matmul(ps(bank[1], 0, 256), Ustr, Cf, start=True, stop=True), k, k_lg, bank[0])
            k = pe.do(lambda e: e.matmul(ps(bank[1], 256, 512), ones[:, :], Cf, start=True, stop=True), k_ones)
            TOT = A
            k = V(lambda e: e.tensor_copy(TOT, ps(bank[1], 256, 512).rearrange("p (i e) -> p i e", i=NT)), k)
            k = V(lambda e: e.tensor_copy(C, ps(bank[1], 0, 256).rearrange("p (i e) -> p i e", i=NT)), k)
            bank[0] = k
            k = V(lambda e: e.tensor_copy(B, TOT), k)
            yield
            src, dst = B, IXF
            for st in (1, 2, 4, 8, 16):
                V(lambda e, st=st, s=src, d=dst: e.tensor_copy(d[:, 0:st, :], s[:, 0:st, :]), k)
                k = V(lambda e, st=st, s=src, d=dst: e.tensor_tensor(d[:, st:NT, :], s[:, st:NT, :], s[:, 0:NT - st, :], ALU.add), k)
                src, dst = dst, src
            cum, oth = src, dst
            n_e = cum[:, NT - 1, :]
            yield
            k = V(lambda e: e.tensor_tensor(NTB, n_e.unsqueeze(2).to_broadcast([128, 8, 32]),
                                            iota128.unsqueeze(1).to_broadcast([128, 8, 32]), ALU.is_gt), k)
            k = V(lambda e: e.tensor_reduce(n8[0], NTB, AX.X, ALU.add), k)
            a, b_ = n8[0], n8[1]
            for st in (1, 2, 4):
                V(lambda e, st=st, s=a, d=b_: e.tensor_copy(d[:, 0:st], s[:, 0:st]), k)
                k = V(lambda e, st=st, s=a, d=b_: e.tensor_tensor(d[:, st:8], s[:, st:8], s[:, 0:8 - st], ALU.add), k)
                if st == 1:
                    a, b_ = n8[1], n8[2]
                elif st == 2:
                    a, b_ = n8[2], n8[3]
            tend = n8[3]
            yield
            k = V(lambda e: e.tensor_tensor(n8[4], tend, n8[0], ALU.subtract), k)
            k = V(lambda e: e.tensor_scalar(n8[4], n8[4], 128.0, None, ALU.mult), k)
            k5 = V(lambda e: e.tensor_tensor(CMP[:, 0:NTILE, :], tend[:, 0:7].unsqueeze(1).to_broadcast([128, NTILE, 7]),
                                             iotaT[:, 0:NTILE].unsqueeze(2).to_broadcast([128, NTILE, 7]), ALU.is_le), k)
            k5 = V(lambda e: e.tensor_reduce(TEXP[:, 0:NTILE], CMP[:, 0:NTILE, :], AX.X, ALU.add), k5)
            k_tex = V(lambda e: e.tensor_copy(TEXI[:, 0:NTILE], TEXP[:, 0:NTILE]), k5)
            k = V(lambda e: e.tensor_tensor(oth, cum, TOT, ALU.subtract), k)
            k = V(lambda e: e.tensor_tensor(oth, oth, n8[4].unsqueeze(1).to_broadcast([128, NT, 8]), ALU.add), k)
            k = V(lambda e: e.tensor_tensor(oth, C, oth, ALU.add), k)
            yield
            for n, oh in enumerate((OH1, OH2)):
                k = V(lambda e, oh=oh: e.tensor_tensor(oh, oh, oth, ALU.mult), k)
                k = V(lambda e, n=n, oh=oh: e.tensor_reduce(TMPS[:, 64:96], oh, AX.X, ALU.add), k)
                k = V(lambda e, n=n: e.tensor_copy(POS[:, n, :], TMPS[:, 64:96]), k)
            res.update(w12=k_w, tex=k_tex, pos=k)

        def scatter(layer, k_store, k_pos, k_clear, res, nring=4):
            ring = [view(carve(2 * ROW), 2 * ROW).rearrange("p (k n) -> p k n", k=2) for _ in range(nring)]
            cl = [count(f"c_sl{layer}{n}") for n in range(nring)]
            cs = [count(f"c_ss{layer}{n}") for n in range(nring)]
            used = [None] * nring
            for i in range(NT):
                yield
                r = i % nring
                for n in range(2):
                    k = sp.dma(lambda e, i=i, r=r, n=n: e.dma_start(ring[r][:, n, 0:D], XN[128 * i:128 * i + 128, :]), cl[r], k_store, k_pos, used[r])
                k_meta[0] = pool.do(lambda e, i=i, r=r: e.tensor_copy(ring[r][:, :, D:ROW], META[:, i, :, :]), used[r], res["w12"], k_pos)
                for n in range(2):
                    used[r] = pool.dma(lambda e, i=i, r=r, n=n: e.indirect_dma_start(
                        Xs[layer], bass.IndirectOffsetOnAxis(ap=POS[:, n, i:i + 1], axis=0), ring[r][:, n, :], None), cs[r], k, k_clear, k_pos, k_meta[0])
            res["scat"] = [(c.sem, c.n) for c in cs]
            yield

        def moe(layer, F, WU, WD, k_wu, k_wd, k_scat, k_tex, biases, free, sums, k_sums, lag=0, high=None, extra=(), xr_at=None):
            nf = F // 128
            nh = F // 512
            xr = [view(carve(ROW) if xr_at is None else xr_at + ROW * n, ROW) for n in range(3)]
            xt = [view(carve(256), 256) for _ in range(2)]
            h = [view(carve(F), F) for _ in range(2)]
            hT = [view(carve(F), F) for _ in range(2 + lag)] if high is None else high
            y = [view(carve(256), 256) for _ in range(2)]
            NH, NHT = len(h), len(hT)
            cl = [count(f"c_ml{layer}{n}") for n in range(3)]
            cy = count(f"c_my{layer}")
            load = {}
            k_xtp, k_xte, k_up, k_gelu, k_tr, k_hte, k_dn, k_ye, k_ys, k_mi = ({} for _ in range(10))
            UPB = [1, 1 + nh]
            HTB = 1 + 2 * nh
            YB = 7
            val = {}

            def expert(e, i):
                val[i] = e.value_load(TEXI[0:1, i:i + 1], min_val=0, max_val=7)

            def load_in(i):
                if i < NTILE:
                    load[i] = sp.dma(lambda e, i=i: e.dma_start(xr[i % 3][:, :], Xs[layer][128 * i:128 * i + 128, :]), cl[i % 3], k_scat, k_xtp.get(i - 3), k_mi.get(i - 3), free)

            def xtr(i):
                if i >= NTILE:
                    return
                for c in range(2):
                    f = lambda e, i=i, c=c: e.transpose(ps(0, 256 * (i % 2) + 128 * c, 256 * (i % 2) + 128 * c + 128), xr[i % 3][:, 128 * c:128 * c + 128], ident)
                    if c:
                        k_xtp[i] = pe.do(f)
                    else:
                        pe.put(f, load[i], k_xte.get(i - 1), free)
                k_xte[i] = dve.do(lambda e, i=i: e.tensor_copy(xt[i % 2][:, :], ps(0, 256 * (i % 2), 256 * (i % 2) + 256)), k_xtp[i], k_up.get(i - 2), free)
                dve.put(lambda e, i=i: e.tensor_copy(MW[:, i % 8:i % 8 + 1], xr[i % 3][:, D:D + 1]), load[i], k_ye.get(i - 8))
                k_mi[i] = dve.do(lambda e, i=i: e.tensor_copy(MI[:, i % 8:i % 8 + 1], xr[i % 3][:, D + 1:ROW]), k_ys.get(i - 8))

            def up(i):
                if i >= NTILE:
                    return
                pe.wait(k_xte[i], k_gelu.get(i - 2), k_wu, k_tex, free)
                pe.queue.append(("do", lambda e, i=i: expert(e, i), None, 0))
                for n in range(nh):
                    for c in range(2):
                        def f(e, i=i, n=n, c=c):
                            return e.matmul(ps(UPB[i % 2] + n, 0, 512), xt[i % 2][:, 128 * c:128 * c + 128],
                                            WU[:, bass.ds(val[i] * (2 * F) + (c * F + 512 * n), 512)],
                                            start=(c == 0), stop=(c == 1 and biases is None))
                        last = f
                        if biases is None and n == nh - 1 and c == 1:
                            k_up[i] = pe.do(f)
                        else:
                            pe.put(f)
                    if biases is not None:
                        def f(e, i=i, n=n):
                            return e.matmul(ps(UPB[i % 2] + n, 0, 512), biases[2][:, bass.ds(val[i] * 128, 128)],
                                            biases[0][:, 512 * n:512 * n + 512], start=False, stop=True)
                        if n == nh - 1:
                            k_up[i] = pe.do(f)
                        else:
                            pe.put(f)
                k_gelu[i] = act.do(lambda e, i=i: e.activation(h[i % NH][:, :], ps(UPB[i % 2], 0, F), ACT.Gelu), k_up[i], k_tr.get(i - NH), free)

            def htr(i):
                for c in range(nf):
                    f = lambda e, i=i, c=c: e.transpose(ps(HTB, 128 * c, 128 * c + 128), h[i % NH][:, 128 * c:128 * c + 128], ident)
                    if c == nf - 1:
                        k_tr[i] = pe.do(f)
                    else:
                        pe.put(f, k_gelu[i], k_hte.get(i - 1))
                k_hte[i] = dve.do(lambda e, i=i: e.tensor_copy(hT[i % NHT][:, :], ps(HTB, 0, F)), k_tr[i], k_dn.get(i - NHT), free)

            def down(i):
                if i < 0:
                    return
                pe.wait(k_hte[i], k_ye.get(i - 1), k_wd)
                if lag:
                    pe.queue.append(("do", lambda e, i=i: expert(e, i), None, 0))
                o = 256 * (i % 2)
                for c in range(nf):
                    def f(e, i=i, c=c, o=o):
                        return e.matmul(ps(YB, o, o + 256), hT[i % NHT][:, 128 * c:128 * c + 128],
                                        WD[:, bass.ds(val[i] * (nf * 256) + c * 256, 256)], start=(c == 0), stop=(c == nf - 1 and biases is None))
                    if biases is None and c == nf - 1:
                        k_dn[i] = pe.do(f)
                    else:
                        pe.put(f)
                if biases is not None:
                    k_dn[i] = pe.do(lambda e, i=i, o=o: e.matmul(ps(YB, o, o + 256), biases[2][:, bass.ds(val[i] * 128, 128)],
                                                                biases[1][:, :], start=False, stop=True))
                k_ye[i] = act.do(lambda e, i=i, o=o: e.activation(y[i % 2][:, :], ps(YB, o, o + 256), ACT.Copy, scale=MW[:, i % 8:i % 8 + 1]), k_dn[i], k_ys.get(i - 2), k_mi[i], free)
                k_ys[i] = pool.dma(lambda e, i=i: e.indirect_dma_start(
                    sums, bass.IndirectOffsetOnAxis(ap=MI[:, i % 8:i % 8 + 1], axis=0), y[i % 2][:, :], None, compute_op=ALU.add), cy, k_ye[i], k_mi[i], k_ys.get(i - 1, k_sums))

            load_in(0), load_in(1), load_in(2)
            k_sums = k_sums()
            xtr(0), xtr(1)
            up(0)
            for i in range(NTILE):
                load_in(i + 3)
                for f in extra[2 * i:2 * i + 2]:
                    f()
                htr(i)
                up(i + 1)
                xtr(i + 2)
                down(i - lag)
            for i in range(NTILE - lag, NTILE):
                down(i)
            return [(cy.sem, cy.n)], [k_dn[NTILE - 1], k_ye[NTILE - 1], k_hte[NTILE - 1], k_gelu[NTILE - 1]]

        def combine(k_y, k_acc, free, done, at):
            G = [view(at + 1024 * n, 1024).rearrange("p (i d) -> p i d", i=4) for n in range(4)]
            cg = [count(f"c_g{n}") for n in range(4)]
            sv = SUM[0:T, :].rearrange("(b i p) d -> b p i d", b=NB, p=128)
            load = lambda b: sp.dma(lambda e: e.dma_start(G[b % 4], sv[b]), cg[b % 4], k_y, done.get(b - 4), free)
            k = {b: load(b) for b in range(4)}
            for b in range(NB):
                done[b] = pool.do(lambda e, b=b: e.tensor_tensor(ACC[:, 4 * b:4 * b + 4, :], ACC[:, 4 * b:4 * b + 4, :], G[b % 4], ALU.add), k[b], k_acc[b])
                if b + 4 < NB:
                    k[b + 4] = load(b + 4)
                yield

        WRV = SEL.bitcast(F32)[:, 0:256].rearrange("p (c n) -> p c n", c=2)
        c_wr, c_w = count("c_wr"), count("c_w")
        k_wr = sp.dma(lambda e: e.dma_start(WRV[:, :, :], t["Wg"]), c_wr)
        ATT = top[0]
        WQ = view(carve(512), 512).rearrange("p (c n) -> p c n", c=2)
        WK = view(carve(512), 512).rearrange("p (c n) -> p c n", c=2)
        WV = view(carve(512), 512).rearrange("p (c n) -> p c n", c=2)
        WO = view(carve(1024), 1024).rearrange("p (g n) -> p g n", g=4)
        for dst, name in ((WQ, "Wq"), (WK, "Wk"), (WV, "Wv"), (WO, "Wo")):
            k_w = sp.dma(lambda e, d=dst, n=name: e.dma_start(d[:, :, :], t[n]), c_w)
        Vb = [view(carve(2048), 2048).rearrange("p (i h d) -> p i h d", i=4, h=16) for _ in range(2)]
        STK = [[view(carve(2048), 2048, BF16).rearrange("p (j s) -> p j s", j=8) for _ in range(2)] for _ in range(3)]
        OT = [view(carve(512), 512) for _ in range(4)]
        RC = view(carve(512), 512)
        R16 = view(carve(16), 16)
        PT = [view(carve(768), 768, BF16).rearrange("p (k s) -> p k s", k=3) for _ in range(2)]
        R1 = [view(carve(512), 512) for _ in range(2)]
        NM = [view(carve(32), 32).rearrange("p (i j) -> p i j", i=4) for _ in range(2)]
        NM2 = view(carve(32), 32).rearrange("p (i j) -> p i j", i=4)
        NP = [view(carve(48), 48, BF16).rearrange("p (i k j) -> p i k j", i=4, k=3) for _ in range(2)]
        MT = [view(carve(256), 256, BF16) for _ in range(2)]
        NPB = 5
        pb0 = top[0]
        PB = [view(carve(1280), 1280) for n in range(NPB)]
        lgall = view(carve(256), 256)
        route0 = top[0]
        assert route0 + 2100 <= LIMIT, route0
        banks0 = [[None, n] for n in (4, 5, 6, 7)]
        k_mb = banks0[3]
        first = {bk[1]: bk for bk in banks0}
        ln0 = norm_and_route(0, k_x, route0, None, WRV, k_wr, 8, lgall, [None] * NB, banks0, 1)
        k_T, k_lg, lgall, k_store, k_last = next(ln0)
        while k_last["at"] != (1, 0):
            next(ln0)
        k_ob = first[6]
        banks0[:] = [k_mb, k_ob]

        def pick():
            banks0.append(banks0.pop(0))
            return banks0[-1]

        c_z, c_z0 = count("c_z"), count("c_z0")

        def clear():
            rows = lambda a: a.rearrange("(i p) d -> p i d", p=128)
            todo = [(rows(Xs[0]), c_z0)] + [(rows(Xs[1]), c_z), (rows(SUM), c_z), (out[T:T + 128, :].unsqueeze(1), c_z)]
            for dst, c in todo:
                for lo in range(0, dst.shape[1], 9):
                    piece = dst[:, lo:min(lo + 9, dst.shape[1]), :]
                    k_clear[c] = sp.dma(lambda e, piece=piece: e.dma_start(piece, NONE[:, 0:piece.shape[2]].unsqueeze(1).to_broadcast(list(piece.shape))), c, k_cst)
                    yield

        k_clear = {}
        clearing = clear()
        k_meta = [[dve.do(lambda e, n=n: e.tensor_copy(META[:, :, n, 1], token), k_cst) for n in range(2)]]
        R0 = {}
        top[0] = route0

        def routing0():
            top[0] = route0
            yield from top2(lgall, [k_lg[-1], k_store[-1]], 0, k_mb, R0)
            assert top[0] <= LIMIT
            top[0] = route0
            yield from scatter(0, k_store[-2:], R0["pos"], k_clear[c_z0], R0)

        free = []
        k_init = k_eps
        for n in range(3):
            k_init = pool.do(lambda e, s=STK[n][1]: e.memset(s[96:99, :, :], 1.0), k_init)
        k_vinit = [pool.do(lambda e, v=v: e.memset(v, 0.0), k_init) for v in Vb]
        k_vinit = [pool.do(lambda e, v=v: e.memset(v[:, :, :, 16:17], 1.0), *k_vinit) for v in Vb][-1]
        c_st = [[count(f"c_st{n}{m}") for m in range(2)] for n in range(3)]
        c_sp = [[count(f"c_sp{n}{m}") for m in range(2)] for n in range(3)]
        c_m = [count(f"c_m{n}") for n in range(3)]
        SLOTS = [[0, 0, 1, 1, 0, 2], [0, 1, 0, 1, 2, 0]]
        off = {3: 0, 2: 512, 0: 896, 1: 1024}
        offT = {0: 0, 1: 512, 3: 896, 2: 1024}
        SB0, TB0, OB, MB = 0, 3, 6, 7
        k_stack, k_mrow, k_s, k_red, k_st_, k_exp, k_pv, k_pt, k_v = ({} for _ in range(9))
        k_pt_free = [None, None]
        NHB = 2 * NB

        def project(n):
            b, half = divmod(n, 2)
            assert k_T[b] is not None
            todo = []
            for m, W in enumerate((WQ, WK)):
                bk = pick()
                for c in range(2):
                    f = lambda e, bk=bk, m=m, W=W, c=c: e.matmul(ps(bk[1], 0, 512), W[:, c, 128 * half:128 * half + 128], xnT[:, c, 512 * b:512 * b + 512], start=(c == 0), stop=(c == 1))
                    if c:
                        k = pe.do(f)
                    else:
                        pe.put(f, k_T[b], k_w, bk[0], *free)
                pt, r1 = PT[m], R1[m]
                k1 = act.do(lambda e, bk=bk, pt=pt: e.activation(pt[:, 0, :], ps(bk[1], 0, 512), ACT.Copy), k, k_pt_free[m], *free)
                k2 = dve.do(lambda e, bk=bk, pt=pt, r1=r1: e.tensor_tensor(r1[:, :], ps(bk[1], 0, 512), pt[:, 0, :], ALU.subtract), k1, k_pt_free[m])
                bk[0] = k2
                k3 = dve.do(lambda e, pt=pt, r1=r1: e.tensor_copy(pt[:, 1, :], r1[:, :]), k2, k_init)
                k4 = pool.do(lambda e, pt=pt, r1=r1: e.tensor_tensor(pt[:, 2, :], r1[:, :], pt[:, 1, :], ALU.subtract), k3)
                dst = STK[n % 3][m]
                box = SPL[n % 3, m]
                k_pt_free[m] = sp.dma(lambda e, box=box, pt=pt: e.dma_start(box, pt), c_sp[n % 3][m], k4, k_stack.get((n - 3, m)))
                todo.append((m, dst, box))
                if m == 0:
                    yield
            for m, dst, box in todo:
                for sl, part in enumerate(SLOTS[m]):
                    kk = sp.dma(lambda e, dst=dst, box=box, sl=sl, part=part: e.dma_start(
                        dst[16 * sl:16 * sl + 16, :, :], box[:, part, :].rearrange("(j d) s -> d j s", j=8)),
                        c_st[n % 3][m], k_pt_free[m], k_st_.get((n - 3, 7)), k_s.get((n - 3, 7)))
                k_stack[n, m] = kk

        def project_v(b):
            vb = Vb[b % 2]
            assert k_T[b] is not None
            for i in range(4):
                o = 256 * (i % 2)
                if i % 2 == 0:
                    bk = pick()
                for c in range(2):
                    f = lambda e, bk=bk, i=i, c=c, o=o: e.matmul(ps(bk[1], o, o + 256), xnT[:, c, 512 * b + 128 * i:512 * b + 128 * i + 128], WV[:, c, :], start=(c == 0), stop=(c == 1))
                    if c:
                        k = pe.do(f)
                    else:
                        pe.put(f, k_T[b], k_w, bk[0], *free)
                if i % 2:
                    bk[0] = k_v[b] = act.do(lambda e, bk=bk, i=i, vb=vb: e.activation(vb[:, i - 1:i + 1, :, 0:16], ps(bk[1], 0, 512).rearrange("p (i h d) -> p i h d", i=2, h=16), ACT.Copy), k, k_vinit, k_pv.get((2 * b - 3, 1)))
                    yield

        def scores(n, j):
            q, k = STK[n % 3]
            for i in (3, 2, 0, 1):
                w = 128 * (i + 1)
                pe.put(lambda e, i=i, w=w: e.matmul(ps(SB0, off[i], off[i] + w), q[0:96, j, 128 * i:128 * i + 128], k[0:96, j, 0:w], start=True, stop=False),
                       k_stack[n, 0], k_stack[n, 1], k_sbank[off[i] // 512], k_init)
                kk = pe.do(lambda e, i=i, w=w: e.matmul(ps(SB0, off[i] + w - 128, off[i] + w), identb, M1b, start=False, stop=True))
                for r in {3: (3,), 2: (), 0: (2, 0), 1: (1,)}[i]:
                    k_sbank[off[r] // 512] = k_red[n, j] = dve.do(lambda e, r=r: e.tensor_reduce(NM[n % 2][:, r, j:j + 1], ps(SB0, off[r], off[r] + 128 * (r + 1)), AX.X, ALU.max, negate=True), kk, k_pt.get(n - 2), *free)
            k_s[n, j] = kk

        def maxima(n):
            yield
            nm, np_, mt = NM[n % 2], NP[n % 2], MT[n % 2]
            k1 = dve.do(lambda e: e.tensor_copy(np_[:, :, 0, :], nm), k_red[n, 7], k_pt.get(n - 2))
            k1 = dve.do(lambda e: e.tensor_tensor(NM2, nm, np_[:, :, 0, :], ALU.subtract), k1)
            k1 = dve.do(lambda e: e.tensor_copy(np_[:, :, 1, :], NM2), k1)
            k1 = dve.do(lambda e: e.tensor_tensor(np_[:, :, 2, :], NM2, np_[:, :, 1, :], ALU.subtract), k1)
            yield
            bk = pick()
            pmt = ps(bk[1], 0, 256).bitcast(BF16)
            for i in range(4):
                f = lambda e, bk=bk, i=i: e.transpose(pmt[0:24, 128 * i:128 * i + 128], np_[:, i, :, :].rearrange("p k j -> p (k j)"), identb)
                if i == 3:
                    k_pt[n] = pe.do(f)
                else:
                    pe.put(f, k1, bk[0])
            k2 = act.do(lambda e: e.activation(mt[0:24, :], pmt[0:24, :], ACT.Copy), k_pt[n], k_mrow.get(n - 2), *free)
            bk[0] = k2
            for k in range(3):
                k_mrow[n] = sp.dma(lambda e, k=k: e.dma_start(STK[n % 3][0][96 + k:97 + k, :, :], mt[8 * k:8 * k + 8, :]), c_m[n % 3], k2, k_s[n, 7], k_st_.get((n - 3, 7)), k_init)

        def scoresT(n, j):
            q, k = STK[n % 3]
            idx = 8 * n + j
            o = idx - NPB
            for kb in (0, 1, 3, 2):
                w = 512 - 128 * kb
                pe.put(lambda e, kb=kb, w=w: e.matmul(ps(TB0, offT[kb], offT[kb] + w), k[0:99, j, 128 * kb:128 * kb + 128], q[0:99, j, 128 * kb:512], start=True, stop=False),
                       k_mrow[n], k_tbank[offT[kb] // 512])
                kk = pe.do(lambda e, kb=kb: e.matmul(ps(TB0, offT[kb], offT[kb] + 128), identb, M2b, start=False, stop=True))
                if kb in (0, 2):
                    lo, hi = (0, 512) if kb == 0 else (512, 1280)
                    k_exp[n, j] = act.do(lambda e, lo=lo, hi=hi: e.activation(PB[idx % NPB][:, lo:hi], ps(TB0, lo, hi), ACT.Exp, scale=0.25), kk, k_pv.get((o // 8, (o % 8) // 4)) if o >= 0 else k_br)
                    for bank in range(lo // 512, (hi + 511) // 512):
                        k_tbank[bank] = k_exp[n, j]
            k_st_[n, j] = kk

        def values(n, g):
            b, half = divmod(n, 2)
            vb = Vb[b % 2]
            for kb in range(4):
                w = 512 - 128 * kb
                for j in range(4):
                    jj = 4 * g + j
                    p = PB[(8 * n + jj) % NPB]
                    f = lambda e, kb=kb, j=j, jj=jj, p=p, w=w: e.matmul(
                        PS[32 * j:32 * j + 32, OB, 128 * kb:512], vb[:, kb, 8 * half + jj, :], p[:, offT[kb]:offT[kb] + w], start=(kb == 0), stop=(kb == 3))
                    if kb == 3 and j == 3:
                        k_pv[n, g] = pe.do(f)
                    else:
                        pe.put(f, k_exp[n, jj], k_v[b], k_ob[0])
            assert b == 0 or b - 1 in k_wo
            G = 2 * half + g
            ot = OT[G]
            k1 = act.do(lambda e: e.activation(ot[:, :], ps(OB, 0, 512), ACT.Copy), k_pv[n, g], k_wo.get(b - 1), *free)
            k_ob[0] = k1
            yield
            bk = pick()
            for i in range(4):
                f = lambda e, bk=bk, i=i: e.transpose(ps(bk[1], 128 * i, 128 * i + 128), ot[:, 128 * i:128 * i + 128], ident)
                if i == 3:
                    k2 = pe.do(f)
                else:
                    pe.put(f, k1, bk[0])
            tm = ps(bk[1], 0, 512).rearrange("p (h r) -> p h r", r=32)
            k3 = dve.do(lambda e, tm=tm: e.reciprocal(R16, tm[:, :, 16]), k2, k_nrm[0])
            bk[0] = k3 = dve.do(lambda e, tm=tm: e.tensor_tensor(RC[:, :].rearrange("p (h r) -> p h r", r=32), tm, R16.unsqueeze(2).to_broadcast([128, 16, 32]), ALU.mult), k3)
            yield
            bk = pick()
            for i in range(4):
                f = lambda e, bk=bk, i=i: e.transpose(ps(bk[1], 128 * i, 128 * i + 128), RC[:, 128 * i:128 * i + 128], ident)
                if i == 3:
                    k4 = pe.do(f)
                else:
                    pe.put(f, k3, bk[0])
            bk[0] = k_nrm[0] = act.do(lambda e, bk=bk: e.activation(ot[:, :], ps(bk[1], 0, 512), ACT.Copy), k4, k2)

        def output(b):
            for i in range(4):
                o = 256 * (i % 2)
                if i % 2 == 0:
                    bk = pick()
                for g in range(4):
                    f = lambda e, bk=bk, i=i, g=g, o=o: e.matmul(ps(bk[1], o, o + 256), OT[g][:, 128 * i:128 * i + 128], WO[:, g, :], start=(g == 0), stop=(g == 3))
                    if g == 3:
                        k = pe.do(f)
                    else:
                        pe.put(f, k_nrm[0], bk[0])
                if i == 3:
                    k_wo[b] = k
                if i % 2:
                    k_acc0[b] = bk[0] = dve.do(lambda e, bk=bk, i=i: e.tensor_tensor(ACC[:, 4 * b + i - 1:4 * b + i + 1, :], ps(bk[1], 0, 512).rearrange("p (i d) -> p i d", i=2), ACC[:, 4 * b + i - 1:4 * b + i + 1, :], ALU.add), k)
                    yield

        k_sbank, k_tbank = [None] * 3, [None, first[4][0], first[5][0]]
        k_nrm, k_wo, k_acc0 = [None], {}, {}
        steps = []

        def later(order, gen):
            steps.append((order, len(done_steps), gen))
            done_steps.append(None)
            steps.sort(key=lambda x: x[:2])

        done_steps = []

        def step():
            while steps:
                try:
                    next(steps[0][2])
                    return
                except StopIteration:
                    steps.pop(0)

        for n in range(2):
            for _ in project(n):
                pass
        for _ in project_v(0):
            pass
        k_b3 = pool.do(lambda e: e.memset(B1S, 0.0), *free)
        k_b3 = pool.do(lambda e: e.memset(B2S, 0.0))
        c_bl, c_br = count("c_bl"), count("c_br")
        bf = view(pb0, 1280)
        b3 = view(pb0 + 1280, 3 * 640, BF16).rearrange("p (k n) -> p k n", k=3)
        kb = sp.dma(lambda e: e.dma_start(bf[0:8, 0:1024], t["b1"]), c_bl)
        kb = sp.dma(lambda e: e.dma_start(bf[0:8, 1024:1280], t["b2"]), c_bl)
        for k in range(3):
            kb = pool.do(lambda e, k=k: e.tensor_copy(b3[0:8, k, :], bf[0:8, :]), kb)
            if k < 2:
                kb = pool.do(lambda e, k=k: e.tensor_tensor(bf[0:8, :], bf[0:8, :], b3[0:8, k, :], ALU.subtract), kb)
        for k in range(3):
            k_br = sp.dma(lambda e, k=k: e.dma_start(B1S[8 * k:8 * k + 8, :], b3[0:8, k, 0:1024]), c_br, kb, k_b3)
            k_br = sp.dma(lambda e, k=k: e.dma_start(B2S[8 * k:8 * k + 8, :], b3[0:8, k, 1024:1280]), c_br, kb, k_b3)

        rt = routing0()
        LEAD, NH = 11, 8 * NHB
        for idx in range(-LEAD, NH + 1):
            if idx % 8 == 0 and 2 <= idx // 8 + 2 < NHB:
                later(0, project(idx // 8 + 2))
            lead = idx + LEAD
            if lead < NH:
                scores(lead // 8, lead % 8)
                if lead % 8 == 7:
                    later(0, maxima(lead // 8))
                step()
            if 0 <= idx < NH:
                scoresT(idx // 8, idx % 8)
            step()
            if idx >= 4 and idx % 4 == 0:
                gq = idx // 4 - 1
                vals = values(gq // 2, gq % 2)
                next(vals)
                later(1, vals)
                if gq % 4 == 3:
                    later(2, output(gq // 4))
            if idx % 16 == 0 and idx // 16 + 1 < NB and idx >= 0:
                later(3, project_v(idx // 16 + 1))
            if k_last["at"] != (NB, 0):
                next(ln0)
            elif idx >= 0:
                next(rt, None)
            if idx > 5:
                next(clearing, None)
        while steps:
            step()
        k_zero = k_clear[c_z]
        assert next(clearing, 0) == 0
        for _ in rt:
            pass

        top[0] = base
        free = [k_wo[NB - 1], k_nrm[0], k_acc0[NB - 1], *R0["scat"]]
        WU = view(carve(8192), 8192)
        WD = view(carve(8192), 8192)
        top[0] = LIMIT - 11520
        W1 = view(carve(1024), 1024).rearrange("p (c n) -> p c n", c=2)
        W2 = view(carve(1024), 1024).rearrange("p (c n) -> p c n", c=4)
        hs = [view(carve(2048), 2048).rearrange("p (c n) -> p c n", c=4) for _ in range(2)]
        c_w0, c_wu, c_wd = count("c_w0"), count("c_wu"), count("c_wd")
        k_w0 = sp.dma(lambda e: e.dma_start(W1[:, :, :], t["W1"]), c_w0, *free)
        k_w0 = sp.dma(lambda e: e.dma_start(W2[:, :, :], t["W2"]), c_w0)
        for q in range(4):
            k_wu = sp.dma(lambda e, q=q: e.dma_start(WU[:, 2048 * q:2048 * q + 2048], t["Wu"][:, 2048 * q:2048 * q + 2048]), c_wu)
        for q in range(4):
            k_wd = sp.dma(lambda e, q=q: e.dma_start(WD[:, 2048 * q:2048 * q + 2048], t["Wd"][:, 2048 * q:2048 * q + 2048]), c_wd)
        k_g, k_sd, k_dn, k_acc1 = {}, [None, None], {}, {}

        def shared_up(b):
            for fc in range(4):
                bank = fc % 2
                for c in range(2):
                    f = lambda e, fc=fc, c=c, bank=bank: e.matmul(ps(bank, 0, 512), W1[:, c, 128 * fc:128 * fc + 128], xnT[:, c, 512 * b:512 * b + 512], start=(c == 0), stop=(c == 1))
                    if c:
                        k = pe.do(f)
                    else:
                        pe.put(f, k_w0, k_g.get((b - 1, fc + 2) if fc < 2 else (b, fc - 2)), *free)
                k_g[b, fc] = act.do(lambda e, fc=fc, bank=bank: e.activation(hs[b % 2][:, fc, :], ps(bank, 0, 512), ACT.Gelu), k, k_dn.get(b - 2), *free)
                yield

        def shared_down(b):
            for i in range(4):
                bank = 2 + i % 2
                for fc in range(4):
                    f = lambda e, i=i, fc=fc, bank=bank: e.matmul(ps(bank, 0, 256), hs[b % 2][:, fc, 128 * i:128 * i + 128], W2[:, fc, :], start=(fc == 0), stop=(fc == 3))
                    if fc == 3:
                        k_dn[b] = pe.do(f)
                    else:
                        pe.put(f, k_g[b, 3], k_sd[i % 2], *free)
                k_sd[i % 2] = k_acc1[b] = dve.do(lambda e, i=i, bank=bank: e.tensor_tensor(ACC[:, 4 * b + i, :], ps(bank, 0, 256), ACC[:, 4 * b + i, :], ALU.add), k_dn[b], k_acc0[b])
                yield

        def shared(lo, hi, then=lambda: None, after=lambda b: None):
            for b in range(lo, hi + 1):
                for g in ([shared_up(b)] if b < hi else []) + ([shared_down(b - 1)] if b > lo else []):
                    for _ in g:
                        then()
                if b > lo:
                    after(b - 1)

        HB = 3
        shared(0, HB)
        k_y, k_end = moe(0, F0, WU, WD, k_wu, k_wd, R0["scat"], R0["tex"], None, [*free, k_acc1[HB - 1], k_g[HB - 1, 3]], SUM, lambda: k_zero)
        free = [*free, *k_end]
        k_x1 = {}
        comb = combine(k_y, k_acc1, free, k_x1, LIMIT - 11520 + 6144)
        top[0] = base
        WCR = view(carve(256), 256).rearrange("p (c n) -> p c n", c=2)
        NW = view(carve(2), 2)
        QKW = view(carve(1536), 1536).rearrange("p (c n) -> p c n", c=2)
        WOUT = view(carve(512), 512).rearrange("p (c n) -> p c n", c=2)
        COS = view(carve(128), 128).rearrange("p (i d) -> p i d", i=4)
        SIN = view(carve(128), 128).rearrange("p (i d) -> p i d", i=4)
        GB = view(carve(24), 24)
        RB = view(carve(8), 8)
        BO = view(carve(256), 256)
        LREG = top[0]
        c_w1 = count("c_w1")
        ends = k_end
        for dst, name in ((WCR, "Wcr"), (NW, "nw"), (QKW, "Wqkv"), (WOUT, "Wout"), (COS, "cos"), (SIN, "sin"), (GB, "gb"), (RB, "rb"), (BO, "bo"), (SEL.bitcast(F32), "sel")):
            k_w1 = sp.dma(lambda e, d=dst, n=name: e.dma_start(d, t[n]), c_w1, *ends)
        k_nw = k_w1
        for c in range(2):
            k_nw = pool.do(lambda e, c=c: e.tensor_scalar(QKW[:, c, :], QKW[:, c, :], NW[:, c:c + 1], None, ALU.mult), k_w1)
            k_nw = pool.do(lambda e, c=c: e.tensor_scalar(WCR[:, c, 8:32], WCR[:, c, 8:32], NW[:, c:c + 1], None, ALU.mult), k_w1)
        top[0] = LREG + 9800
        g_r, g_o, LF, EF, EU = (view(carve(256), 256).rearrange("p (i h) -> p i h", i=NT) for _ in range(5))
        ET = view(carve(64), 64).rearrange("p (g i) -> p g i", g=2)
        MST = view(carve(2048), 2048).rearrange("p (b g n) -> p b g n", b=NB, g=2)
        BD = view(carve(128), 128)
        MTMP = view(carve(256), 256).rearrange("p (g n) -> p g n", g=2)
        low_end = top[0]
        LRT = view(carve(256), 256).rearrange("p (i e) -> p i e", i=NT)
        route1 = top[0]
        lgall = view(carve(NT * 32), NT * 32)
        GZ = view(carve(NT * 24), NT * 24).rearrange("p (i n) -> p i n", i=NT)
        eta = carve(512)
        ETA = view(eta, 512).rearrange("p (g i h) -> p g i h", g=2, i=NT)
        route1_end = route1 + 2100
        k_xfree = {b: k_g[b, 3] for b in range(HB)}
        banks1 = [[None, n] for n in (4, 5, 6, 7)]
        ln1 = norm_and_route(1, k_x1, LREG, [*k_end], WCR, [k_nw], 32, lgall, k_xfree, banks1, 2)
        k_T, k_lg, lgall, k_store, k_last = next(ln1)

        calls, SKIP = [], 10

        def advance():
            calls.append(None)
            b = k_last["at"][0]
            for nb in range(len(k_x1), min(b + 2, NB)):
                if nb in k_xfree:
                    next(comb)
            if b in k_x1 and len(calls) > SKIP:
                next(ln1)

        shared(HB, NB, advance, lambda b: k_xfree.update({b: k_g[b, 3]}))
        while k_last["at"] != (NB, 0):
            advance()
        fre = [*k_end, k_x1[NB - 1], k_last["pe"], k_last["norm"], k_last["sq"], *k_store[-2:], k_dn[NB - 1], k_acc1[NB - 1]]
        k = dve.do(lambda e: e.tensor_tensor(LRT, lgall[:, :, 0:8], RB.unsqueeze(1).to_broadcast([128, NT, 8]), ALU.add), k_lg[-1], k_w1, *fre)
        k_lrt = k
        kr = act.do(lambda e: e.activation(RT[:, :], SS[:, :], ACT.Sqrt, bias=EPS6[:, :], scale=1.0 / D), k_last["sq"])
        kr = dve.do(lambda e: e.reciprocal(RT[:, :], RT[:, :]), kr)
        kz = dve.do(lambda e: e.tensor_tensor(GZ, lgall[:, :, 8:32], RT.unsqueeze(2).to_broadcast([128, NT, 24]), ALU.mult), kr)
        kz = dve.do(lambda e: e.tensor_tensor(GZ, GZ, GB.unsqueeze(1).to_broadcast([128, NT, 24]), ALU.add), kz)
        kz = act.do(lambda e: e.activation(GZ, GZ, ACT.Exp, scale=-1.0), kz)
        kz = dve.do(lambda e: e.tensor_scalar(GZ, GZ, 2.0 ** 62, 1.0, ALU.min, ALU.add), kz)
        kl = act.do(lambda e: e.activation(LF, GZ[:, :, 0:8], ACT.Ln), kz, *fre)
        kg = dve.do(lambda e: e.reciprocal(GZ[:, :, 8:24], GZ[:, :, 8:24]), kz)
        kg = dve.do(lambda e: e.tensor_tensor(GZ[:, :, 8:24], GZ[:, :, 8:24], RT.unsqueeze(2).to_broadcast([128, NT, 16]), ALU.mult), kg)
        kg1 = dve.do(lambda e: e.tensor_scalar(g_r, GZ[:, :, 8:16], float(1.0 / np.sqrt(32.0)), None, ALU.mult), kg)
        k_gates = dve.do(lambda e: e.tensor_copy(g_o, GZ[:, :, 16:24]), kg)
        LFf = LF.rearrange("p i h -> p (i h)")
        kd = None
        for n, (mat, dst) in enumerate(((Uinc, EF), (Lstr, EU), (ones, None))):
            kd = pe.do(lambda e, mat=mat: e.matmul(ps(0, 0, 256), mat[:, :], LFf, start=True, stop=True), kl, kd, k_T[NB - 1])
            if dst is not None:
                kd = act.do(lambda e, dst=dst: e.activation(dst, ps(0, 0, 256).rearrange("p (i h) -> p i h", i=NT), ACT.Exp, scale=-1.0), kd, *fre)
            else:
                for g in range(2):
                    kd = act.do(lambda e, g=g: e.activation(ETA[:, g, :, :], ps(0, 0, 256).rearrange("p (i h) -> p i h", i=NT), ACT.Exp, scale=-1.0), kd)
        for g in range(2):
            kd = dve.do(lambda e, g=g: e.tensor_tensor(ETA[:, g, :, :], ETA[:, g, :, :], hsel[:, 8 * g:8 * g + 8].unsqueeze(1).to_broadcast([128, NT, 8]), ALU.mult), kd)
        k_dec = dve.do(lambda e: e.tensor_reduce(ET, ETA, AX.X, ALU.add), kd)
        RR1 = {}
        bank5 = [None, 5]

        def routing1():
            top[0] = route1
            yield from top2(LRT, [k_lrt, k_gates, k_dec], 1, bank5, RR1)
            assert top[0] <= route1_end
            top[0] = route1
            yield from scatter(1, k_store[-2:], RR1["pos"], k_zero, RR1)

        rt = routing1()

        top[0] = LREG
        lf = [k_gates, k_dec, kg1]
        T1, T2 = (view(carve(512), 512).rearrange("p (h d) -> p h d", h=16) for _ in range(2))
        QO2, QE2, KR2, KD2, VP2 = ([view(carve(256), 256) for _ in range(2)] for _ in range(5))
        LU = view(carve(1024), 1024).rearrange("p (h n) -> p h n", h=8)
        DD2 = [view(carve(1024), 1024).rearrange("p (g n) -> p g n", g=2) for _ in range(2)]
        QB = [view(carve(512), 512).rearrange("p (j n) -> p j n", j=4) for _ in range(2)]
        QET = view(carve(256), 256)
        KT = view(carve(256), 256)
        WT = [view(carve(512), 512) for _ in range(2)]
        YT = view(carve(256), 256)
        XB = view(carve(256), 256)
        assert top[0] <= LREG + 9800
        h8 = lambda ap: ap.rearrange("p (h d) -> p h d", h=8)
        kq0 = pool.do(lambda e: e.memset(QB[0], 0.0), *lf)
        kq0 = pool.do(lambda e: e.memset(QB[1], 0.0), *lf)
        order = [4 * b + c for c in range(4) for b in range(NB)]
        K = {}
        k_m = {}
        k_acc2 = {}

        hb = lambda ap: ap.unsqueeze(2).to_broadcast([128, 8, 32])

        def project_qk(i, p, pp, par):
            c4 = i % 4
            QO, QE, KR = (z[par] for z in (QO2, QE2, KR2))
            for c in range(2):
                f = lambda e, c=c: e.matmul(ps(0, 0, 512), xnT[:, c, 128 * i:128 * i + 128], QKW[:, c, 0:512], start=(c == 0), stop=(c == 1))
                if c:
                    kqk = pe.do(f)
                else:
                    pe.put(f, k_T[-1], k_nw, K.get(("rope", p)), *lf)
            q3 = ps(0, 0, 512).rearrange("p (h d) -> p h d", h=16)
            cs, sn = COS[:, c4, :], SIN[:, c4, :]
            bc = lambda ap: ap.unsqueeze(1).to_broadcast([128, 16, ap.shape[1]])
            dve.put(lambda e: e.tensor_tensor(T1, q3, bc(cs), ALU.mult), kqk, K.get(("rot", p)), *lf)
            dve.put(lambda e: e.tensor_tensor(T2[:, :, 0:16], q3[:, :, 16:32], bc(sn[:, 0:16]), ALU.mult))
            r2 = dve.do(lambda e: e.tensor_tensor(T2[:, :, 16:32], q3[:, :, 0:16], bc(sn[:, 16:32]), ALU.mult))
            K["rope", i] = r2
            rr = pool.do(lambda e: e.tensor_tensor(T1, T1, T2, ALU.add), r2)
            a2 = act.do(lambda e: e.activation(h8(KR), T1[:, 8:16, :], ACT.Copy, scale=RT[:, i:i + 1]), rr, K.get(("T", pp)), K.get(("kd", pp)))
            a1 = pool.do(lambda e: e.tensor_tensor(h8(QO), T1[:, 0:8, :], hb(g_o[:, i, :]), ALU.mult), rr, K.get(("T", pp)))
            a3 = pool.do(lambda e: e.tensor_tensor(h8(QE), h8(QO), hb(EF[:, i, :]), ALU.mult), a1, K.get(("T", pp)))
            K["rot", i] = [a1, a2]
            K["pre", i] = [a1, a2, a3]

        def project_val(i, p, pp, par):
            for c in range(2):
                f = lambda e, c=c: e.matmul(ps(1, 0, 256), xnT[:, c, 128 * i:128 * i + 128], QKW[:, c, 512:768], start=(c == 0), stop=(c == 1))
                if c:
                    kv = pe.do(f)
                else:
                    pe.put(f, K.get(("dMe", pp)), K.get(("vp", p)))
            K["vp", i] = dve.do(lambda e: e.tensor_tensor(h8(VP2[par]), h8(ps(1, 0, 256)), hb(g_r[:, i, :]), ALU.mult), kv, K.get(("dM", pp)))

        def logs(i, p):
            K["lu", i] = pool.do(lambda e: e.tensor_tensor(LU, Uinc.unsqueeze(1).to_broadcast([128, 8, 128]), LF[:, i, :].unsqueeze(2).to_broadcast([128, 8, 128]), ALU.mult), K.get(("D", p)), kbd, *lf)

        def decays(i, p, pp, par):
            for g in range(2):
                pe.put(lambda e, g=g: e.matmul(ps(2 + g, 0, 512), Lstr, LU[:, 4 * g:4 * g + 4, :].rearrange("p h n -> p (h n)"), start=True, stop=False), K["lu", i], K.get(("DD", p)), *lf)
                kD = pe.do(lambda e, g=g: e.matmul(ps(2 + g, 0, 512).rearrange("p (h n) -> p h n", h=4), identb, M2p.unsqueeze(1).to_broadcast([128, 4, 128]), start=False, stop=True))
            K["D", i] = kD
            K["DD", i] = act.do(lambda e: e.activation(DD2[par], PS[:, 2:4, :], ACT.Exp, scale=-1.0), kD, K.get(("W", pp)), *lf)

        def turn(i, p, pp, par):
            c4 = i % 4
            QO, QE, KR = (z[par] for z in (QO2, QE2, KR2))
            for g in range(2):
                for n, src in enumerate((QO, KR, QE)):
                    if n == 2 and c4 == 0:
                        continue
                    f = lambda e, g=g, n=n, src=src: e.transpose(ps(4 + g, 128 * n, 128 * n + 128), src[:, 128 * g:128 * g + 128], ident)
                    kt = pe.do(f, K["pre", i], K.get(("ev", p)), K.get(("acc", pp)), K.get(("W", p)), bank5[0])
                K["T", i] = kt
                def copy(dst, src, *ticks, g=g):
                    if g == 0:
                        return act.do(lambda e: e.activation(dst, src, ACT.Copy), *ticks)
                    return dve.do(lambda e: e.tensor_copy(dst, src), *ticks)
                ev = []
                for j in range(4):
                    ev.append(copy(QB[g][32 * j:32 * j + 32, j, :], PS[32 * j:32 * j + 32, 4 + g, 0:128], kt, K.get(("A", p)), kq0))
                ev.append(copy(KT[:, 128 * g:128 * g + 128], ps(4 + g, 128, 256), kt, K.get(("A", p))))
                if c4:
                    ev.append(copy(QET[:, 128 * g:128 * g + 128], ps(4 + g, 256, 384), kt, K.get(("Y", p))))
                K["evg", i, g] = ev
            K["ev", i] = [*K["evg", i, 0], *K["evg", i, 1]]

        def affinity(i, p, par, g):
            bank = (6, 5)[g]
            kA = pe.do(lambda e, g=g: e.matmul(ps(bank, 0, 512), KT[:, 128 * g:128 * g + 128], QB[g].rearrange("p j n -> p (j n)"), start=True, stop=True), *K["evg", i, g], K.get(("W0", p)) if g == 0 else None)
            K["W", i] = dve.do(lambda e, g=g: e.tensor_tensor(WT[g][:, :], ps(bank, 0, 512), DD2[par][:, g, :], ALU.mult), kA, K["DD", i], K.get(("Y", p)))
            if g == 0:
                K["W0", i] = K["W", i]
            K["A", i] = kA

        def read_and_update(i, p, pp, par):
            b, c4 = divmod(i, 4)
            KR, KD, VP = KR2[par], KD2[par], VP2[par]
            K["kd", i] = dve.do(lambda e: e.tensor_tensor(h8(KD), h8(KR), hb(EU[:, i, :]), ALU.mult), K["pre", i], K.get(("dM", pp)))
            for g in range(2):
                if c4:
                    pe.put(lambda e, g=g: e.matmul(ps(7, 128 * g, 128 * g + 128), MST[:, b, g, :], QET[:, 128 * g:128 * g + 128], start=True, stop=False, skip_group_check=True), k_m[b], K.get(("ye", p)))
                for j in range(4):
                    h = 4 * g + j
                    kY = pe.do(lambda e, g=g, j=j, h=h: e.matmul(PS[32 * j:32 * j + 32, 7, 128 * g:128 * g + 128], VP[:, 32 * h:32 * h + 32], WT[g][:, 128 * j:128 * j + 128],
                                                                start=(c4 == 0), stop=True, skip_group_check=True), K["W", i], K["vp", i], K.get(("ye", p)))
            K["Y", i] = kY
            K["ye", i] = act.do(lambda e: e.activation(YT[:, :], ps(7, 0, 256), ACT.Copy), kY, K.get(("O", p)))
            for g in range(2):
                kM = pe.do(lambda e, g=g: e.matmul(ps(1, 256 + 128 * g, 384 + 128 * g), KD[:, 128 * g:128 * g + 128], VP[:, 128 * g:128 * g + 128], start=True, stop=True, skip_group_check=True),
                           K["kd", i], K.get(("vp", after[i])), K.get(("dMe", p)))
            K["dM", i] = kM
            for g in range(2):
                if c4 == 0:
                    km = dve.do(lambda e, g=g: e.tensor_tensor(MST[:, b, g, :], ps(1, 256 + 128 * g, 384 + 128 * g), BD, ALU.mult), kM, kbd)
                else:
                    k1 = dve.do(lambda e, g=g: e.tensor_tensor(MTMP[:, g, :], ps(1, 256 + 128 * g, 384 + 128 * g), BD, ALU.mult), kM, kbd, K.get(("dMe", p)))
                    km = dve.do(lambda e, g=g: e.scalar_tensor_tensor(MST[:, b, g, :], MST[:, b, g, :], ET[:, g, i:i + 1], MTMP[:, g, :], ALU.mult, ALU.add), k1, kY)
            k_m[b] = km
            K["dMe", i] = km

        def project_out(i, p):
            if i is None:
                return
            for g in range(2):
                kO = pe.do(lambda e, g=g: e.matmul(ps(4, 0, 256), YT[:, 128 * g:128 * g + 128], WOUT[:, g, :], start=(g == 0), stop=(g == 1)), K["ye", i], K["ev", order[-1] if i == order[-1] else after[i]], K.get(("acc", p)))
            K["O", i] = kO
            kx = pool.do(lambda e: e.tensor_tensor(XB[:, :], ACC[:, i, :], BO[:, :], ALU.add), K.get(("acc", p)), k_w1)
            K["acc", i] = k_acc2[i] = dve.do(lambda e: e.tensor_tensor(ACC[:, i, :], ps(4, 0, 256), XB[:, :], ALU.add), kO, kx)

        kbd = pool.do(lambda e: e.memset(BD[:, :], 0.0), kq0, *fre)
        for j in range(4):
            kbd = pool.do(lambda e, j=j: e.memset(BD[32 * j:32 * j + 32, 32 * j:32 * j + 32], 1.0), kbd)
        WD1 = view(base, 16384)
        wu1 = LIMIT - 16384
        assert low_end <= wu1 and base + 16384 <= wu1
        WU1 = view(wu1, 16384)
        c_u1, c_d1 = count("c_u1"), count("c_d1")

        def load_wu(q, *ticks):
            return sp.dma(lambda e: e.dma_start(WU1[:, 2048 * q:2048 * q + 2048], t["w1"][:, 2048 * q:2048 * q + 2048]), c_u1, *ticks)

        early = [q for q in range(8) if wu1 + 2048 * q >= route1_end]
        for q in early:
            load_wu(q, *fre)
        c_o = count("c_o")
        ov = out[0:T, :].rearrange("(b i p) d -> i p b d", b=NB, p=128)

        def store_sums(c):
            k_sums1[:] = [sp.dma(lambda e: e.dma_start(ov[c], ACC.rearrange("p (b i) d -> p i b d", b=NB)[:, c]), c_o, k_acc2[order[8 * c + 7]])]

        k_sums1 = []
        at = lambda n: order[n] if 0 <= n < len(order) else None
        after = {order[n]: at(n + 1) for n in range(NT)}
        logs(at(0), None)
        project_qk(at(0), None, None, 0)
        project_val(at(0), None, None, 0)
        decays(at(0), None, None, 0)
        logs(at(1), at(0))
        for n, i in enumerate(order):
            p, pp, nx, par = at(n - 1), at(n - 2), at(n + 1), n % 2
            turn(i, p, pp, par)
            if nx is not None:
                project_qk(nx, i, p, 1 - par)
            affinity(i, p, par, 0)
            if nx is not None:
                project_val(nx, i, p, 1 - par)
            affinity(i, p, par, 1)
            project_out(p, pp)
            if nx is not None:
                decays(nx, i, p, 1 - par)
            read_and_update(i, p, pp, par)
            if at(n + 2) is not None:
                logs(at(n + 2), nx)
            bank5[0] = K["W", i]
            next(rt, None)
            if n > 5:
                next(rt, None)
            if n % 8 == 1 and n > 8:
                store_sums(n // 8 - 1)
        project_out(at(NT - 1), at(NT - 2))
        last = order[-1]
        fre1 = [K["O", last], K["acc", last], K["dMe", last], K["W", last]]
        for _ in rt:
            pass
        for q in range(8):
            if q not in early:
                k_u1 = load_wu(q, *RR1["scat"], *fre1)
        extra = []
        for q in range(8):
            def load_wd(q=q):
                k_d1[:] = [sp.dma(lambda e: e.dma_start(WD1[:, 2048 * q:2048 * q + 2048], t["w2"][:, 2048 * q:2048 * q + 2048]), c_d1, *fre1)]
            extra.append(load_wd)
        store_sums(3)
        k_d1 = []

        top[0] = NT * D
        fixed = 2 * 256 + 2 * F1 + 2 * 256
        hT = [view(NT * D + fixed + F1 * n, F1) for n in range((2 * T - fixed) // F1)]
        assert base + 16384 + 3 * ROW <= wu1
        k_y, k_end = moe(1, F1, WU1, WD1, k_u1, k_d1, RR1["scat"], RR1["tex"], (B1S, B2S, SEL), [*fre1, k_br], out, lambda: k_sums1, len(hT) - 1, hT, extra, base + 16384)
        assert top[0] == NT * D + fixed
        pool.wait(k_y)

        block = ctx.enter_context(nc.Block())
        block.sync(sp.play)
        block.gpsimd(pool.play)
        block.scalar(act.play)
        block.tensor(pe.play)
        block.vector(dve.play)


def kernel(**inputs):
    import concourse.bacc as bacc
    from concourse.bass_utils import run_bass_kernel_spmd as run

    a = {k: np.ascontiguousarray(v) for k, v in inputs.items()}
    f32 = np.float32

    def rows(w):
        c = w.shape[0] // 128
        return np.ascontiguousarray(w.reshape(c, 128, -1).transpose(1, 0, 2))

    def wide(w):
        return np.concatenate([w, np.zeros((w.shape[0], 128 - w.shape[1]), w.dtype)], 1)

    def experts(w):
        e, k, n = w.shape
        return np.ascontiguousarray(w.reshape(e, k // 128, 128, n).transpose(2, 0, 1, 3).reshape(128, -1))

    def over(v):
        return np.ascontiguousarray(np.broadcast_to(v, (128, v.shape[-1])))

    r = np.arange(128)
    ident = np.eye(128, dtype=f32)
    uinc = (r[:, None] <= r[None, :]).astype(f32)
    ustr = (r[:, None] < r[None, :]).astype(f32)
    lstr = (r[:, None] > r[None, :]).astype(f32)
    hsel = np.concatenate([(4 * g + r[:, None] // 32 == np.arange(8)[None, :]).astype(f32) for g in range(2)], 1)
    token = (128 * np.arange(NT)[None, :] + r[:, None]).astype(f32)
    none = np.concatenate([np.zeros((128, ROW - 1), f32), (T + r[:, None]).astype(f32)], 1)
    cst = np.concatenate([ident, uinc, ustr, lstr, over(np.arange(8, dtype=f32)), over(128 * np.arange(32, dtype=f32)),
                          over(np.arange(72, dtype=f32)), hsel, token, none], 1).astype(f32)
    bfb = mybir.dt.np(BF16)
    cbf = np.concatenate([ident, np.where(r[None, :] > r[:, None], NEG, 0.0), np.where(r[None, :] < r[:, None], NEG, 0.0),
                          np.where(r[None, :] < r[:, None], -NEG, 0.0)], 1).astype(bfb)
    cbf = np.ascontiguousarray(cbf).view(f32)
    half = 16
    selx = np.zeros((128, 8, 128), f32)
    for e in range(8):
        selx[[e, 8 + e, 16 + e], e, :] = 1.0
    selx = np.ascontiguousarray(selx.reshape(128, 1024).astype(bfb)).view(f32)
    inv = (1.0 / np.power(f32(10000.0), np.arange(half, dtype=f32) / f32(half))).astype(f32)
    fr = np.arange(S, dtype=f32)[:, None] * inv[None, :]
    cos, sin = np.cos(fr.astype(np.float64)).astype(f32), np.sin(fr.astype(np.float64)).astype(f32)
    cos = np.concatenate([cos, cos], 1).reshape(4, 128, 32).transpose(1, 0, 2)
    sin = np.concatenate([-sin, sin], 1).reshape(4, 128, 32).transpose(1, 0, 2)
    wo = np.zeros((4, 4, 32, D), f32)
    wo[:, :, 0:16, :] = a["L0_attn_Wo"].T.reshape(4, 4, 16, D)
    arrays = {
        "x": a["L0_attn_in_features"].reshape(T, D),
        "cst": cst, "cbf": cbf,
        "Wg": rows(wide(a["L0_ffn_Wg"])),
        "Wq": rows(a["L0_attn_Wq"].T), "Wk": rows(a["L0_attn_Wk"].T), "Wv": rows(a["L0_attn_Wv"].T),
        "Wo": np.ascontiguousarray(wo.reshape(4, 128, D).transpose(1, 0, 2)),
        "W1": rows(a["L0_ffn_W1"]), "W2": rows(a["L0_ffn_W2"]),
        "Wu": experts(a["L0_ffn_Wu"]), "Wd": experts(a["L0_ffn_Wd"]),
        "Wcr": rows(wide(np.concatenate([a["L1_ffn_router_w"], a["L1_attn_Wbeta"].T, a["L1_attn_Wig"].T, a["L1_attn_Wog"].T], 1))),
        "nw": np.ascontiguousarray(a["L1_attn_norm_w"].reshape(2, 128).T),
        "Wqkv": rows(np.concatenate([a["L1_attn_Wq"].T, a["L1_attn_Wk"].T, a["L1_attn_Wv"].T], 1)),
        "Wout": rows(a["L1_attn_Wout"].T),
        "cos": np.ascontiguousarray(cos), "sin": np.ascontiguousarray(sin),
        "gb": over(np.concatenate([a["L1_attn_bbeta"], a["L1_attn_big"], a["L1_attn_bog"]])),
        "rb": over(a["L1_ffn_router_b"]), "bo": over(a["L1_attn_bout"]),
        "b1": a["L1_ffn_b1"], "b2": a["L1_ffn_b2"],
        "sel": selx, "w1": experts(a["L1_ffn_w1"]), "w2": experts(a["L1_ffn_w2"]),
    }
    nc = bacc.Bacc("TRN2", target_bir_lowering=False, num_devices=1)
    t = {n: nc.dram_tensor("in_" + n, v.shape, mybir.dt.from_np(v.dtype), kind="ExternalInput").ap() for n, v in arrays.items()}
    out = nc.dram_tensor("out_0", (T + 128, D), F32, kind="ExternalOutput").ap()
    build(nc, t, out)
    res = run(nc, [{"in_" + n: np.ascontiguousarray(v) for n, v in arrays.items()}], core_ids=[0])
    return res.results[0]["out_0"][:T].reshape(NB, S, D)
```
